# Optimizing a Trainium2 kernel written in Bass

```python
import numpy as np
import jax
import jax.numpy as jnp

def _softmax(x, axis=-1):
    return jax.nn.softmax(x, axis=axis)

def _gelu(x):
    return jax.nn.gelu(x, approximate=True)

def _silu(x):
    return jax.nn.silu(x)

def _sigmoid(x):
    return jax.nn.sigmoid(x)

def _layernorm(x, axis=-1, eps=1e-05):
    m = jnp.mean(x, axis=axis, keepdims=True)
    v = jnp.var(x, axis=axis, keepdims=True)
    return (x - m) / jnp.sqrt(v + eps)

def _scatter_add(tgt, idx, src, axis=0):
    return tgt.at[idx].add(src)

def _segment_sum(src, seg, n):
    return jax.ops.segment_sum(src, seg, n)
kernel_name = 'mk_seq_preln_d2_jaxref_r8_34ec51'

def setup_inputs(seed: int=0):
    np.random.seed(seed)
    _w = jnp.asarray

    def _L0_attn_setup():
        import jax, jax.numpy as jnp
        import numpy as np
        B, L, D_MODEL = (4, 256, 128)
        EXPAND = 2
        D_INNER = EXPAND * D_MODEL
        D_STATE = 16
        D_CONV = 4
        DT_RANK = (D_MODEL + 15) // 16
        EPS = 1e-05

        def _rmsnorm(x, w):
            return x * jax.lax.rsqrt(jnp.mean(x * x, axis=-1, keepdims=True) + EPS) * w

        def _causal_depthwise_conv(x, w, b):
            xp = jnp.pad(x, ((0, 0), (0, 0), (D_CONV - 1, 0)))
            y = jax.lax.conv_general_dilated(xp, w[:, None, :], window_strides=(1,), padding='VALID', dimension_numbers=('NCH', 'OIH', 'NCH'), feature_group_count=D_INNER)
            return y + b[None, :, None]

        def _selective_scan(u, delta, A, Bm, Cm, D):

            def step(s, inp):
                d_t, B_t, C_t, u_t = inp
                dA = jnp.exp(d_t[..., None] * A)
                dBu = d_t[..., None] * B_t[:, None, :] * u_t[..., None]
                s = s * dA + dBu
                y = jnp.einsum('bds,bs->bd', s, C_t)
                return (s, y)
            s0 = jnp.zeros((u.shape[0], D_INNER, D_STATE), u.dtype)
            xs = (delta.swapaxes(0, 1), Bm.swapaxes(0, 1), Cm.swapaxes(0, 1), u.swapaxes(0, 1))
            _, ys = jax.lax.scan(step, s0, xs)
            return ys.swapaxes(0, 1) + u * D
        key = jax.random.key(seed)
        ks = jax.random.split(key, 10)
        s = 0.02
        return {'x': jax.random.normal(ks[0], (B, L, D_MODEL), jnp.float32), 'norm_w': jnp.ones((D_MODEL,), jnp.float32), 'in_proj_w': jax.random.normal(ks[1], (2 * D_INNER, D_MODEL), jnp.float32) * s, 'conv_w': jax.random.normal(ks[2], (D_INNER, D_CONV), jnp.float32) * s, 'conv_b': jnp.zeros((D_INNER,), jnp.float32), 'x_proj_w': jax.random.normal(ks[3], (DT_RANK + 2 * D_STATE, D_INNER), jnp.float32) * s, 'dt_proj_w': jax.random.normal(ks[4], (D_INNER, DT_RANK), jnp.float32) * s, 'dt_proj_b': jnp.log(jnp.expm1(jnp.full((D_INNER,), 0.01, jnp.float32))), 'A_log': jnp.log(jnp.broadcast_to(jnp.arange(1, D_STATE + 1, dtype=jnp.float32), (D_INNER, D_STATE))), 'D': jnp.ones((D_INNER,), jnp.float32), 'out_proj_w': jax.random.normal(ks[5], (D_MODEL, D_INNER), jnp.float32) * s}
    _L0_attn_in = _L0_attn_setup()

    def _L0_ffn_setup():
        import math
        import jax, jax.numpy as jnp
        import numpy as np
        B, T, D, H, E, K, S = (4, 512, 128, 256, 16, 2, 2)
        ROUTE_SCALE = 1.0

        def _swiglu(x, w1, w3, w2):
            return jax.nn.silu(x @ w1) * (x @ w3) @ w2
        key = jax.random.key(seed)
        ks = jax.random.split(key, 9)
        s = 0.02
        return {'x': jax.random.normal(ks[0], (B, T, D), jnp.float32), 'gate_w': jax.random.normal(ks[1], (D, E), jnp.float32) * s, 'gate_b': jnp.zeros((E,), jnp.float32), 'ew1': jax.random.normal(ks[2], (E, D, H), jnp.float32) * s, 'ew3': jax.random.normal(ks[3], (E, D, H), jnp.float32) * s, 'ew2': jax.random.normal(ks[4], (E, H, D), jnp.float32) * s, 'sw1': jax.random.normal(ks[5], (S, D, H), jnp.float32) * s, 'sw3': jax.random.normal(ks[6], (S, D, H), jnp.float32) * s, 'sw2': jax.random.normal(ks[7], (S, H, D), jnp.float32) * s}
    _L0_ffn_in = _L0_ffn_setup()

    def _L1_attn_setup():
        import jax, jax.numpy as jnp
        import numpy as np
        import math
        D_MODEL = 128
        NUM_HEADS = 16
        D_HEAD = D_MODEL // NUM_HEADS
        BATCH = 4
        SEQ = 256

        def _trunc_normal(key, shape, sd):
            return sd * jax.random.truncated_normal(key, -3.0, 3.0, shape, dtype=jnp.float32)
        key = jax.random.key(seed)
        kx, kq, kk, kv, ko = jax.random.split(key, 5)
        sd = (2.0 / (NUM_HEADS * D_HEAD + D_MODEL)) ** 0.5
        x = jax.random.normal(kx, (BATCH, SEQ, D_MODEL), dtype=jnp.float32)
        WQ = _trunc_normal(kq, (NUM_HEADS, D_HEAD, D_MODEL), sd)
        WK = _trunc_normal(kk, (NUM_HEADS, D_HEAD, D_MODEL), sd)
        WV = _trunc_normal(kv, (NUM_HEADS, D_HEAD, D_MODEL), sd)
        WO = _trunc_normal(ko, (NUM_HEADS, D_MODEL, D_HEAD), sd)
        return {'x': x, 'WQ': WQ, 'WK': WK, 'WV': WV, 'WO': WO}
    _L1_attn_in = _L1_attn_setup()

    def _L1_ffn_setup():
        import jax, jax.numpy as jnp
        import numpy as np
        MAX_THRESHOLD = 0.125
        key = jax.random.key(seed)
        ks = jax.random.split(key, 5)
        B, S, D, FF, E = (2, 256, 128, 512, 8)
        sd = 1.0 / np.sqrt(D)
        sf = 1.0 / np.sqrt(FF)
        return {'inputs': jax.random.normal(ks[0], (B, S, D), dtype=jnp.float32), 'Wg': jax.random.normal(ks[1], (D, E), dtype=jnp.float32) * sd, 'bg': jnp.zeros((E,), dtype=jnp.float32), 'Wt': jax.random.normal(ks[2], (D, 1), dtype=jnp.float32) * sd, 'bt': jnp.zeros((1,), dtype=jnp.float32), 'W1': jax.random.normal(ks[3], (E, D, FF), dtype=jnp.float32) * sd, 'b1': jnp.zeros((E, FF), dtype=jnp.float32), 'W2': jax.random.normal(ks[4], (E, FF, D), dtype=jnp.float32) * sf, 'b2': jnp.zeros((E, D), dtype=jnp.float32)}
    _L1_ffn_in = _L1_ffn_setup()
    _d = {'L0_attn_x': _L0_attn_in['x'], 'L0_attn_norm_w': _L0_attn_in['norm_w'], 'L0_attn_in_proj_w': _L0_attn_in['in_proj_w'], 'L0_attn_conv_w': _L0_attn_in['conv_w'], 'L0_attn_conv_b': _L0_attn_in['conv_b'], 'L0_attn_x_proj_w': _L0_attn_in['x_proj_w'], 'L0_attn_dt_proj_w': _L0_attn_in['dt_proj_w'], 'L0_attn_dt_proj_b': _L0_attn_in['dt_proj_b'], 'L0_attn_A_log': _L0_attn_in['A_log'], 'L0_attn_D': _L0_attn_in['D'], 'L0_attn_out_proj_w': _L0_attn_in['out_proj_w'], 'L0_ffn_gate_w': _L0_ffn_in['gate_w'], 'L0_ffn_gate_b': _L0_ffn_in['gate_b'], 'L0_ffn_ew1': _L0_ffn_in['ew1'], 'L0_ffn_ew3': _L0_ffn_in['ew3'], 'L0_ffn_ew2': _L0_ffn_in['ew2'], 'L0_ffn_sw1': _L0_ffn_in['sw1'], 'L0_ffn_sw3': _L0_ffn_in['sw3'], 'L0_ffn_sw2': _L0_ffn_in['sw2'], 'L1_attn_WQ': _L1_attn_in['WQ'], 'L1_attn_WK': _L1_attn_in['WK'], 'L1_attn_WV': _L1_attn_in['WV'], 'L1_attn_WO': _L1_attn_in['WO'], 'L1_ffn_Wg': _L1_ffn_in['Wg'], 'L1_ffn_bg': _L1_ffn_in['bg'], 'L1_ffn_Wt': _L1_ffn_in['Wt'], 'L1_ffn_bt': _L1_ffn_in['bt'], 'L1_ffn_W1': _L1_ffn_in['W1'], 'L1_ffn_b1': _L1_ffn_in['b1'], 'L1_ffn_W2': _L1_ffn_in['W2'], 'L1_ffn_b2': _L1_ffn_in['b2']}
    _x0 = _d['L0_attn_x']
    _d['L0_attn_x'] = jax.random.normal(jax.random.fold_in(jax.random.key(seed), 1), (4, 1024, 128), dtype=_x0.dtype)
    del _x0
    return _d

def reference(L0_attn_x, L0_attn_norm_w, L0_attn_in_proj_w, L0_attn_conv_w, L0_attn_conv_b, L0_attn_x_proj_w, L0_attn_dt_proj_w, L0_attn_dt_proj_b, L0_attn_A_log, L0_attn_D, L0_attn_out_proj_w, L0_ffn_gate_w, L0_ffn_gate_b, L0_ffn_ew1, L0_ffn_ew3, L0_ffn_ew2, L0_ffn_sw1, L0_ffn_sw3, L0_ffn_sw2, L1_attn_WQ, L1_attn_WK, L1_attn_WV, L1_attn_WO, L1_ffn_Wg, L1_ffn_bg, L1_ffn_Wt, L1_ffn_bt, L1_ffn_W1, L1_ffn_b1, L1_ffn_W2, L1_ffn_b2):

    def _L0_attn_ref(x, norm_w, in_proj_w, conv_w, conv_b, x_proj_w, dt_proj_w, dt_proj_b, A_log, D, out_proj_w):
        import jax, jax.numpy as jnp
        import numpy as np
        B, L, D_MODEL = (4, 256, 128)
        EXPAND = 2
        D_INNER = EXPAND * D_MODEL
        D_STATE = 16
        D_CONV = 4
        DT_RANK = (D_MODEL + 15) // 16
        EPS = 1e-05

        def _rmsnorm(x, w):
            return x * jax.lax.rsqrt(jnp.mean(x * x, axis=-1, keepdims=True) + EPS) * w

        def _causal_depthwise_conv(x, w, b):
            xp = jnp.pad(x, ((0, 0), (0, 0), (D_CONV - 1, 0)))
            y = jax.lax.conv_general_dilated(xp, w[:, None, :], window_strides=(1,), padding='VALID', dimension_numbers=('NCH', 'OIH', 'NCH'), feature_group_count=D_INNER)
            return y + b[None, :, None]

        def _selective_scan(u, delta, A, Bm, Cm, D):

            def step(s, inp):
                d_t, B_t, C_t, u_t = inp
                dA = jnp.exp(d_t[..., None] * A)
                dBu = d_t[..., None] * B_t[:, None, :] * u_t[..., None]
                s = s * dA + dBu
                y = jnp.einsum('bds,bs->bd', s, C_t)
                return (s, y)
            s0 = jnp.zeros((u.shape[0], D_INNER, D_STATE), u.dtype)
            xs = (delta.swapaxes(0, 1), Bm.swapaxes(0, 1), Cm.swapaxes(0, 1), u.swapaxes(0, 1))
            _, ys = jax.lax.scan(step, s0, xs)
            return ys.swapaxes(0, 1) + u * D
        h = _rmsnorm(x, norm_w)
        xz = jnp.einsum('bld,ed->ble', h, in_proj_w)
        xi, z = jnp.split(xz, 2, axis=-1)
        xi = _causal_depthwise_conv(xi.swapaxes(1, 2), conv_w, conv_b).swapaxes(1, 2)
        xi = jax.nn.silu(xi)
        x_dbl = jnp.einsum('bld,ed->ble', xi, x_proj_w)
        dt, Bm, Cm = jnp.split(x_dbl, [DT_RANK, DT_RANK + D_STATE], axis=-1)
        delta = jax.nn.softplus(jnp.einsum('blr,dr->bld', dt, dt_proj_w) + dt_proj_b)
        A = -jnp.exp(A_log)
        y = _selective_scan(xi, delta, A, Bm, Cm, D)
        y = y * jax.nn.silu(z)
        out = jnp.einsum('bld,ed->ble', y, out_proj_w)
        return out + x

    def _L0_ffn_ref(x, gate_w, gate_b, ew1, ew3, ew2, sw1, sw3, sw2):
        import math
        import jax, jax.numpy as jnp
        import numpy as np
        B, T, D, H, E, K, S = (4, 512, 128, 256, 16, 2, 2)
        ROUTE_SCALE = 1.0

        def _swiglu(x, w1, w3, w2):
            return jax.nn.silu(x @ w1) * (x @ w3) @ w2
        Bx, Tx, Dx = x.shape
        flat = x.reshape(-1, Dx)
        N = flat.shape[0]
        n_experts = gate_w.shape[1]
        logits = flat @ gate_w
        scores = jax.nn.softmax(logits.astype(jnp.float32), -1) + gate_b
        _, topi = jax.lax.top_k(scores, K)
        weights = jnp.take_along_axis(logits, topi, axis=-1) * ROUTE_SCALE
        weights = weights.astype(flat.dtype)
        capacity = math.ceil(N * K / n_experts * 1.25)

        def per_expert(gid, w1, w3, w2):
            match = topi == gid
            assigned = match.any(-1)
            w_tok = jnp.sum(jnp.where(match, weights, 0.0), -1)
            wm = jnp.where(assigned, w_tok, -jnp.inf)
            vals, idx = jax.lax.top_k(wm, capacity)
            valid = assigned[idx]
            xs = flat[idx]
            y = _swiglu(xs, w1, w3, w2) * jnp.where(valid, vals, 0.0)[:, None]
            return (idx, y)
        idxs, ys = jax.vmap(per_expert)(jnp.arange(n_experts), ew1, ew3, ew2)
        out = jnp.zeros_like(flat).at[idxs.reshape(-1)].add(ys.reshape(-1, Dx))
        shared = jax.vmap(lambda w1, w3, w2: _swiglu(flat, w1, w3, w2))(sw1, sw3, sw2)
        out = out + shared.mean(0)
        return out.reshape(Bx, Tx, Dx)

    def _L1_attn_ref(x, WQ, WK, WV, WO):
        import jax, jax.numpy as jnp
        import numpy as np
        import math
        D_MODEL = 128
        NUM_HEADS = 16
        D_HEAD = D_MODEL // NUM_HEADS
        BATCH = 4
        SEQ = 256

        def _trunc_normal(key, shape, sd):
            return sd * jax.random.truncated_normal(key, -3.0, 3.0, shape, dtype=jnp.float32)
        Q = jnp.einsum('bsd,hkd->bhsk', x, WQ)
        K = jnp.einsum('bsd,hkd->bhsk', x, WK)
        V = jnp.einsum('bsd,hkd->bhsk', x, WV)
        d_k = Q.shape[-1]
        scores = jnp.einsum('bhqd,bhkd->bhqk', Q, K) / math.sqrt(d_k)
        seq_len = x.shape[-2]
        causal = jnp.tril(jnp.ones((seq_len, seq_len), dtype=bool))
        scores = jnp.where(causal, scores, -jnp.inf)
        probs = jax.nn.softmax(scores, axis=-1)
        attn = jnp.einsum('bhqk,bhkv->bhqv', probs, V)
        return jnp.einsum('bhsv,hdv->bsd', attn, WO)

    def _L1_ffn_ref(inputs, Wg, bg, Wt, bt, W1, b1, W2, b2):
        import jax, jax.numpy as jnp
        import numpy as np
        MAX_THRESHOLD = 0.125
        x = inputs.reshape(-1, inputs.shape[-1])
        gate = jax.nn.softmax(x @ Wg + bg, axis=-1)
        thr = jax.nn.sigmoid(x @ Wt + bt) * MAX_THRESHOLD
        adapted = gate - thr
        mask = (adapted >= 0).astype(x.dtype)
        w = adapted * mask
        s = jnp.sum(w, axis=-1, keepdims=True)
        s = jnp.where(s == 0, jnp.ones_like(s), s)
        w = w / s
        h = jax.nn.gelu(jnp.einsum('td,edf->etf', x, W1) + b1[:, None, :])
        eo = jnp.einsum('etf,efd->etd', h, W2) + b2[:, None, :]
        out = jnp.einsum('te,etd->td', w, eo)
        return out.reshape(inputs.shape)
    x = L0_attn_x
    x = x + _L0_attn_ref(_layernorm(x, axis=-1), L0_attn_norm_w, L0_attn_in_proj_w, L0_attn_conv_w, L0_attn_conv_b, L0_attn_x_proj_w, L0_attn_dt_proj_w, L0_attn_dt_proj_b, L0_attn_A_log, L0_attn_D, L0_attn_out_proj_w)
    x = x + _L0_ffn_ref(_layernorm(x, axis=-1), L0_ffn_gate_w, L0_ffn_gate_b, L0_ffn_ew1, L0_ffn_ew3, L0_ffn_ew2, L0_ffn_sw1, L0_ffn_sw3, L0_ffn_sw2)
    x = x + _L1_attn_ref(_layernorm(x, axis=-1), L1_attn_WQ, L1_attn_WK, L1_attn_WV, L1_attn_WO)
    x = x + _L1_ffn_ref(_layernorm(x, axis=-1), L1_ffn_Wg, L1_ffn_bg, L1_ffn_Wt, L1_ffn_bt, L1_ffn_W1, L1_ffn_b1, L1_ffn_W2, L1_ffn_b2)
    return x

_drawn_inputs = setup_inputs


def setup_inputs(seed=0):
    import zlib

    import numpy as np

    out = dict(_drawn_inputs(seed))
    spreads = {'L0_attn_norm_w': (1.0, 0.6),
     'L0_attn_conv_b': (0.0, 0.8),
     'L0_attn_dt_proj_b': (-4.600166320800781, 0.6),
     'L0_attn_D': (1.0, 0.6),
     'L0_ffn_gate_b': (0.0, 0.8),
     'L1_ffn_bg': (0.0, 2.0),
     'L1_ffn_b1': (0.0, 2.0),
     'L1_ffn_b2': (0.0, 2.0)}
    factors = {'L0_attn_in_proj_w': 8.0,
     'L0_attn_conv_w': 8.0,
     'L0_attn_x_proj_w': 8.0,
     'L0_attn_dt_proj_w': 8.0,
     'L0_attn_A_log': 8.0,
     'L0_attn_out_proj_w': 8.0,
     'L0_ffn_gate_w': 8.0,
     'L0_ffn_ew1': 8.0,
     'L0_ffn_ew3': 8.0,
     'L0_ffn_ew2': 8.0,
     'L0_ffn_sw1': 8.0,
     'L0_ffn_sw3': 8.0,
     'L0_ffn_sw2': 8.0,
     'L1_attn_WQ': 8.0,
     'L1_attn_WK': 8.0,
     'L1_attn_WV': 2.834,
     'L1_attn_WO': 3.123,
     'L1_ffn_Wg': 3.46,
     'L1_ffn_Wt': 8.0,
     'L1_ffn_W1': 3.364,
     'L1_ffn_W2': 2.801}
    for name, (base, spread) in spreads.items():
        noise = np.random.default_rng([zlib.crc32(name.encode()), seed]).standard_normal(out[name].shape)
        drawn = base * np.exp(spread * noise) if base else spread * noise
        out[name] = jnp.asarray(drawn.astype(out[name].dtype))
    for name, factor in factors.items():
        out[name] = (out[name] * factor).astype(out[name].dtype)
    return out
```

```python
from contextlib import ExitStack

import concourse.bass as bass
from concourse import mybir

F32 = mybir.dt.float32
BF16 = mybir.dt.bfloat16
ALU = mybir.AluOpType
ACT = mybir.ActivationFunctionType
AX = mybir.AxisListType

P = 128
D = 128
BATCH, SEQ = 4, 1024
TOK = BATCH * SEQ
CH = 512
NCH = TOK // CH
CPB = SEQ // CH
NT = TOK // P
EPS = 1e-5

INNER = 256
NBLK = INNER // P
STATE = 16
RANK = 8
TAPS = 4
HALO = TAPS - 1


class Phase:

    def __init__(self, nc, name):
        self.nc, self.name, self.stack, self.sems = nc, name, ExitStack(), []

    def __enter__(self):
        return self

    def __exit__(self, *what):
        self.stack.close()
        if self.sems:
            self.nc.clear_and_free_semaphores(self.sems)
            self.nc.all_engine_barrier()

    def sb(self, name, shape, dt=F32):
        return self.stack.enter_context(self.nc.sbuf_tensor(f"{self.name}_{name}", shape, dt))

    def ps(self, name, shape, dt=F32):
        return self.stack.enter_context(self.nc.psum_tensor(f"{self.name}_{name}", shape, dt))

    def sem(self, name):
        self.sems.append(self.nc.alloc_semaphore(f"{self.name}_{name}"))
        return self.sems[-1]

    def block(self):
        return self.nc.Block()


def waited(eng, passed):
    eng.sem_inc(passed, 1)


def mamba_prep(nc, xT, delta, du, bc_split, x_dram, w, scratch):
    with Phase(nc, "prep") as ph:
        ones = ph.sb("ones_over_d", [P, P])
        w_in = ph.sb("w_in", [P, 2 * INNER])
        w_x = ph.sb("w_x", [P, NBLK, P])
        w_dt = ph.sb("w_dt", [P, NBLK * P])
        norm_w = ph.sb("norm_w", [P, 1])
        conv_w = ph.sb("conv_w", [P, NBLK, TAPS])
        conv_b = ph.sb("conv_b", [P, NBLK])
        dt_b = ph.sb("dt_b", [P, NBLK])
        eps = ph.sb("eps", [P, 1])
        xc = ph.sb("xc", [P, CH])
        sq = ph.sb("sq", [P, CH])
        lnv = ph.sb("lnv", [P, CH])
        rstd = ph.sb("rstd", [P, CH])
        msn = ph.sb("msn", [P, CH])
        msn2 = ph.sb("msn2", [P, CH])
        lnv2 = ph.sb("lnv2", [P, CH])
        rms = ph.sb("rms", [P, CH])
        xn = ph.sb("xn", [P, CH])
        hT = ph.sb("hT", [P, CH])
        xi = ph.sb("xi", [P, 2, NBLK, HALO + CH])
        cacc = ph.sb("cacc", [P, NBLK, CH])
        u = ph.sb("u", [P, 2, NBLK, CH])
        zs = ph.sb("zs", [P, 2, NBLK, CH])
        hi = ph.sb("hi", [P, CH], BF16)
        rest = ph.sb("rest", [P, CH])
        mid = ph.sb("mid", [P, CH], BF16)
        crow = ph.sb("crow", [32, 2, CH])
        dtb = ph.sb("dtb", [P, CH])
        absd = ph.sb("absd", [P, NBLK, CH])
        expd = ph.sb("expd", [P, NBLK, CH])
        lnd = ph.sb("lnd", [P, NBLK, CH])
        maxd = ph.sb("maxd", [P, NBLK, CH])

        p_mean = ph.ps("p_mean", [P, CH])
        p_var = ph.ps("p_var", [P, CH])
        p_in = ph.ps("p_in", [P, 2 * NBLK, CH])
        p_x = p_mean
        p_dt = ph.ps("p_dt", [P, NBLK, CH])

        s_w = ph.sem("weights_loaded")
        s_x = [ph.sem(f"x_loaded{i}") for i in range(NCH)]
        s_zero = ph.sem("zeroed")
        s_mean = ph.sem("mean_ready")
        s_xc = ph.sem("centred")
        s_sq = ph.sem("squared")
        s_var = ph.sem("var_ready")
        s_lnv = ph.sem("log_var")
        s_rstd = ph.sem("rstd_ready")
        s_msn = ph.sem("mean_square")
        s_rms = ph.sem("rms_ready")
        s_xn = ph.sem("normed")
        s_h = ph.sem("h_ready")
        s_in = ph.sem("in_proj_done")
        s_xi = ph.sem("xi_copied")
        s_halo = ph.sem("halo_ready")
        s_cstep = ph.sem("conv_step")
        s_u = ph.sem("u_ready")
        s_zs = ph.sem("z_silu_ready")
        s_xp = ph.sem("x_proj_done")
        s_crow = ph.sem("crow_ready")
        s_split = ph.sem("split_step")
        s_dtb = ph.sem("dt_rows_ready")
        s_dt = ph.sem("dt_proj_done")
        s_abs = ph.sem("abs_done")
        s_exp = ph.sem("exp_done")
        s_ln = ph.sem("log_done")
        s_maxd = ph.sem("max_done")
        s_delta = ph.sem("delta_ready")
        s_du = ph.sem("du_ready")
        s_res = ph.sem("residual_added")
        s_st = [ph.sem(f"stored{i}") for i in range(2)]

        with ph.block() as block:

            @block.sync
            def _(sp):
                for dst, src in ((ones, w["ones_over_d"]), (w_in, w["in_proj"]), (norm_w, w["norm_w"]),
                                 (w_x, w["x_proj"]), (w_dt, w["dt_proj"]), (conv_w, w["conv_w"]),
                                 (conv_b, w["conv_b"]), (dt_b, w["dt_b"])):
                    sp.dma_start(dst[:], src).then_inc(s_w, 16)
                for g in range(NCH):
                    sp.dma_start(xT[:, g * CH:(g + 1) * CH], x_dram[:, g * CH:(g + 1) * CH]).then_inc(s_x[g], 16)
                for g in range(NCH):
                    b, half = g // CPB, g % CPB
                    sp.wait_ge(s_u, g + 1)
                    sp.dma_start(scratch["u"][b, :, :, half * CH:(half + 1) * CH], u[:, g % 2]).then_inc(s_st[g % 2], 16)
                    sp.wait_ge(s_zs, g + 1)
                    sp.dma_start(scratch["zs"][b, :, :, half * CH:(half + 1) * CH], zs[:, g % 2]).then_inc(s_st[g % 2], 16)
                    sp.wait_ge(s_crow, g + 1)
                    sp.dma_start(scratch["c"][b, :, half * CH:(half + 1) * CH], crow[16:32, g % 2]).then_inc(s_st[g % 2], 16)
                for i in range(2):
                    sp.wait_ge(s_st[i], 48 * (NCH // 2))

            @block.tensor
            def _(pe):
                pe.wait_ge(s_w, 16 * 8)
                pe.wait_ge(s_zero, 4)
                for g in range(NCH + 1):
                    if g < NCH:
                        pe.wait_ge(s_x[g], 16)
                        if g >= 2:
                            pe.wait_ge(s_split, 6 * (g - 1))
                            pe.wait_ge(s_crow, g - 1)
                        pe.matmul(p_mean[:], ones[:], xT[:, g * CH:(g + 1) * CH], start=True, stop=True).then_inc(s_mean, 1)
                        pe.wait_ge(s_sq, g + 1)
                        if g >= 1:
                            pe.wait_ge(s_msn, 2 * g)
                        pe.matmul(p_var[:], ones[:], sq[:], start=True, stop=True).then_inc(s_var, 1)
                    if g >= 1:
                        pe.wait_ge(s_u, g)
                        pe.wait_ge(s_xc, min(g + 1, NCH))
                        for k in range(NBLK):
                            mm = pe.matmul(p_x[:], w_x[:, k], u[:, (g - 1) % 2, k], start=(k == 0), stop=(k == NBLK - 1))
                        mm.then_inc(s_xp, 1)
                        pe.wait_ge(s_dtb, g)
                        if g >= 2:
                            pe.wait_ge(s_abs, g - 1)
                            pe.wait_ge(s_maxd, g - 1)
                        for k in range(NBLK):
                            mm = pe.matmul(p_dt[:, k], w_dt[:, k * P:(k + 1) * P], dtb[:], start=True, stop=True)
                        mm.then_inc(s_dt, 1)
                    if g < NCH:
                        pe.wait_ge(s_h, g + 1)
                        if g >= 1:
                            pe.wait_ge(s_xi, g)
                            pe.wait_ge(s_zs, g)
                        for m in range(2 * NBLK):
                            mm = pe.matmul(p_in[:, m], w_in[:, m * P:(m + 1) * P], hT[:], start=True, stop=True)
                        mm.then_inc(s_in, 1)

            @block.scalar
            def _(act):
                act.wait_ge(s_w, 16 * 8)
                act.wait_ge(s_zero, 4)
                for g in range(NCH + 1):
                    q = g - 1
                    if g < NCH:
                        act.wait_ge(s_xc, g + 1)
                        act.activation(sq[:], xc[:], ACT.Square).then_inc(s_sq, 1)
                        act.wait_ge(s_var, g + 1)
                        act.activation(lnv[:], p_var[:], ACT.Ln, bias=eps[:]).then_inc(s_lnv, 1)
                        act.wait_ge(s_lnv, g + 1)
                        if g >= 1:
                            act.wait_ge(s_msn, 2 * g)
                        act.activation(rstd[:], lnv[:], ACT.Exp, scale=-0.5).then_inc(s_rstd, 1)
                    if g >= 1:
                        if q >= 2:
                            act.wait_ge(s_st[q % 2], 48 * (q // 2))
                        act.activation(zs[:, q % 2], p_in[:, NBLK:], ACT.Silu).then_inc(s_zs, 1)
                        act.wait_ge(s_cstep, 8 * q + 8)
                        if q >= 2:
                            act.wait_ge(s_du, q - 1)
                        act.activation(u[:, q % 2], cacc[:], ACT.Silu).then_inc(s_u, 1)
                    if g < NCH:
                        act.wait_ge(s_msn, 2 * g + 2)
                        act.activation(lnv2[:], msn2[:], ACT.Ln, bias=eps[:]).then_inc(s_rms, 1)
                        act.wait_ge(s_rms, 2 * g + 1)
                        if g >= 1:
                            act.wait_ge(s_h, g)
                        act.activation(rms[:], lnv2[:], ACT.Exp, scale=-0.5).then_inc(s_rms, 1)
                    if g >= 1:
                        act.wait_ge(s_xp, q + 1)
                        if q >= 1:
                            act.wait_ge(s_dt, q)
                        act.activation(dtb[96:96 + RANK], p_x[96:96 + RANK], ACT.Copy).then_inc(s_dtb, 1)
                        act.activation(crow[:, q % 2], p_x[0:32], ACT.Copy).then_inc(s_crow, 1)
                        act.wait_ge(s_dt, q + 1)
                        for k in range(NBLK):
                            ins = act.activation(absd[:, k], p_dt[:, k], ACT.Abs, bias=dt_b[:, k:k + 1])
                        ins.then_inc(s_abs, 1)
                        act.wait_ge(s_abs, q + 1)
                        act.activation(expd[:], absd[:], ACT.Exp, scale=-1.0).then_inc(s_exp, 1)
                        act.wait_ge(s_exp, q + 1)
                        if q >= 1:
                            act.wait_ge(s_delta, q)
                        act.activation(lnd[:], expd[:], ACT.Ln, bias=1.0).then_inc(s_ln, 1)
                    if g < NCH:
                        act.wait_ge(s_in, g + 1)
                        act.wait_ge(s_halo, g + 1)
                        if g >= 2:
                            act.wait_ge(s_cstep, 8 * (g - 1))
                        act.activation(xi[:, g % 2, :, HALO:], p_in[:, 0:NBLK], ACT.Copy).then_inc(s_xi, 1)

            @block.vector
            def _(dve):
                dve.memset(dtb[:], 0.0).then_inc(s_zero, 1)
                dve.memset(bc_split[:].bitcast(mybir.dt.uint32), 0).then_inc(s_zero, 1)
                dve.memset(xi[:], 0.0).then_inc(s_zero, 1)
                dve.memset(eps[:], EPS).then_inc(s_zero, 1)
                dve.wait_ge(s_w, 16 * 8)
                dve.wait_ge(s_zero, 4)
                for g in range(NCH + 1):
                    q = g - 1
                    if g < NCH:
                        dve.wait_ge(s_mean, g + 1)
                        if g >= 1:
                            dve.wait_ge(s_xn, g)
                        dve.tensor_tensor(xc[:], xT[:, g * CH:(g + 1) * CH], p_mean[:], ALU.subtract).then_inc(s_xc, 1)
                        if g >= 2:
                            dve.wait_ge(s_cstep, 8 * (g - 1))
                        if g % CPB == 0:
                            dve.memset(xi[:, g % 2, :, 0:HALO], 0.0).then_inc(s_halo, 1)
                        else:
                            dve.wait_ge(s_xi, g)
                            dve.tensor_copy(xi[:, g % 2, :, 0:HALO], xi[:, (g + 1) % 2, :, CH:CH + HALO]).then_inc(s_halo, 1)
                    if g >= 1:
                        dve.wait_ge(s_xi, q + 1)
                        dve.wait_ge(s_halo, q + 1)
                        if q >= 1:
                            dve.wait_ge(s_u, q)
                        for k in range(NBLK):
                            dve.tensor_scalar(cacc[:, k], xi[:, q % 2, k, HALO:], conv_w[:, k, HALO:TAPS],
                                              conv_b[:, k:k + 1], ALU.mult, ALU.add).then_inc(s_cstep, 1)
                        for j in range(HALO):
                            for k in range(NBLK):
                                dve.wait_ge(s_cstep, 8 * q + 2 * j + k + 1)
                                dve.scalar_tensor_tensor(cacc[:, k], xi[:, q % 2, k, j:j + CH], conv_w[:, k, j:j + 1],
                                                         cacc[:, k], ALU.mult, ALU.add).then_inc(s_cstep, 1)
                    if g < NCH:
                        dve.wait_ge(s_rstd, g + 1)
                        if g >= 1:
                            dve.wait_ge(s_res, g)
                        dve.tensor_tensor(xn[:], xc[:], rstd[:], ALU.mult).then_inc(s_xn, 1)
                        dve.wait_ge(s_var, g + 1)
                        dve.tensor_tensor(msn[:], rstd[:], p_var[:], ALU.mult).then_inc(s_msn, 1)
                        dve.wait_ge(s_msn, 2 * g + 1)
                        dve.tensor_tensor(msn2[:], msn[:], rstd[:], ALU.mult).then_inc(s_msn, 1)
                    if g >= 1:
                        tok = slice(q * CH, (q + 1) * CH)
                        dve.wait_ge(s_crow, q + 1)
                        dve.tensor_copy(hi[0:96], p_x[0:96]).then_inc(s_split, 1)
                        dve.wait_ge(s_split, 6 * q + 1)
                        dve.tensor_tensor(rest[0:96], p_x[0:96], hi[0:96], ALU.subtract).then_inc(s_split, 1)
                        dve.tensor_copy(bc_split[0:32, tok], hi[0:32]).then_inc(s_split, 1)
                        dve.wait_ge(s_split, 6 * q + 2)
                        dve.tensor_copy(mid[0:96], rest[0:96]).then_inc(s_split, 1)
                        dve.wait_ge(s_split, 6 * q + 4)
                        dve.tensor_copy(bc_split[32:64, tok], mid[32:64]).then_inc(s_split, 1)
                        dve.tensor_tensor(bc_split[64:96, tok], rest[64:96], mid[64:96], ALU.subtract).then_inc(s_split, 1)
                    if g < NCH:
                        dve.wait_ge(s_rms, 2 * g + 2)
                        dve.wait_ge(s_xn, g + 1)
                        if g >= 1:
                            dve.wait_ge(s_in, g)
                        dve.scalar_tensor_tensor(hT[:], xn[:], norm_w[:], rms[:], ALU.mult, ALU.mult).then_inc(s_h, 1)
                    if g >= 1:
                        b, half = q // CPB, q % CPB
                        dve.wait_ge(s_abs, q + 1)
                        for k in range(NBLK):
                            ins = dve.tensor_scalar(maxd[:, k], p_dt[:, k], dt_b[:, k:k + 1], 0.0, ALU.add, ALU.max)
                        ins.then_inc(s_maxd, 1)
                        dve.wait_ge(s_ln, q + 1)
                        dve.wait_ge(s_maxd, q + 1)
                        dve.tensor_tensor(delta[:, b, :, half * CH:(half + 1) * CH], maxd[:], lnd[:], ALU.add).then_inc(s_delta, 1)

            @block.gpsimd
            def _(pool):
                for g in range(NCH + 1):
                    if g < NCH:
                        tok = slice(g * CH, (g + 1) * CH)
                        pool.wait_ge(s_xn, g + 1)
                        pool.wait_ge(s_xc, g + 1)
                        pool.tensor_tensor(xT[:, tok], xT[:, tok], xn[:], ALU.add).then_inc(s_res, 1)
                    if g >= 1:
                        q = g - 1
                        b, seg = q // CPB, slice(q % CPB * CH, (q % CPB + 1) * CH)
                        pool.wait_ge(s_delta, q + 1)
                        pool.wait_ge(s_u, q + 1)
                        pool.tensor_tensor(du[:, b, :, seg], delta[:, b, :, seg], u[:, q % 2], ALU.mult).then_inc(s_du, 1)


def mamba_scan(nc, xT, delta, du, bc_split, w, scratch):
    NIT = NBLK * STATE
    with Phase(nc, "scan") as ph:
        ident = ph.sb("ident", [P, P])
        sel = ph.sb("sel", [P, STATE, P], BF16)
        a_log = ph.sb("a_log", [P, NBLK, STATE])
        a_exp = ph.sb("a_exp", [P, NBLK, STATE])
        a_neg = ph.sb("a_neg", [P, NBLK, STATE])
        d_skip = ph.sb("d_skip", [P, NBLK])
        w_out = ph.sb("w_out", [P, NBLK, D])
        c_bc = ph.sb("c_bc", [P, STATE, SEQ])
        decay = ph.sb("decay", [P, 2, SEQ])
        h = ph.sb("h", [P, 2, SEQ])
        hc = ph.sb("hc", [P, 2, SEQ])
        u = ph.sb("u", [P, NBLK, SEQ])
        zs = ph.sb("zs", [P, NBLK, SEQ])
        y1 = u
        p_b = ph.ps("p_b", [P, 2, SEQ])
        p_y = ph.ps("p_y", [P, SEQ])
        p_o = ph.ps("p_o", [P, SEQ])

        s_w = ph.sem("weights_loaded")
        s_a = ph.sem("a_ready")
        s_c = [ph.sem(f"c_loaded{i}") for i in range(STATE)]
        s_uz = ph.sem("u_zs_loaded")
        s_b = ph.sem("b_broadcast")
        s_dec = ph.sem("decay_ready")
        s_dbu = ph.sem("dbu_ready")
        s_scan = ph.sem("scan_done")
        s_hc = ph.sem("hc_ready")
        s_acc = ph.sem("hc_summed")
        s_y1 = ph.sem("y_read")
        s_y = ph.sem("y_gated")
        s_o = ph.sem("out_proj_done")
        s_x = ph.sem("residual_added")
        hold = ph.sem("wait_passed")

        with ph.block() as block:

            @block.sync
            def _(sp):
                for dst, src in ((ident, w["ident"]), (sel, w["sel"]), (a_log, w["a_log"]),
                                 (d_skip, w["d_skip"]), (w_out, w["out_proj"])):
                    sp.dma_start(dst[:], src).then_inc(s_w, 16)
                for b in range(BATCH):
                    if b:
                        sp.wait_ge(s_o, b)
                    sp.dma_start(u[:], scratch["u"][b]).then_inc(s_uz, 16)
                    sp.dma_start(zs[:], scratch["zs"][b]).then_inc(s_uz, 16)
                    for s in range(STATE):
                        if b:
                            sp.wait_ge(s_hc, (b - 1) * NIT + STATE + s + 1)
                        sp.dma_start(c_bc[:, s], scratch["c"][b, s:s + 1, :].to_broadcast([P, SEQ])).then_inc(s_c[s], 16)

            def accumulate(pe, b, i):
                blk, s = i // STATE, i % STATE
                if s == 0:
                    if i:
                        pe.wait_ge(s_y1, NBLK * b + blk)
                    else:
                        pe.wait_ge(s_y1, NBLK * b)
                pe.wait_ge(s_hc, b * NIT + i + 1)
                for c in range(CPB):
                    mm = pe.matmul(p_y[:, c * CH:(c + 1) * CH], ident[:], hc[:, i % 2, c * CH:(c + 1) * CH],
                                   start=(s == 0), stop=(s == STATE - 1))
                mm.then_inc(s_acc, 1)

            @block.tensor
            def _(pe):
                pe.wait_ge(s_w, 16 * 5)
                with pe.Fori(0, BATCH) as b:
                    for i in range(NIT):
                        s = i % STATE
                        if i >= 2:
                            pe.wait_ge(s_scan, b * NIT + i - 1)
                        else:
                            pe.wait_ge(s_scan, b * NIT)
                        for c in range(CPB):
                            mm = pe.matmul(p_b[:, i % 2, c * CH:(c + 1) * CH], sel[:, s],
                                           bc_split[:, bass.ds(b * SEQ + c * CH, CH)], start=True, stop=True)
                        mm.then_inc(s_b, 1)
                        if i >= 2:
                            accumulate(pe, b, i - 2)
                    accumulate(pe, b, NIT - 2)
                    accumulate(pe, b, NIT - 1)
                    pe.wait_ge(s_y, (b + 1) * NBLK)
                    pe.wait_ge(s_x, b)
                    for c in range(CPB):
                        for k in range(NBLK):
                            mm = pe.matmul(p_o[:, c * CH:(c + 1) * CH], w_out[:, k], y1[:, k, c * CH:(c + 1) * CH],
                                           start=(k == 0), stop=(k == NBLK - 1))
                    mm.then_inc(s_o, 1)

            @block.scalar
            def _(act):
                act.wait_ge(s_w, 16 * 5)
                act.activation(a_exp[:], a_log[:], ACT.Exp).then_inc(s_a, 1)
                act.wait_ge(s_a, 1)
                act.mul(a_neg[:], a_exp[:], -1.0).then_inc(s_a, 1)
                act.wait_ge(s_a, 2)
                with act.Fori(0, BATCH) as b:
                    for i in range(NIT):
                        blk, s = i // STATE, i % STATE
                        act.wait_ge(s_scan, b * NIT + max(i - 1, 0))
                        waited(act, hold)
                        act.activation(decay[:, i % 2], delta[:, bass.ds(b, 1), blk, :].rearrange("p o t -> p (o t)"), ACT.Exp,
                                       scale=a_neg[:, blk, s:s + 1]).then_inc(s_dec, 1)

            def gate(dve, b, blk):
                dve.wait_ge(s_acc, b * NIT + (blk + 1) * STATE)
                dve.wait_ge(s_uz, (b + 1) * 32)
                dve.scalar_tensor_tensor(y1[:, blk], u[:, blk], d_skip[:, blk:blk + 1], p_y[:], ALU.mult, ALU.add).then_inc(s_y1, 1)
                dve.wait_ge(s_y1, b * NBLK + blk + 1)
                dve.tensor_tensor(y1[:, blk], y1[:, blk], zs[:, blk], ALU.mult).then_inc(s_y, 1)

            @block.vector
            def _(dve):
                dve.wait_ge(s_w, 16 * 5)

                def times_b(b, i):
                    dve.wait_ge(s_b, b * NIT + i + 1)
                    dve.tensor_tensor(p_b[:, i % 2], du[:, bass.ds(b, 1), i // STATE, :].rearrange("p o t -> p (o t)"), p_b[:, i % 2], ALU.mult).then_inc(s_dbu, 1)

                with dve.Fori(0, BATCH) as b:
                    times_b(b, 0)
                    for i in range(NIT):
                        if i + 1 < NIT:
                            times_b(b, i + 1)
                        dve.wait_ge(s_dec, b * NIT + i + 1)
                        dve.wait_ge(s_dbu, b * NIT + i + 1)
                        dve.wait_ge(s_hc, b * NIT + max(i - 1, 0))
                        dve.tensor_tensor_scan(h[:, i % 2], decay[:, i % 2], p_b[:, i % 2], 0.0, ALU.mult, ALU.add).then_inc(s_scan, 1)
                        if i == STATE + 1:
                            gate(dve, b, 0)
                    gate(dve, b, 1)
                    dve.wait_ge(s_o, b + 1)
                    xt = xT[:, bass.ds(b * SEQ, SEQ)]
                    dve.tensor_tensor(xt, xt, p_o[:], ALU.add).then_inc(s_x, 1)

            @block.gpsimd
            def _(pool):
                with pool.Fori(0, BATCH) as b:
                    for i in range(NIT):
                        blk, s = i // STATE, i % STATE
                        pool.wait_ge(s_scan, b * NIT + i + 1)
                        pool.wait_ge(s_c[s], b * 16 + 16)
                        pool.wait_ge(s_acc, b * NIT + max(i - 1, 0))
                        pool.tensor_tensor(hc[:, i % 2], h[:, i % 2], c_bc[:, s], ALU.mult).then_inc(s_hc, 1)


EXP0, HID0, SHARED = 16, 256, 2
SLOTS0 = EXP0 + SHARED
TOPK = 2
CAP = -(-TOK * TOPK * 5 // (EXP0 * 4))
FILL = -3.4028234663852886e38


def layer_norm(nc, xT, lnT, w, name):
    with Phase(nc, name) as ph:
        ones = ph.sb("ones_over_d", [P, P])
        eps = ph.sb("eps", [P, 1])
        sq = ph.sb("sq", [P, SEQ])
        lnv = ph.sb("lnv", [P, SEQ])
        rstd = ph.sb("rstd", [P, SEQ])
        p_mean = ph.ps("p_mean", [P, SEQ])
        p_var = ph.ps("p_var", [P, SEQ])
        s_w = ph.sem("ones_loaded")
        s_eps = ph.sem("eps_set")
        s_mean = ph.sem("mean_ready")
        s_xc = ph.sem("centred")
        s_sq = ph.sem("squared")
        s_var = ph.sem("var_ready")
        s_lnv = ph.sem("log_var")
        s_rstd = ph.sem("rstd_ready")
        s_xn = ph.sem("normed")
        hold = ph.sem("wait_passed")

        with ph.block() as block:
            @block.sync
            def _(sp):
                sp.dma_start(ones[:], w["ones_over_d"]).then_inc(s_w, 16)

            @block.tensor
            def _(pe):
                pe.wait_ge(s_w, 16)
                with pe.Fori(0, BATCH) as b:
                    pe.wait_ge(s_xc, b)
                    for c in range(CPB):
                        mm = pe.matmul(p_mean[:, c * CH:(c + 1) * CH], ones[:], xT[:, bass.ds(b * SEQ + c * CH, CH)],
                                       start=True, stop=True)
                    mm.then_inc(s_mean, 1)
                    pe.wait_ge(s_sq, b + 1)
                    for c in range(CPB):
                        mm = pe.matmul(p_var[:, c * CH:(c + 1) * CH], ones[:], sq[:, c * CH:(c + 1) * CH],
                                       start=True, stop=True)
                    mm.then_inc(s_var, 1)

            @block.scalar
            def _(act):
                act.wait_ge(s_eps, 1)
                with act.Fori(0, BATCH) as b:
                    act.wait_ge(s_xc, b + 1)
                    waited(act, hold)
                    act.activation(sq[:], lnT[:, bass.ds(b * SEQ, SEQ)], ACT.Square).then_inc(s_sq, 1)
                    act.wait_ge(s_var, b + 1)
                    act.activation(lnv[:], p_var[:], ACT.Ln, bias=eps[:]).then_inc(s_lnv, 1)
                    act.wait_ge(s_lnv, b + 1)
                    act.wait_ge(s_xn, b)
                    act.activation(rstd[:], lnv[:], ACT.Exp, scale=-0.5).then_inc(s_rstd, 1)

            @block.vector
            def _(dve):
                dve.memset(eps[:], EPS).then_inc(s_eps, 1)
                with dve.Fori(0, BATCH) as b:
                    seq = bass.ds(b * SEQ, SEQ)
                    dve.wait_ge(s_mean, b + 1)
                    dve.tensor_tensor(lnT[:, seq], xT[:, seq], p_mean[:], ALU.subtract).then_inc(s_xc, 1)
                    dve.wait_ge(s_rstd, b + 1)
                    dve.tensor_tensor(lnT[:, seq], lnT[:, seq], rstd[:], ALU.mult).then_inc(s_xn, 1)


def router0(nc, lnT, wtok, w):
    E, T = EXP0, NT
    U32 = mybir.dt.uint32
    with Phase(nc, "router") as ph:
        gate_w = ph.sb("gate_w", [P, E])
        gate_b = ph.sb("gate_b", [P, E])
        prio = ph.sb("prio", [P, E])
        before = ph.sb("before", [P, P], BF16)
        ones = ph.sb("ones", [P, P], BF16)
        again = ph.sb("again", [P, E, T])
        score = ph.sb("score", [P, T, E])
        tmp = ph.sb("tmp", [P, T, E])
        best = ph.sb("best", [P, T])
        norm = ph.sb("norm", [P, T])
        oh = ph.sb("oh", [P, 2, T, E])
        logit = ph.sb("logit", [P, T, E])
        asg = ph.sb("asg", [P, E, T])
        wk = ph.sb("wk", [P, E, T])
        bits = ph.sb("bits", [P, E], U32)
        cand = ph.sb("cand", [P, E], U32)
        flip = ph.sb("flip", [P, E], U32)
        add = ph.sb("add", [P, E], U32)
        cnt = ph.sb("cnt", [P, E])
        need = ph.sb("need", [P, E])
        ge = ph.sb("ge", [P, E, T], BF16)
        gt = ph.sb("gt", [P, E, T], BF16)
        eq = ph.sb("eq", [P, E, T], BF16)
        tot = ph.sb("tot", [P, E, T])
        cum = ph.sb("cum", [P, E, T])
        pre = ph.sb("pre", [P, E, T])
        keep = ph.sb("keep", [P, E, T])
        p_lg = ph.ps("p_lg", [P, T, E])
        p_cnt = ph.ps("p_cnt", [P, E, T])
        p_pre = ph.ps("p_pre", [P, E, T])
        s_w = ph.sem("weights_loaded")
        s_lg = ph.sem("logits_ready")
        s_v = ph.sem("vector_step")
        s_mask = ph.sem("mask_ready")
        s_cnt = ph.sem("count_ready")
        s_exp = ph.sem("exp_done")

        with ph.block() as block:
            @block.sync
            def _(sp):
                for dst, src in ((gate_w, w["gate_w"]), (gate_b, w["gate_b"]), (prio, w["prio"]),
                                 (before, w["before"]), (ones, w["ones_bf16"]), (again, w["again"])):
                    sp.dma_start(dst[:], src).then_inc(s_w, 16)

            @block.tensor
            def _(pe):
                pe.wait_ge(s_w, 16 * 6)
                for t in range(T):
                    mm = pe.matmul(p_lg[:, t], lnT[:, t * P:(t + 1) * P], gate_w[:], start=True, stop=True)
                mm.then_inc(s_lg, 1)
                with pe.Fori(0, 32) as n:
                    pe.wait_ge(s_mask, n + 1)
                    pe.matmul(p_cnt[:], ones[:], ge[:], start=True, stop=True).then_inc(s_cnt, 1)
                pe.wait_ge(s_mask, 33)
                pe.matmul(p_cnt[:], ones[:], gt[:], start=True, stop=True).then_inc(s_cnt, 1)
                pe.wait_ge(s_mask, 34)
                pe.matmul(p_pre[:], before[:], eq[:], start=True, stop=True)
                pe.matmul(p_cnt[:], ones[:], eq[:], start=True, stop=True).then_inc(s_cnt, 1)

            @block.scalar
            def _(act):
                act.wait_ge(s_v, 3)
                act.activation(tmp[:], score[:], ACT.Exp).then_inc(s_exp, 1)

            @block.vector
            def _(dve):
                count = [0]

                def step(ins):
                    count[0] += 1
                    ins.then_inc(s_v, 1)
                    dve.wait_ge(s_v, count[0])

                dve.wait_ge(s_w, 16 * 6)
                dve.wait_ge(s_lg, 1)
                step(dve.tensor_copy(logit[:], p_lg[:]))
                step(dve.tensor_reduce(best[:], logit[:], AX.X, ALU.max))
                over = best[:].rearrange("p (t o) -> p t o", o=1).to_broadcast([P, T, E])
                step(dve.tensor_tensor(score[:], logit[:], over, ALU.subtract))
                dve.wait_ge(s_exp, 1)
                step(dve.tensor_reduce(norm[:], tmp[:], AX.X, ALU.add))
                step(dve.reciprocal(norm[:], norm[:]))
                step(dve.tensor_tensor(score[:], tmp[:], norm[:].rearrange("p (t o) -> p t o", o=1).to_broadcast([P, T, E]), ALU.mult))
                bias = gate_b[:].rearrange("p (o e) -> p o e", o=1).to_broadcast([P, T, E])
                order = prio[:].rearrange("p (o e) -> p o e", o=1).to_broadcast([P, T, E])
                step(dve.tensor_tensor(score[:], score[:], bias, ALU.add))
                for k in range(TOPK):
                    step(dve.tensor_reduce(best[:], score[:], AX.X, ALU.max))
                    step(dve.tensor_tensor(tmp[:], score[:], over, ALU.is_ge))
                    step(dve.tensor_tensor(tmp[:], tmp[:], order, ALU.mult))
                    step(dve.tensor_reduce(best[:], tmp[:], AX.X, ALU.max))
                    step(dve.tensor_tensor(oh[:, k], over, order, ALU.is_equal))
                    if k == 0:
                        step(dve.scalar_tensor_tensor(score[:], oh[:, k], FILL, score[:], ALU.mult, ALU.add))
                by_expert = lambda a: a.rearrange("p t e -> p e t")
                step(dve.tensor_tensor(asg[:], by_expert(oh[:, 0]), by_expert(oh[:, 1]), ALU.add))
                step(dve.tensor_scalar(wk[:], asg[:], -1.0, -FILL, ALU.add, ALU.mult))
                step(dve.tensor_tensor(tot[:], asg[:], by_expert(logit[:]), ALU.mult))
                step(dve.tensor_tensor(wk[:], wk[:], tot[:], ALU.add))
                thr = cand[:].bitcast(F32).rearrange("p (e o) -> p e o", o=1).to_broadcast([P, E, T])

                def over_tokens(dst, value):
                    dve.wait_ge(s_cnt, value)
                    step(dve.tensor_reduce(dst, p_cnt[:], AX.X, ALU.add))

                step(dve.memset(cand[:], 0))
                dve.tensor_tensor(ge[:], wk[:], thr, ALU.is_ge).then_inc(s_mask, 1)
                over_tokens(cnt[:], 1)
                step(dve.tensor_scalar(bits[:], cnt[:], CAP - 0.5, float(2 ** 31), ALU.is_ge, ALU.mult))
                step(dve.tensor_scalar(flip[:], bits[:], 31, 31, ALU.logical_shift_right, ALU.logical_shift_left))
                step(dve.tensor_scalar(flip[:].bitcast(mybir.dt.int32), bits[:].bitcast(mybir.dt.int32), 31, None, ALU.arith_shift_right))
                step(dve.tensor_scalar(flip[:], flip[:], 0xFFFFFFFF, 0x80000000, ALU.bitwise_xor, ALU.bitwise_or))
                for n in range(1, 32):
                    bit = 1 << (31 - n)
                    step(dve.scalar_tensor_tensor(cand[:], bits[:], bit, flip[:], ALU.bitwise_or, ALU.bitwise_xor))
                    dve.tensor_tensor(ge[:], wk[:], thr, ALU.is_ge).then_inc(s_mask, 1)
                    over_tokens(cnt[:], n + 1)
                    step(dve.tensor_scalar(add[:], cnt[:], CAP - 0.5, float(bit), ALU.is_ge, ALU.mult))
                    step(dve.tensor_tensor(bits[:], bits[:], add[:], ALU.bitwise_or))
                step(dve.tensor_tensor(cand[:], bits[:], flip[:], ALU.bitwise_xor))
                dve.tensor_tensor(gt[:], wk[:], thr, ALU.is_gt).then_inc(s_mask, 1)
                step(dve.tensor_tensor(pre[:], wk[:], thr, ALU.is_equal))
                over_tokens(cnt[:], 33)
                dve.tensor_tensor(eq[:], pre[:], asg[:], ALU.mult).then_inc(s_mask, 1)
                step(dve.tensor_scalar(need[:], cnt[:], -1.0, float(CAP), ALU.mult, ALU.add))
                dve.wait_ge(s_cnt, 34)
                step(dve.tensor_copy(tot[:], p_cnt[:]))
                step(dve.tensor_tensor_scan(cum[:].rearrange("p e t -> p (e t)"), again[:].rearrange("p e t -> p (e t)"),
                                            tot[:].rearrange("p e t -> p (e t)"), 0.0, ALU.mult, ALU.add))
                step(dve.tensor_tensor(cum[:], cum[:], tot[:], ALU.subtract))
                step(dve.tensor_tensor(pre[:], cum[:], p_pre[:], ALU.add))
                step(dve.tensor_tensor(keep[:], pre[:], need[:].rearrange("p (e o) -> p e o", o=1).to_broadcast([P, E, T]), ALU.is_lt))
                step(dve.tensor_tensor(keep[:], keep[:], eq[:], ALU.mult))
                step(dve.tensor_tensor(keep[:], keep[:], gt[:], ALU.add))
                dve.tensor_tensor(wtok[:, 0:E], keep[:], by_expert(logit[:]), ALU.mult)
                dve.memset(wtok[:, E:SLOTS0], 1.0 / SHARED)


def experts0(nc, xT, lnT, wtok, w):
    M = HID0 // P
    UNITS = 2 * NCH
    with Phase(nc, "experts") as ph:
        ident = ph.sb("ident", [P, P])
        wts = ph.sb("wts", [P, 2, 3 * HID0])
        gated = ph.sb("gated", [P, M, CH])
        g = ph.sb("g", [P, 2, M, CH])
        acc = ph.sb("acc", [P, NT, D])
        p_h = ph.ps("p_h", [P, M, 2, CH])
        p_y = ph.ps("p_y", [P, 2, CH // P, D])
        s_id = ph.sem("ident_loaded")
        s_w = ph.sem("weights_loaded")
        s_zero = ph.sem("acc_zeroed")
        s_up = ph.sem("up_done")
        s_silu = ph.sem("silu_done")
        s_g = ph.sem("gated_ready")
        s_y = ph.sem("down_done")
        s_acc = ph.sem("accumulated")
        s_t = ph.sem("turned")
        s_x = ph.sem("residual_added")

        with ph.block() as block:
            @block.sync
            def _(sp):
                sp.dma_start(ident[:], w["ident"]).then_inc(s_id, 16)
                with sp.Fori(0, SLOTS0 // 2) as i:
                    for s in range(2):
                        sp.wait_ge(s_y, i * UNITS)
                        sp.dma_start(wts[:, s], w["ew"][bass.ds(i * 2 + s, 1)].rearrange("o p n -> p (o n)")).then_inc(s_w, 16)

            def down(pe, i, v):
                s = v // NCH
                pe.wait_ge(s_g, i * (UNITS * M) + (v + 1) * M)
                pe.wait_ge(s_acc, i * UNITS + max(v - 1, 0))
                for t in range(CH // P):
                    for k in range(M):
                        mm = pe.matmul(p_y[:, v % 2, t], g[:, v % 2, k, t * P:(t + 1) * P],
                                       wts[:, s, (2 * M + k) * P:(2 * M + k + 1) * P], start=(k == 0), stop=(k == M - 1))
                mm.then_inc(s_y, 1)

            @block.tensor
            def _(pe):
                with pe.Fori(0, SLOTS0 // 2) as i:
                    for v in range(UNITS):
                        s, c = v // NCH, v % NCH
                        if c == 0:
                            pe.wait_ge(s_w, i * 32 + 32)
                        for m in range(M):
                            pe.wait_ge(s_g, i * (UNITS * M) + (max((v - 1) * M + m + 1, 0)))
                            for j in range(2):
                                mm = pe.matmul(p_h[:, m, j], wts[:, s, (j * M + m) * P:(j * M + m + 1) * P],
                                               lnT[:, c * CH:(c + 1) * CH], start=True, stop=True)
                            mm.then_inc(s_up, 1)
                        if v:
                            down(pe, i, v - 1)
                    down(pe, i, UNITS - 1)
                pe.wait_ge(s_id, 16)
                for c in range(NCH):
                    pe.wait_ge(s_acc, SLOTS0 * NCH)
                    if c >= 2:
                        pe.wait_ge(s_x, c - 1)
                    for t in range(CH // P):
                        mm = pe.transpose(p_y[:, c % 2, t], acc[:, c * (CH // P) + t], ident[:])
                    mm.then_inc(s_t, 1)

            @block.scalar
            def _(act):
                with act.Fori(0, SLOTS0 // 2) as i:
                    for v in range(UNITS):
                        for m in range(M):
                            act.wait_ge(s_up, i * (UNITS * M) + v * M + m + 1)
                            act.activation(gated[:, m], p_h[:, m, 0], ACT.Silu).then_inc(s_silu, 1)

            def accumulate(dve, i, v):
                s, c = v // NCH, v % NCH
                dve.wait_ge(s_y, i * UNITS + v + 1)
                for t in range(CH // P):
                    tile = c * (CH // P) + t
                    ins = dve.scalar_tensor_tensor(acc[:, tile], p_y[:, v % 2, t], wtok[:, bass.ds(i * 2 + s, 1), tile],
                                                   acc[:, tile], ALU.mult, ALU.add)
                ins.then_inc(s_acc, 1)

            @block.vector
            def _(dve):
                dve.memset(acc[:], 0.0).then_inc(s_zero, 1)
                dve.wait_ge(s_zero, 1)
                with dve.Fori(0, SLOTS0 // 2) as i:
                    for v in range(UNITS):
                        for m in range(M):
                            dve.wait_ge(s_silu, i * (UNITS * M) + v * M + m + 1)
                            dve.wait_ge(s_y, i * UNITS + max(v - 1, 0))
                            dve.tensor_tensor(g[:, v % 2, m], gated[:, m], p_h[:, m, 1], ALU.mult).then_inc(s_g, 1)
                        if v:
                            accumulate(dve, i, v - 1)
                    accumulate(dve, i, UNITS - 1)
                for c in range(NCH):
                    dve.wait_ge(s_t, c + 1)
                    dve.tensor_tensor(xT[:, c * CH:(c + 1) * CH], xT[:, c * CH:(c + 1) * CH],
                                      p_y[:, c % 2].rearrange("p t d -> p (t d)"), ALU.add).then_inc(s_x, 1)


HEADS, DH = 16, 8
GH = 4
GROUPS = HEADS // GH
UNITS = BATCH * GROUPS
KT = SEQ // P
VW = DH + 1
PARTS = 3
PAIRS = PARTS * PARTS
MROW = 96
SCALE = DH ** -0.5
MASKED = -1e30


def qkv(nc, lnT, w, scratch):
    with Phase(nc, "qkv") as ph:
        wqk = ph.sb("wqk", [P, 2, P])
        wv = ph.sb("wv", [P, P])
        rest = ph.sb("rest", [P, CH])
        parts = ph.sb("parts", [P, 2, PARTS, CH], BF16)
        vp = ph.sb("vp", [P, 2, GROUPS, CH // P, GH, VW])
        p_qk = ph.ps("p_qk", [P, 2, CH])
        p_v = ph.ps("p_v", [P, CH // P, P])
        s_w = ph.sem("weights_loaded")
        s_one = ph.sem("ones_set")
        s_qk = ph.sem("projected")
        s_hi = ph.sem("hi_cut")
        s_rest = ph.sem("rest_cut")
        s_mid = ph.sem("mid_cut")
        s_cut = ph.sem("parts_ready")
        s_v = ph.sem("v_projected")
        s_vc = ph.sem("v_copied")
        s_st = [ph.sem(f"parts_stored{i}") for i in range(2)]
        s_vst = [ph.sem(f"v_stored{i}") for i in range(2)]

        with ph.block() as block:
            @block.sync
            def _(sp):
                sp.dma_start(wqk[:], w["wqk"]).then_inc(s_w, 16)
                sp.dma_start(wv[:], w["wv"]).then_inc(s_w, 16)
                with sp.Fori(0, BATCH) as b:
                    for c in range(CPB):
                        for j in range(2):
                            sp.wait_ge(s_cut, b * 4 + 2 * c + j + 1)
                            for a in range(PARTS + 2 * j):
                                sp.dma_start(scratch["parts"][j, bass.ds(b, 1), :, a, :, c * CH:(c + 1) * CH]
                                             .rearrange("o h r t -> (o h) r t"),
                                             parts[:, j, a % PARTS]).then_inc(s_st[j], 16)
                        sp.wait_ge(s_vc, b * 2 + c + 1)
                        sp.dma_start(scratch["v"][bass.ds(b, 1), :, :, c * (KT // CPB):(c + 1) * (KT // CPB)]
                                     .rearrange("o g p k n -> p (o g) k n"),
                                     vp[:, c].rearrange("p g k h v -> p g k (h v)")).then_inc(s_vst[c], 16)
                for j in range(2):
                    sp.wait_ge(s_st[j], 16 * (PARTS + 2 * j) * NCH)
                    sp.wait_ge(s_vst[j], 16 * BATCH)

            @block.tensor
            def _(pe):
                pe.wait_ge(s_w, 32)
                for g in range(NCH):
                    for j in range(2):
                        pe.wait_ge(s_rest, 2 * max(g - 1, 0) + j + 1 if g else 0)
                        pe.matmul(p_qk[:, j], wqk[:, j], lnT[:, g * CH:(g + 1) * CH], start=True, stop=True).then_inc(s_qk, 1)
                    pe.wait_ge(s_vc, g)
                    for t in range(CH // P):
                        mm = pe.matmul(p_v[:, t], lnT[:, g * CH + t * P:g * CH + (t + 1) * P], wv[:], start=True, stop=True)
                    mm.then_inc(s_v, 1)

            @block.scalar
            def _(act):
                act.wait_ge(s_one, 1)
                with act.Fori(0, BATCH) as b:
                    for c in range(CPB):
                        act.wait_ge(s_v, b * 2 + c + 1)
                        act.wait_ge(s_vst[c], b * 16)
                        for t in range(CH // P):
                            ins = act.activation(vp[:, c, :, t, :, 0:DH],
                                                 p_v[:, t].rearrange("p (g h v) -> p g h v", g=GROUPS, h=GH), ACT.Copy)
                        ins.then_inc(s_vc, 1)

            @block.vector
            def _(dve):
                dve.memset(vp[:], 1.0).then_inc(s_one, 1)
                with dve.Fori(0, NCH) as g:
                    for j in range(2):
                        n = g * 2 + j
                        dve.wait_ge(s_qk, n + 1)
                        dve.wait_ge(s_st[j], g * (16 * (PARTS + 2 * j)))
                        dve.tensor_copy(parts[:, j, 0], p_qk[:, j]).then_inc(s_hi, 1)
                        dve.wait_ge(s_hi, n + 1)
                        dve.wait_ge(s_cut, n)
                        dve.tensor_tensor(rest[:], p_qk[:, j], parts[:, j, 0], ALU.subtract).then_inc(s_rest, 1)
                        dve.wait_ge(s_rest, n + 1)
                        dve.tensor_copy(parts[:, j, 1], rest[:]).then_inc(s_mid, 1)
                        dve.wait_ge(s_mid, n + 1)
                        dve.tensor_tensor(parts[:, j, 2], rest[:], parts[:, j, 1], ALU.subtract).then_inc(s_cut, 1)


def attention(nc, w, scratch):
    NMAX = GH * (KT + KT // 2)
    NST = KT + KT // 2
    LOADS = 16 * (3 + 3 + 1)
    with Phase(nc, "attn") as ph:
        identb = ph.sb("identb", [P, P], BF16)
        mask_q = ph.sb("mask_q", [P, P], BF16)
        mask_k = ph.sb("mask_k", [P, P], BF16)
        qs = [ph.sb(f"qs{i}", [P, GH, SEQ], BF16) for i in range(2)]
        ks = [ph.sb(f"ks{i}", [P, GH, SEQ], BF16) for i in range(2)]
        vs = [ph.sb(f"vs{i}", [P, KT, GH, VW]) for i in range(2)]
        mx = ph.sb("mx", [P, 2, GH, KT])
        top = ph.sb("top", [P, GH * KT])
        ntop = ph.sb("ntop", [P, GH * KT])
        mrest = ph.sb("mrest", [P, GH * KT])
        mparts = ph.sb("mparts", [P, PARTS, GH * KT], BF16)
        mt = ph.sb("mt", [PARTS * GH * KT, P], BF16)
        prob = ph.sb("prob", [P, 2, GH, CH])
        ob = ph.sb("ob", [P, 2, CH])
        p_m = ph.ps("p_m", [P, 3, CH])
        p_t = p_m[0:PARTS * GH * KT, 0, 0:P // 2].bitcast(BF16)
        p_s = ph.ps("p_s", [P, 2, 2, CH])
        p_o = ph.ps("p_o", [P, CH])

        s_w = ph.sem("masks_loaded")
        s_qset = ph.sem("query_stacks_zeroed")
        s_kset = ph.sem("key_stacks_set")
        s_mx0 = ph.sem("maxima_filled")
        s_po0 = ph.sem("out_bank_zeroed")
        s_load = [ph.sem(f"loaded{i}") for i in range(2)]
        s_qz = ph.sem("max_rows_zeroed")
        s_mm = ph.sem("scores_for_max")
        s_red = ph.sem("maxima_taken")
        s_m = ph.sem("max_step")
        s_mid = ph.sem("max_mid_cut")
        s_kz = ph.sem("key_stacks_zeroed")
        s_mp = ph.sem("max_parts_ready")
        s_tr = ph.sem("max_turned")
        s_mt = ph.sem("max_copied")
        s_mrow = ph.sem("max_rows_loaded")
        s_st = ph.sem("scores_ready")
        s_exp = ph.sem("exp_done")
        s_pv = ph.sem("pv_done")
        s_ev = ph.sem("out_copied")
        s_out = [ph.sem(f"out_stored{i}") for i in range(2)]
        hold = ph.sem("wait_passed")

        with ph.block() as block:
            pairs = UNITS // 2

            @block.sync
            def _(sp):
                for dst, src in ((identb, w["ident_bf16"]), (mask_q, w["mask_q"]), (mask_k, w["mask_k"])):
                    sp.dma_start(dst[:], src).then_inc(s_w, 16)
                sp.wait_ge(s_qset, 2)
                sp.wait_ge(s_kset, 1)

                def load(u, s):
                    part = scratch["parts"].rearrange("j b (g h) a r t -> j (b g) (a r) h t", g=GROUPS)
                    for m in range(PARTS):
                        rows = slice(m * PARTS * DH, (m + 1) * PARTS * DH)
                        for j, dst, first in ((0, qs[s], 0), (1, ks[s], m)):
                            src = part[j, bass.ds(u, 1), first * DH:(first + PARTS) * DH]
                            sp.dma_start(dst[rows], src.rearrange("o a h t -> (o a) h t")).then_inc(s_load[s], 16)
                    v = scratch["v"].rearrange("b g p k n -> (b g) p k n")
                    sp.dma_start(vs[s][:].rearrange("p k h v -> p k (h v)"),
                                 v[bass.ds(u, 1)].rearrange("o p k n -> (o p) k n")).then_inc(s_load[s], 16)

                def max_rows(u, s):
                    sp.wait_ge(s_mt, u + 1)
                    for a in range(PARTS):
                        sp.dma_start(qs[s][MROW + a:MROW + a + 1].rearrange("a h (t p) -> a (h t) p", p=P),
                                     mt[a * GH * KT:(a + 1) * GH * KT]).then_inc(s_mrow, 16)

                def store(u, half):
                    sp.wait_ge(s_ev, u * 2 + half + 1)
                    out = scratch["o"].rearrange("u h v t -> u h v t")
                    for h in range(GH):
                        sp.dma_start(out[bass.ds(u, 1), h, :, half * CH:(half + 1) * CH].rearrange("o v t -> (o v) t"),
                                     ob[32 * h:32 * h + VW, half]).then_inc(s_out[half], 16)

                load(0, 0)
                max_rows(0, 0)

                def unit(u, s, last):
                    if not last:
                        sp.wait_ge(s_pv, u * NST)
                        load(u + 1, 1 - s)
                    store(u, 0)
                    if not last:
                        max_rows(u + 1, 1 - s)
                    store(u, 1)

                with sp.Fori(0, pairs - 1) as i:
                    unit(i * 2, 0, False)
                    unit(i * 2 + 1, 1, False)
                unit(UNITS - 2, 0, False)
                unit(UNITS - 1, 1, True)
                for half in range(2):
                    sp.wait_ge(s_out[half], 16 * GH * UNITS)

            maxima = [(qt, c, h) for qt in range(KT) for c in range(qt // (KT // 2) + 1) for h in range(GH)]
            steps = [(half, kt) for half in range(CPB) for kt in range((half + 1) * KT // 2)]

            def width(qt, c):
                return min(CH, (qt + 1) * P - c * CH)

            def first_query(half, kt):
                return max(kt * P - half * CH, 0)

            @block.tensor
            def _(pe):
                pe.wait_ge(s_w, 48)
                pe.wait_ge(s_po0, 1)

                def max_product(u, s, n, pair_of):
                    qt, c, h = maxima[n]
                    if n == 0:
                        pe.wait_ge(s_load[s], (pair_of + 1) * LOADS)
                        pe.wait_ge(s_qz, u + 1)
                        pe.wait_ge(s_mt, u)
                    pe.wait_ge(s_red, u * NMAX + max(n - 2, 0))
                    wd = width(qt, c)
                    diagonal = (qt + 1) * P - c * CH <= CH
                    mm = pe.matmul(p_m[:, n % 3, 0:wd], qs[s][:, h, qt * P:(qt + 1) * P],
                                   ks[s][:, h, c * CH:c * CH + wd], start=True, stop=not diagonal)
                    if diagonal:
                        mm = pe.matmul(p_m[:, n % 3, wd - P:wd], identb[:], mask_q[:], start=False, stop=True)
                    mm.then_inc(s_mm, 1)

                def turn(u):
                    pe.wait_ge(s_mp, u + 1)
                    pe.transpose(p_t, mparts[:].rearrange("p a n -> p (a n)"), identb[:]).then_inc(s_tr, 1)

                def scores(u, s, t, pair):
                    half, kt = steps[t]
                    q0 = first_query(half, kt)
                    k = 2 * t + pair
                    if k == 0:
                        pe.wait_ge(s_mrow, u * 48 + 48)
                    pe.wait_ge(s_exp, u * 2 * NST + max(k - 1, 0))
                    for j in range(2):
                        h = 2 * pair + j
                        on_diagonal = kt * P >= half * CH
                        mm = pe.matmul(p_s[:, pair, j, 0:CH - q0], ks[s][:, h, kt * P:(kt + 1) * P],
                                       qs[s][:, h, half * CH + q0:(half + 1) * CH], start=True, stop=not on_diagonal)
                        if on_diagonal:
                            mm = pe.matmul(p_s[:, pair, j, 0:P], identb[:], mask_k[:], start=False, stop=True)
                    mm.then_inc(s_st, 1)

                def values(u, s, t):
                    half, kt = steps[t]
                    q0 = first_query(half, kt)
                    if kt == 0:
                        pe.wait_ge(s_ev, u * 2 + half)
                    pe.wait_ge(s_exp, u * 2 * NST + 2 * t + 2)
                    for h in range(GH):
                        mm = pe.matmul(p_o[32 * h:32 * h + VW, q0:CH], vs[s][:, kt, h], prob[:, t % 2, h, 0:CH - q0],
                                       start=(kt == 0), stop=(kt == (half + 1) * KT // 2 - 1))
                    mm.then_inc(s_pv, 1)

                def unit(i, s, last):
                    u = i * 2 + s
                    ahead = 0
                    for t in range(NST):
                        scores(u, s, t, 0)
                        scores(u, s, t, 1)
                        if t:
                            values(u, s, t - 1)
                        if not last:
                            while ahead < NMAX * (t - 1) // (NST - 2) and ahead < NMAX:
                                max_product(u + 1, 1 - s, ahead, i + s)
                                ahead += 1
                    values(u, s, NST - 1)
                    if not last:
                        turn(u + 1)

                for n in range(NMAX):
                    max_product(0, 0, n, 0)
                turn(0)
                with pe.Fori(0, pairs - 1) as i:
                    unit(i, 0, False)
                    unit(i, 1, False)
                unit(pairs - 1, 0, False)
                unit(pairs - 1, 1, True)

            @block.scalar
            def _(act):
                def unit(u):
                    for t, (half, kt) in enumerate(steps):
                        q0 = first_query(half, kt)
                        for pair in range(2):
                            k = 2 * t + pair
                            act.wait_ge(s_st, u * 2 * NST + k + 1)
                            if pair == 0:
                                act.wait_ge(s_pv, u * NST + max(t - 1, 0))
                            act.activation(prob[:, t % 2, 2 * pair:2 * pair + 2, 0:CH - q0], p_s[:, pair, :, 0:CH - q0],
                                           ACT.Exp, scale=SCALE).then_inc(s_exp, 1)
                        if kt == (half + 1) * KT // 2 - 1:
                            act.wait_ge(s_pv, u * NST + t + 1)
                            act.wait_ge(s_out[half], u * (16 * GH))
                            act.activation(ob[:, half], p_o[:], ACT.Copy).then_inc(s_ev, 1)

                with act.Fori(0, UNITS) as u:
                    unit(u)

            @block.vector
            def _(dve):
                for s in range(2):
                    dve.memset(qs[s][:].bitcast(mybir.dt.uint32), 0).then_inc(s_qset, 1)
                dve.memset(p_o[:], 0.0).then_inc(s_po0, 1)
                dve.memset(mx[:], FILL).then_inc(s_mx0, 1)
                dve.wait_ge(s_mx0, 1)

                def find(u):
                    for n, (qt, c, h) in enumerate(maxima):
                        dve.wait_ge(s_mm, u * NMAX + n + 1)
                        dve.tensor_reduce(mx[:, c, h, qt:qt + 1], p_m[:, n % 3, 0:width(qt, c)], AX.X, ALU.max).then_inc(s_red, 1)
                    dve.wait_ge(s_red, (u + 1) * NMAX)
                    halves = mx[:].rearrange("p c h t -> p c (h t)")
                    dve.tensor_tensor(top[:], halves[:, 0], halves[:, 1], ALU.max).then_inc(s_m, 1)
                    dve.wait_ge(s_m, u * 4 + 1)
                    dve.wait_ge(s_tr, u)
                    dve.tensor_scalar(ntop[:], top[:], -1.0, None, ALU.mult).then_inc(s_m, 1)
                    dve.tensor_scalar(mparts[:, 0], top[:], -1.0, None, ALU.mult).then_inc(s_m, 1)
                    dve.wait_ge(s_m, u * 4 + 3)
                    dve.tensor_tensor(mrest[:], ntop[:], mparts[:, 0], ALU.subtract).then_inc(s_m, 1)
                    dve.wait_ge(s_m, u * 4 + 4)
                    dve.tensor_copy(mparts[:, 1], mrest[:]).then_inc(s_mid, 1)
                    dve.wait_ge(s_mid, u + 1)
                    dve.tensor_tensor(mparts[:, 2], mrest[:], mparts[:, 1], ALU.subtract).then_inc(s_mp, 1)
                    dve.wait_ge(s_tr, u + 1)
                    dve.wait_ge(s_mrow, u * 48)
                    dve.tensor_copy(mt[:], p_t).then_inc(s_mt, 1)

                with dve.Fori(0, UNITS) as u:
                    find(u)

            @block.gpsimd
            def _(pool):
                for s in range(2):
                    pool.memset(ks[s][:].bitcast(mybir.dt.uint32), 0).then_inc(s_kz, 1)
                pool.wait_ge(s_kz, 2)
                for s in range(2):
                    ins = pool.memset(ks[s][MROW:MROW + PARTS], 1.0)
                ins.then_inc(s_kset, 1)

                def zero(u, s, first):
                    if not first:
                        pool.wait_ge(s_pv, (u - 1) * NST)
                        waited(pool, hold)
                    pool.memset(qs[s][MROW:MROW + PARTS].bitcast(mybir.dt.uint32), 0).then_inc(s_qz, 1)
                pool.wait_ge(s_qset, 2)
                zero(0, 0, True)
                zero(1, 1, True)
                with pool.Fori(1, pairs) as i:
                    zero(i * 2, 0, False)
                    zero(i * 2 + 1, 1, False)


def attention_out(nc, xT, w, scratch):
    with Phase(nc, "attn_out") as ph:
        wo = ph.sb("wo", [P, D])
        num = ph.sb("num", [P, BATCH, SEQ])
        den = ph.sb("den", [P, BATCH, HEADS * SEQ // P])
        rden = ph.sb("rden", [P, BATCH, HEADS * SEQ // P])
        rbc = ph.sb("rbc", [P, BATCH, SEQ])
        att = ph.sb("att", [P, 2, SEQ])
        p_o = ph.ps("p_o", [P, 2, SEQ])
        s_w = ph.sem("weights_loaded")
        s_den = ph.sem("denominators_loaded")
        s_rec = ph.sem("reciprocals_ready")
        s_rst = ph.sem("reciprocals_stored")
        s_num = [ph.sem(f"numerators_loaded{i}") for i in range(BATCH)]
        s_att = ph.sem("divided")
        s_o = ph.sem("projected")
        s_x = ph.sem("residual_added")
        o_heads = scratch["o"].rearrange("(b g) h v t -> b (g h) v t", b=BATCH)

        with ph.block() as block:
            @block.sync
            def _(sp):
                sp.dma_start(wo[:], w["wo"]).then_inc(s_w, 16)
                for b in range(BATCH):
                    for h in range(HEADS):
                        sp.dma_start(den[KT * h:KT * (h + 1), b], o_heads[b, h, DH].rearrange("(k p) -> k p", p=P)).then_inc(s_den, 16)
                for b in range(BATCH):
                    for h in range(HEADS):
                        sp.dma_start(num[DH * h:DH * (h + 1), b], o_heads[b, h, 0:DH]).then_inc(s_num[b], 16)
                sp.wait_ge(s_rec, 1)
                for b in range(BATCH):
                    sp.dma_start(scratch["r"][b].rearrange("h (k p) -> (h k) p", p=P), rden[:, b]).then_inc(s_rst, 16)
                sp.wait_ge(s_rst, 16 * BATCH)
                for b in range(BATCH):
                    for h in range(HEADS):
                        sp.dma_start(rbc[DH * h:DH * (h + 1), b], scratch["r"][b, h:h + 1].to_broadcast([DH, SEQ])).then_inc(s_num[b], 16)

            @block.tensor
            def _(pe):
                pe.wait_ge(s_w, 16)
                for b in range(BATCH):
                    pe.wait_ge(s_att, b + 1)
                    if b >= 2:
                        pe.wait_ge(s_x, b - 1)
                    for c in range(CPB):
                        mm = pe.matmul(p_o[:, b % 2, c * CH:(c + 1) * CH], wo[:], att[:, b % 2, c * CH:(c + 1) * CH], start=True, stop=True)
                    mm.then_inc(s_o, 1)

            @block.vector
            def _(dve):
                dve.wait_ge(s_den, 16 * BATCH * HEADS)
                dve.reciprocal(rden[:], den[:]).then_inc(s_rec, 1)
                for b in range(BATCH + 1):
                    if b < BATCH:
                        dve.wait_ge(s_num[b], 16 * 2 * HEADS)
                        if b >= 2:
                            dve.wait_ge(s_o, b - 1)
                        dve.tensor_tensor(att[:, b % 2], num[:, b], rbc[:, b], ALU.mult).then_inc(s_att, 1)
                    if b:
                        dve.wait_ge(s_o, b)
                        xt = xT[:, (b - 1) * SEQ:b * SEQ]
                        dve.tensor_tensor(xt, xt, p_o[:, (b - 1) % 2], ALU.add).then_inc(s_x, 1)


EXP1, HID1 = 8, 512
THRESHOLD = 0.125


def router1(nc, xT, lnT, wtok, w):
    E, T = EXP1, NT
    with Phase(nc, "router1") as ph:
        ident = ph.sb("ident", [P, P])
        gate_w = ph.sb("gate_w", [P, E + 1])
        gate_b = ph.sb("gate_b", [P, E + 1])
        b2 = ph.sb("b2", [E, D])
        logit = ph.sb("logit", [P, T, E + 1])
        top = ph.sb("top", [P, T])
        score = ph.sb("score", [P, T, E])
        sig = ph.sb("sig", [P, T])
        total = ph.sb("total", [P, T])
        none = ph.sb("none", [P, T])
        tmp = ph.sb("tmp", [P, T, E])
        wt = ph.sb("wt", [E, TOK])
        p_lg = ph.ps("p_lg", [P, T, E + 1])
        p_t = ph.ps("p_t", [E, 2, CH])
        p_b = ph.ps("p_b", [P, 2, CH])
        s_w = ph.sem("weights_loaded")
        s_lg = ph.sem("logits_ready")
        s_v = ph.sem("vector_step")
        s_e = ph.sem("exp_done")
        s_wt = ph.sem("weights_ready")
        s_t = ph.sem("turned")
        s_tc = ph.sem("turned_copied")
        s_b = ph.sem("bias_product")
        s_x = ph.sem("residual_added")

        with ph.block() as block:
            @block.sync
            def _(sp):
                for dst, src in ((ident, w["ident"]), (gate_w, w["gate1_w"]), (gate_b, w["gate1_b"]), (b2, w["b2"])):
                    sp.dma_start(dst[:], src).then_inc(s_w, 16)

            @block.tensor
            def _(pe):
                pe.wait_ge(s_w, 64)
                for t in range(T):
                    mm = pe.matmul(p_lg[:, t], lnT[:, t * P:(t + 1) * P], gate_w[:], start=True, stop=True)
                mm.then_inc(s_lg, 1)
                pe.wait_ge(s_wt, 1)
                for c in range(NCH):
                    if c >= 2:
                        pe.wait_ge(s_tc, c - 1)
                        pe.wait_ge(s_x, c - 1)
                    for t in range(CH // P):
                        mm = pe.transpose(p_t[:, c % 2, t * P:(t + 1) * P], tmp[:, c * (CH // P) + t], ident[:])
                    mm.then_inc(s_t, 1)
                    pe.wait_ge(s_tc, c + 1)
                    pe.matmul(p_b[:, c % 2], b2[:], wt[:, c * CH:(c + 1) * CH], start=True, stop=True).then_inc(s_b, 1)

            @block.scalar
            def _(act):
                act.wait_ge(s_v, 3)
                act.activation(tmp[:], score[:], ACT.Exp).then_inc(s_e, 1)
                act.activation(sig[:], logit[:, :, E], ACT.Exp, scale=-1.0).then_inc(s_e, 1)

            @block.vector
            def _(dve):
                count = [0]

                def step(ins):
                    count[0] += 1
                    ins.then_inc(s_v, 1)
                    dve.wait_ge(s_v, count[0])

                over = lambda a: a.unsqueeze(2).to_broadcast([P, T, E])
                dve.wait_ge(s_w, 64)
                dve.wait_ge(s_lg, 1)
                step(dve.tensor_tensor(logit[:], p_lg[:], gate_b[:].unsqueeze(1).to_broadcast([P, T, E + 1]), ALU.add))
                step(dve.tensor_reduce(top[:], logit[:, :, 0:E], AX.X, ALU.max))
                step(dve.tensor_tensor(score[:], logit[:, :, 0:E], over(top[:]), ALU.subtract))
                dve.wait_ge(s_e, 2)
                step(dve.tensor_reduce(total[:], tmp[:], AX.X, ALU.add))
                step(dve.reciprocal(total[:], total[:]))
                step(dve.tensor_scalar(sig[:], sig[:], 1.0, None, ALU.add))
                step(dve.reciprocal(sig[:], sig[:]))
                step(dve.tensor_scalar(sig[:], sig[:], THRESHOLD, None, ALU.mult))
                step(dve.tensor_tensor(score[:], tmp[:], over(total[:]), ALU.mult))
                step(dve.tensor_tensor(score[:], score[:], over(sig[:]), ALU.subtract))
                step(dve.tensor_scalar(score[:], score[:], 0.0, None, ALU.max))
                step(dve.tensor_reduce(total[:], score[:], AX.X, ALU.add))
                step(dve.tensor_scalar(none[:], total[:], 0.0, None, ALU.is_equal))
                step(dve.tensor_tensor(total[:], total[:], none[:], ALU.add))
                step(dve.reciprocal(total[:], total[:]))
                step(dve.tensor_tensor(tmp[:], score[:], over(total[:]), ALU.mult))
                dve.tensor_copy(wtok[:], tmp[:].rearrange("p t e -> p e t")).then_inc(s_wt, 1)
                for c in range(NCH):
                    dve.wait_ge(s_t, c + 1)
                    dve.tensor_copy(wt[:, c * CH:(c + 1) * CH], p_t[:, c % 2]).then_inc(s_tc, 1)
                    dve.wait_ge(s_b, c + 1)
                    xt = xT[:, c * CH:(c + 1) * CH]
                    dve.tensor_tensor(xt, xt, p_b[:, c % 2], ALU.add).then_inc(s_x, 1)


def experts1(nc, xT, lnT, wtok, w):
    F = HID1 // P
    NU = 2 * NCH
    with Phase(nc, "experts1") as ph:
        ident = ph.sb("ident", [P, P])
        b1 = ph.sb("b1", [P, EXP1, F])
        wts = ph.sb("wts", [P, 2, 2 * HID1])
        g = ph.sb("g", [P, 2, F, CH])
        acc = ph.sb("acc", [P, NT, D])
        p_h = ph.ps("p_h", [P, F, CH])
        p_y = ph.ps("p_y", [P, 2, CH // P, D])
        s_id = ph.sem("consts_loaded")
        s_w = ph.sem("weights_loaded")
        s_zero = ph.sem("acc_zeroed")
        s_up = ph.sem("up_done")
        s_g = ph.sem("gelu_done")
        s_y = ph.sem("down_done")
        s_acc = ph.sem("accumulated")
        s_t = ph.sem("turned")
        s_x = ph.sem("residual_added")
        hold = ph.sem("wait_passed")

        with ph.block() as block:
            @block.sync
            def _(sp):
                sp.dma_start(ident[:], w["ident"]).then_inc(s_id, 16)
                sp.dma_start(b1[:], w["b1"]).then_inc(s_id, 16)
                with sp.Fori(0, EXP1 // 2) as i:
                    for s in range(2):
                        sp.wait_ge(s_y, i * NU)
                        sp.dma_start(wts[:, s], w["fw"][bass.ds(i * 2 + s, 1)].rearrange("o p n -> p (o n)")).then_inc(s_w, 16)

            def down(pe, i, v):
                s = v // NCH
                pe.wait_ge(s_g, i * (NU * F) + (v + 1) * F)
                pe.wait_ge(s_acc, i * NU + max(v - 1, 0))
                for t in range(CH // P):
                    for k in range(F):
                        mm = pe.matmul(p_y[:, v % 2, t], g[:, v % 2, k, t * P:(t + 1) * P],
                                       wts[:, s, (F + k) * P:(F + k + 1) * P], start=(k == 0), stop=(k == F - 1))
                mm.then_inc(s_y, 1)

            @block.tensor
            def _(pe):
                pe.wait_ge(s_id, 32)
                with pe.Fori(0, EXP1 // 2) as i:
                    for v in range(NU):
                        s, c = v // NCH, v % NCH
                        if c == 0:
                            pe.wait_ge(s_w, i * 32 + 32)
                        for m in range(F):
                            pe.wait_ge(s_g, i * (NU * F) + max((v - 1) * F + m + 1, 0))
                            pe.matmul(p_h[:, m], wts[:, s, m * P:(m + 1) * P], lnT[:, c * CH:(c + 1) * CH],
                                      start=True, stop=True).then_inc(s_up, 1)
                        if v:
                            down(pe, i, v - 1)
                    down(pe, i, NU - 1)
                for c in range(NCH):
                    pe.wait_ge(s_acc, EXP1 * NCH)
                    if c >= 2:
                        pe.wait_ge(s_x, c - 1)
                    for t in range(CH // P):
                        mm = pe.transpose(p_y[:, c % 2, t], acc[:, c * (CH // P) + t], ident[:])
                    mm.then_inc(s_t, 1)

            @block.scalar
            def _(act):
                act.wait_ge(s_id, 32)
                with act.Fori(0, EXP1 // 2) as i:
                    for v in range(NU):
                        for m in range(F):
                            act.wait_ge(s_up, i * (NU * F) + v * F + m + 1)
                            act.wait_ge(s_y, i * NU + max(v - 1, 0))
                            waited(act, hold)
                            act.activation(g[:, v % 2, m], p_h[:, m], ACT.Gelu_apprx_tanh,
                                           bias=b1[:, bass.ds(i * 2 + v // NCH, 1), m]).then_inc(s_g, 1)

            def accumulate(dve, i, v):
                s, c = v // NCH, v % NCH
                dve.wait_ge(s_y, i * NU + v + 1)
                for t in range(CH // P):
                    tile = c * (CH // P) + t
                    ins = dve.scalar_tensor_tensor(acc[:, tile], p_y[:, v % 2, t], wtok[:, bass.ds(i * 2 + s, 1), tile],
                                                   acc[:, tile], ALU.mult, ALU.add)
                ins.then_inc(s_acc, 1)

            @block.vector
            def _(dve):
                dve.memset(acc[:], 0.0).then_inc(s_zero, 1)
                dve.wait_ge(s_zero, 1)
                with dve.Fori(0, EXP1 // 2) as i:
                    for v in range(NU):
                        accumulate(dve, i, v)
                for c in range(NCH):
                    dve.wait_ge(s_t, c + 1)
                    dve.tensor_tensor(xT[:, c * CH:(c + 1) * CH], xT[:, c * CH:(c + 1) * CH],
                                      p_y[:, c % 2].rearrange("p t d -> p (t d)"), ALU.add).then_inc(s_x, 1)


def shape_constants():
    import numpy as np
    bf16 = mybir.dt.np(BF16)
    sel = np.zeros((P, STATE, P), np.float32)
    for s in range(STATE):
        for part in range(3):
            sel[32 * part + s, s, :] = 1.0
    return {
        "ones_over_d": np.full((P, P), 1.0 / D, np.float32),
        "ident": np.eye(P, dtype=np.float32),
        "sel": sel.astype(bf16),
        "prio": np.tile(EXP0 - np.arange(EXP0, dtype=np.float32), (P, 1)),
        "before": np.triu(np.ones((P, P), np.float32), 1).astype(bf16),
        "ones_bf16": np.ones((P, P), bf16),
        "ident_bf16": np.eye(P).astype(bf16),
        "mask_q": (np.triu(np.ones((P, P), np.float32), 1) * MASKED).astype(bf16),
        "mask_k": (np.tril(np.ones((P, P), np.float32), -1) * MASKED).astype(bf16),
        "again": np.tile((np.arange(NT) > 0).astype(np.float32), (P, EXP0, 1)),
    }


def lay_out(inputs):
    import numpy as np
    i = {k: np.asarray(v) for k, v in inputs.items()}
    c = np.ascontiguousarray

    def blocks(a):
        return c(a.reshape((NBLK, P) + a.shape[1:]).swapaxes(0, 1))

    out = {"x": c(i["L0_attn_x"].reshape(TOK, D).T)}
    out["in_proj"] = c(i["L0_attn_in_proj_w"].T)
    out["norm_w"] = c(i["L0_attn_norm_w"].reshape(P, 1))
    out["conv_w"] = blocks(i["L0_attn_conv_w"])
    out["conv_b"] = blocks(i["L0_attn_conv_b"])
    xp = i["L0_attn_x_proj_w"]
    wide = np.zeros((P, INNER), xp.dtype)
    for part in range(3):
        wide[32 * part:32 * part + 32] = xp[RANK:]
    wide[96:96 + RANK] = xp[:RANK]
    out["x_proj"] = blocks(c(wide.T))
    dt = np.zeros((P, INNER), xp.dtype)
    dt[96:96 + RANK] = i["L0_attn_dt_proj_w"].T
    out["dt_proj"] = dt
    out["dt_b"] = blocks(i["L0_attn_dt_proj_b"])
    out["a_log"] = blocks(i["L0_attn_A_log"])
    out["d_skip"] = blocks(i["L0_attn_D"])
    out["out_proj"] = blocks(c(i["L0_attn_out_proj_w"].T))
    out["gate_w"] = c(i["L0_ffn_gate_w"])
    out["gate_b"] = c(np.broadcast_to(i["L0_ffn_gate_b"], (P, EXP0)))

    def expert(w1, w3, w2):
        down = w2.reshape(w2.shape[0], HID0 // P, P, D).swapaxes(1, 2).reshape(w2.shape[0], P, HID0)
        return np.concatenate([w1, w3, down], axis=2)

    out["ew"] = np.concatenate([expert(i["L0_ffn_ew1"], i["L0_ffn_ew3"], i["L0_ffn_ew2"]),
                                expert(i["L0_ffn_sw1"], i["L0_ffn_sw3"], i["L0_ffn_sw2"])], axis=0)
    hk = HEADS * DH
    out["wqk"] = np.stack([i["L1_attn_WQ"].reshape(hk, D).T, i["L1_attn_WK"].reshape(hk, D).T], axis=1)
    out["wv"] = c(i["L1_attn_WV"].reshape(hk, D).T)
    out["wo"] = c(i["L1_attn_WO"].transpose(0, 2, 1).reshape(hk, D))
    out["gate1_w"] = np.concatenate([i["L1_ffn_Wg"], i["L1_ffn_Wt"]], axis=1)
    out["gate1_b"] = c(np.broadcast_to(np.concatenate([i["L1_ffn_bg"], i["L1_ffn_bt"]]), (P, EXP1 + 1)))
    out["b1"] = c(i["L1_ffn_b1"].reshape(EXP1, HID1 // P, P).transpose(2, 0, 1))
    out["b2"] = c(i["L1_ffn_b2"])
    down = i["L1_ffn_W2"].reshape(EXP1, HID1 // P, P, D).swapaxes(1, 2).reshape(EXP1, P, HID1)
    out["fw"] = np.concatenate([i["L1_ffn_W1"], down], axis=2)
    return out


def program(nc, w, scratch, yT, stages=("mamba", "moe0", "attn", "moe1"), x_in=None):
    with Phase(nc, "main") as main:
        xT = main.sb("xT", [P, TOK])
        if x_in is not None:
            with Phase(nc, "load") as ph:
                s_x = ph.sem("x_loaded")
                with ph.block() as block:
                    @block.sync
                    def _(sp):
                        sp.dma_start(xT[:], x_in).then_inc(s_x, 16)
                        sp.wait_ge(s_x, 16)
        if "mamba" in stages:
            with Phase(nc, "mamba") as ph:
                delta = ph.sb("delta", [P, BATCH, NBLK, SEQ])
                du = ph.sb("du", [P, BATCH, NBLK, SEQ])
                bc_split = ph.sb("bc_split", [P, TOK], BF16)
                mamba_prep(nc, xT, delta, du, bc_split, w["x"], w, scratch)
                mamba_scan(nc, xT, delta, du, bc_split, w, scratch)
        if "moe0" in stages:
            with Phase(nc, "moe0") as ph:
                lnT = ph.sb("lnT", [P, TOK])
                wtok = ph.sb("wtok", [P, SLOTS0, NT])
                layer_norm(nc, xT, lnT, w, "norm1")
                router0(nc, lnT, wtok, w)
                experts0(nc, xT, lnT, wtok, w)
        if "attn" in stages:
            with Phase(nc, "qkv_of") as ph:
                lnT = ph.sb("lnT", [P, TOK])
                layer_norm(nc, xT, lnT, w, "norm2")
                qkv(nc, lnT, w, scratch)
            attention(nc, w, scratch)
            attention_out(nc, xT, w, scratch)
        if "moe1" in stages:
            with Phase(nc, "moe1") as ph:
                lnT = ph.sb("lnT", [P, TOK])
                wtok = ph.sb("wtok", [P, EXP1, NT])
                layer_norm(nc, xT, lnT, w, "norm3")
                router1(nc, xT, lnT, wtok, w)
                experts1(nc, xT, lnT, wtok, w)
        with Phase(nc, "store") as ph:
            s_y = ph.sem("y_stored")
            with ph.block() as block:
                @block.sync
                def _(sp):
                    sp.dma_start(yT, xT[:]).then_inc(s_y, 16)
                    sp.wait_ge(s_y, 16)


SCRATCH = {
    "u": ((BATCH, P, NBLK, SEQ), F32), "zs": ((BATCH, P, NBLK, SEQ), F32), "c": ((BATCH, STATE, SEQ), F32),
    "parts": ((2, BATCH, HEADS, PARTS + 2, DH, SEQ), BF16), "v": ((BATCH, GROUPS, P, KT, GH * VW), F32),
    "o": ((UNITS, GH, VW, SEQ), F32), "r": ((BATCH, HEADS, SEQ), F32),
}


def kernel(**inputs):
    import numpy as np
    import concourse.bacc as bacc
    from concourse.bass_utils import run_bass_kernel_spmd

    nc = bacc.Bacc("TRN2", target_bir_lowering=False, num_devices=1)
    arrays = {f"{k}_dram": v for k, v in {**lay_out(inputs), **shape_constants()}.items()}
    w = {k[:-5]: nc.dram_tensor(k, v.shape, mybir.dt.from_np(v.dtype), kind="ExternalInput").ap() for k, v in arrays.items()}
    scratch = {k: nc.dram_tensor(f"{k}_scratch", s, dt, kind="Internal").ap() for k, (s, dt) in SCRATCH.items()}
    yT = nc.dram_tensor("y_dram", (P, TOK), F32, kind="ExternalOutput").ap()
    program(nc, w, scratch, yT)
    got = run_bass_kernel_spmd(nc, [arrays], core_ids=[0]).results[0]["y_dram"]
    return np.ascontiguousarray(got.T).reshape(BATCH, SEQ, D)
```

```python
from contextlib import ExitStack

import concourse.bass as bass
from concourse import mybir

F32 = mybir.dt.float32
BF16 = mybir.dt.bfloat16
ALU = mybir.AluOpType
ACT = mybir.ActivationFunctionType
AX = mybir.AxisListType

P = 128
D = 128
BATCH, SEQ = 4, 1024
TOK = BATCH * SEQ
CH = 512
NCH = TOK // CH
CPB = SEQ // CH
NT = TOK // P
EPS = 1e-5
LN_AND_EXP = "natural_log_exp_and_others"

INNER = 256
NBLK = INNER // P
STATE = 16
RANK = 8
TAPS = 4
HALO = TAPS - 1


class Phase:

    def __init__(self, nc, name):
        self.nc, self.name, self.stack, self.sems = nc, name, ExitStack(), []

    def __enter__(self):
        return self

    def __exit__(self, *what):
        self.stack.close()
        if self.sems:
            self.nc.clear_and_free_semaphores(self.sems)
            self.nc.all_engine_barrier()

    def sb(self, name, shape, dt=F32):
        return self.stack.enter_context(self.nc.sbuf_tensor(f"{self.name}_{name}", shape, dt))

    def ps(self, name, shape, dt=F32):
        return self.stack.enter_context(self.nc.psum_tensor(f"{self.name}_{name}", shape, dt))

    def sem(self, name):
        self.sems.append(self.nc.alloc_semaphore(f"{self.name}_{name}"))
        return self.sems[-1]

    def block(self):
        return self.nc.Block()


def waited(eng, passed):
    eng.sem_inc(passed, 1)


def mamba_prep(nc, xT, delta, du, bc_split, x_dram, w, scratch):
    with Phase(nc, "prep") as ph:
        ones = ph.sb("ones_over_d", [P, P])
        w_in = ph.sb("w_in", [P, 2 * INNER])
        w_x = ph.sb("w_x", [P, NBLK, P])
        w_dt = ph.sb("w_dt", [P, NBLK * P])
        norm_w = ph.sb("norm_w", [P, 1])
        conv_w = ph.sb("conv_w", [P, NBLK, TAPS])
        conv_b = ph.sb("conv_b", [P, NBLK])
        dt_b = ph.sb("dt_b", [P, NBLK])
        eps = ph.sb("eps", [P, 1])
        xc = ph.sb("xc", [P, CH])
        sq = ph.sb("sq", [P, CH])
        lnv = ph.sb("lnv", [P, CH])
        rstd = ph.sb("rstd", [P, CH])
        msn = ph.sb("msn", [P, CH])
        msn2 = ph.sb("msn2", [P, CH])
        lnv2 = ph.sb("lnv2", [P, CH])
        rms = ph.sb("rms", [P, CH])
        xn = ph.sb("xn", [P, CH])
        hT = ph.sb("hT", [P, CH])
        xi = ph.sb("xi", [P, 2, NBLK, HALO + CH])
        cacc = ph.sb("cacc", [P, NBLK, CH])
        u = ph.sb("u", [P, 2, NBLK, CH])
        zs = ph.sb("zs", [P, 2, NBLK, CH])
        hi = ph.sb("hi", [P, CH], BF16)
        rest = ph.sb("rest", [P, CH])
        mid = ph.sb("mid", [P, CH], BF16)
        crow = ph.sb("crow", [32, 2, CH])
        dtb = ph.sb("dtb", [P, CH])
        absd = ph.sb("absd", [P, NBLK, CH])
        expd = ph.sb("expd", [P, NBLK, CH])
        lnd = ph.sb("lnd", [P, NBLK, CH])
        maxd = ph.sb("maxd", [P, NBLK, CH])

        p_mean = ph.ps("p_mean", [P, CH])
        p_var = ph.ps("p_var", [P, CH])
        p_in = ph.ps("p_in", [P, 2 * NBLK, CH])
        p_x = p_mean
        p_dt = ph.ps("p_dt", [P, NBLK, CH])

        s_w = ph.sem("weights_loaded")
        s_x = [ph.sem(f"x_loaded{i}") for i in range(NCH)]
        s_zero = ph.sem("zeroed")
        s_mean = ph.sem("mean_ready")
        s_xc = ph.sem("centred")
        s_sq = ph.sem("squared")
        s_var = ph.sem("var_ready")
        s_lnv = ph.sem("log_var")
        s_rstd = ph.sem("rstd_ready")
        s_msn = ph.sem("mean_square")
        s_rms = ph.sem("rms_ready")
        s_xn = ph.sem("normed")
        s_h = ph.sem("h_ready")
        s_in = ph.sem("in_proj_done")
        s_xi = ph.sem("xi_copied")
        s_halo = ph.sem("halo_ready")
        s_cstep = ph.sem("conv_step")
        s_u = ph.sem("u_ready")
        s_zs = ph.sem("z_silu_ready")
        s_xp = ph.sem("x_proj_done")
        s_crow = ph.sem("crow_ready")
        s_split = ph.sem("split_step")
        s_dtb = ph.sem("dt_rows_ready")
        s_dt = ph.sem("dt_proj_done")
        s_abs = ph.sem("abs_done")
        s_exp = ph.sem("exp_done")
        s_ln = ph.sem("log_done")
        s_maxd = ph.sem("max_done")
        s_delta = ph.sem("delta_ready")
        s_du = ph.sem("du_ready")
        s_res = ph.sem("residual_added")
        s_st = [ph.sem(f"stored{i}") for i in range(2)]

        with ph.block() as block:

            @block.sync
            def _(sp):
                for dst, src in ((ones, w["ones_over_d"]), (w_in, w["in_proj"]), (norm_w, w["norm_w"]),
                                 (w_x, w["x_proj"]), (w_dt, w["dt_proj"]), (conv_w, w["conv_w"]),
                                 (conv_b, w["conv_b"]), (dt_b, w["dt_b"])):
                    sp.dma_start(dst[:], src).then_inc(s_w, 16)
                for g in range(NCH):
                    sp.dma_start(xT[:, g * CH:(g + 1) * CH], x_dram[:, g * CH:(g + 1) * CH]).then_inc(s_x[g], 16)
                for g in range(NCH):
                    b, half = g // CPB, g % CPB
                    sp.wait_ge(s_u, g + 1)
                    sp.dma_start(scratch["u"][b, :, :, half * CH:(half + 1) * CH], u[:, g % 2]).then_inc(s_st[g % 2], 16)
                    sp.wait_ge(s_zs, g + 1)
                    sp.dma_start(scratch["zs"][b, :, :, half * CH:(half + 1) * CH], zs[:, g % 2]).then_inc(s_st[g % 2], 16)
                    sp.wait_ge(s_crow, g + 1)
                    sp.dma_start(scratch["c"][b, :, half * CH:(half + 1) * CH], crow[16:32, g % 2]).then_inc(s_st[g % 2], 16)
                for i in range(2):
                    sp.wait_ge(s_st[i], 48 * (NCH // 2))

            @block.tensor
            def _(pe):
                pe.wait_ge(s_w, 16 * 8)
                pe.wait_ge(s_zero, 4)
                for g in range(NCH + 1):
                    if g < NCH:
                        pe.wait_ge(s_x[g], 16)
                        if g >= 2:
                            pe.wait_ge(s_split, 6 * (g - 1))
                            pe.wait_ge(s_crow, g - 1)
                        pe.matmul(p_mean[:], ones[:], xT[:, g * CH:(g + 1) * CH], start=True, stop=True).then_inc(s_mean, 1)
                        pe.wait_ge(s_sq, g + 1)
                        if g >= 1:
                            pe.wait_ge(s_msn, 2 * g)
                        pe.matmul(p_var[:], ones[:], sq[:], start=True, stop=True).then_inc(s_var, 1)
                    if g >= 1:
                        pe.wait_ge(s_u, g)
                        pe.wait_ge(s_xc, min(g + 1, NCH))
                        for k in range(NBLK):
                            mm = pe.matmul(p_x[:], w_x[:, k], u[:, (g - 1) % 2, k], start=(k == 0), stop=(k == NBLK - 1))
                        mm.then_inc(s_xp, 1)
                        pe.wait_ge(s_dtb, g)
                        if g >= 2:
                            pe.wait_ge(s_abs, g - 1)
                            pe.wait_ge(s_maxd, g - 1)
                        for k in range(NBLK):
                            mm = pe.matmul(p_dt[:, k], w_dt[:, k * P:(k + 1) * P], dtb[:], start=True, stop=True)
                        mm.then_inc(s_dt, 1)
                    if g < NCH:
                        pe.wait_ge(s_h, g + 1)
                        if g >= 1:
                            pe.wait_ge(s_xi, g)
                            pe.wait_ge(s_zs, g)
                        for m in range(2 * NBLK):
                            mm = pe.matmul(p_in[:, m], w_in[:, m * P:(m + 1) * P], hT[:], start=True, stop=True)
                        mm.then_inc(s_in, 1)

            @block.scalar
            def _(act):
                act.preload_act_table_set(LN_AND_EXP)
                act.wait_ge(s_w, 16 * 8)
                act.wait_ge(s_zero, 4)
                for g in range(NCH + 1):
                    q = g - 1
                    if g < NCH:
                        act.wait_ge(s_xc, g + 1)
                        act.activation(sq[:], xc[:], ACT.Square).then_inc(s_sq, 1)
                        act.wait_ge(s_var, g + 1)
                        act.activation(lnv[:], p_var[:], ACT.Ln, bias=eps[:]).then_inc(s_lnv, 1)
                        act.wait_ge(s_lnv, g + 1)
                        if g >= 1:
                            act.wait_ge(s_msn, 2 * g)
                        act.activation(rstd[:], lnv[:], ACT.Exp, scale=-0.5).then_inc(s_rstd, 1)
                    if g >= 1:
                        if q >= 2:
                            act.wait_ge(s_st[q % 2], 48 * (q // 2))
                        act.activation(zs[:, q % 2], p_in[:, NBLK:], ACT.Silu).then_inc(s_zs, 1)
                        act.wait_ge(s_cstep, 8 * q + 8)
                        if q >= 2:
                            act.wait_ge(s_du, q - 1)
                        act.activation(u[:, q % 2], cacc[:], ACT.Silu).then_inc(s_u, 1)
                    if g < NCH:
                        act.preload_act_table_set(LN_AND_EXP)
                        act.wait_ge(s_msn, 2 * g + 2)
                        act.activation(lnv2[:], msn2[:], ACT.Ln, bias=eps[:]).then_inc(s_rms, 1)
                        act.wait_ge(s_rms, 2 * g + 1)
                        if g >= 1:
                            act.wait_ge(s_h, g)
                        act.activation(rms[:], lnv2[:], ACT.Exp, scale=-0.5).then_inc(s_rms, 1)
                    if g >= 1:
                        act.wait_ge(s_xp, q + 1)
                        if q >= 1:
                            act.wait_ge(s_dt, q)
                        act.activation(dtb[96:96 + RANK], p_x[96:96 + RANK], ACT.Copy).then_inc(s_dtb, 1)
                        act.activation(crow[:, q % 2], p_x[0:32], ACT.Copy).then_inc(s_crow, 1)
                        act.wait_ge(s_dt, q + 1)
                        for k in range(NBLK):
                            ins = act.activation(absd[:, k], p_dt[:, k], ACT.Abs, bias=dt_b[:, k:k + 1])
                        ins.then_inc(s_abs, 1)
                        act.wait_ge(s_abs, q + 1)
                        act.activation(expd[:], absd[:], ACT.Exp, scale=-1.0).then_inc(s_exp, 1)
                        act.wait_ge(s_exp, q + 1)
                        if q >= 1:
                            act.wait_ge(s_delta, q)
                        act.activation(lnd[:], expd[:], ACT.Ln, bias=1.0).then_inc(s_ln, 1)
                    if g < NCH:
                        act.wait_ge(s_in, g + 1)
                        act.wait_ge(s_halo, g + 1)
                        if g >= 2:
                            act.wait_ge(s_cstep, 8 * (g - 1))
                        act.activation(xi[:, g % 2, :, HALO:], p_in[:, 0:NBLK], ACT.Copy).then_inc(s_xi, 1)

            @block.vector
            def _(dve):
                dve.memset(dtb[:], 0.0).then_inc(s_zero, 1)
                dve.memset(bc_split[:].bitcast(mybir.dt.uint32), 0).then_inc(s_zero, 1)
                dve.memset(xi[:], 0.0).then_inc(s_zero, 1)
                dve.memset(eps[:], EPS).then_inc(s_zero, 1)
                dve.wait_ge(s_w, 16 * 8)
                dve.wait_ge(s_zero, 4)
                for g in range(NCH + 1):
                    q = g - 1
                    if g < NCH:
                        dve.wait_ge(s_mean, g + 1)
                        if g >= 1:
                            dve.wait_ge(s_xn, g)
                        dve.tensor_tensor(xc[:], xT[:, g * CH:(g + 1) * CH], p_mean[:], ALU.subtract).then_inc(s_xc, 1)
                        if g >= 2:
                            dve.wait_ge(s_cstep, 8 * (g - 1))
                        if g % CPB == 0:
                            dve.memset(xi[:, g % 2, :, 0:HALO], 0.0).then_inc(s_halo, 1)
                        else:
                            dve.wait_ge(s_xi, g)
                            dve.tensor_copy(xi[:, g % 2, :, 0:HALO], xi[:, (g + 1) % 2, :, CH:CH + HALO]).then_inc(s_halo, 1)
                    if g >= 1:
                        dve.wait_ge(s_xi, q + 1)
                        dve.wait_ge(s_halo, q + 1)
                        if q >= 1:
                            dve.wait_ge(s_u, q)
                        for k in range(NBLK):
                            dve.tensor_scalar(cacc[:, k], xi[:, q % 2, k, HALO:], conv_w[:, k, HALO:TAPS],
                                              conv_b[:, k:k + 1], ALU.mult, ALU.add).then_inc(s_cstep, 1)
                        for j in range(HALO):
                            for k in range(NBLK):
                                dve.wait_ge(s_cstep, 8 * q + 2 * j + k + 1)
                                dve.scalar_tensor_tensor(cacc[:, k], xi[:, q % 2, k, j:j + CH], conv_w[:, k, j:j + 1],
                                                         cacc[:, k], ALU.mult, ALU.add).then_inc(s_cstep, 1)
                    if g < NCH:
                        dve.wait_ge(s_rstd, g + 1)
                        if g >= 1:
                            dve.wait_ge(s_res, g)
                        dve.tensor_tensor(xn[:], xc[:], rstd[:], ALU.mult).then_inc(s_xn, 1)
                        dve.wait_ge(s_var, g + 1)
                        dve.tensor_tensor(msn[:], rstd[:], p_var[:], ALU.mult).then_inc(s_msn, 1)
                        dve.wait_ge(s_msn, 2 * g + 1)
                        dve.tensor_tensor(msn2[:], msn[:], rstd[:], ALU.mult).then_inc(s_msn, 1)
                    if g >= 1:
                        tok = slice(q * CH, (q + 1) * CH)
                        dve.wait_ge(s_crow, q + 1)
                        dve.tensor_copy(hi[0:96], p_x[0:96]).then_inc(s_split, 1)
                        dve.wait_ge(s_split, 6 * q + 1)
                        dve.tensor_tensor(rest[0:96], p_x[0:96], hi[0:96], ALU.subtract).then_inc(s_split, 1)
                        dve.tensor_copy(bc_split[0:32, tok], hi[0:32]).then_inc(s_split, 1)
                        dve.wait_ge(s_split, 6 * q + 2)
                        dve.tensor_copy(mid[0:96], rest[0:96]).then_inc(s_split, 1)
                        dve.wait_ge(s_split, 6 * q + 4)
                        dve.tensor_copy(bc_split[32:64, tok], mid[32:64]).then_inc(s_split, 1)
                        dve.tensor_tensor(bc_split[64:96, tok], rest[64:96], mid[64:96], ALU.subtract).then_inc(s_split, 1)
                    if g < NCH:
                        dve.wait_ge(s_rms, 2 * g + 2)
                        dve.wait_ge(s_xn, g + 1)
                        if g >= 1:
                            dve.wait_ge(s_in, g)
                        dve.scalar_tensor_tensor(hT[:], xn[:], norm_w[:], rms[:], ALU.mult, ALU.mult).then_inc(s_h, 1)
                    if g >= 1:
                        b, half = q // CPB, q % CPB
                        dve.wait_ge(s_abs, q + 1)
                        for k in range(NBLK):
                            ins = dve.tensor_scalar(maxd[:, k], p_dt[:, k], dt_b[:, k:k + 1], 0.0, ALU.add, ALU.max)
                        ins.then_inc(s_maxd, 1)
                        dve.wait_ge(s_ln, q + 1)
                        dve.wait_ge(s_maxd, q + 1)
                        dve.tensor_tensor(delta[:, b, :, half * CH:(half + 1) * CH], maxd[:], lnd[:], ALU.add).then_inc(s_delta, 1)

            @block.gpsimd
            def _(pool):
                for g in range(NCH + 1):
                    if g < NCH:
                        tok = slice(g * CH, (g + 1) * CH)
                        pool.wait_ge(s_xn, g + 1)
                        pool.wait_ge(s_xc, g + 1)
                        pool.tensor_tensor(xT[:, tok], xT[:, tok], xn[:], ALU.add).then_inc(s_res, 1)
                    if g >= 1:
                        q = g - 1
                        b, seg = q // CPB, slice(q % CPB * CH, (q % CPB + 1) * CH)
                        pool.wait_ge(s_delta, q + 1)
                        pool.wait_ge(s_u, q + 1)
                        pool.tensor_tensor(du[:, b, :, seg], delta[:, b, :, seg], u[:, q % 2], ALU.mult).then_inc(s_du, 1)


def mamba_scan(nc, xT, delta, du, bc_split, w, scratch):
    NIT = NBLK * STATE
    SLOTS = 3
    LAG = 3
    OUT = SLOTS - 1
    with Phase(nc, "scan") as ph:
        ident = ph.sb("ident", [P, P])
        sel = ph.sb("sel", [P, STATE, P], BF16)
        a_log = ph.sb("a_log", [P, NBLK, STATE])
        a_exp = ph.sb("a_exp", [P, NBLK, STATE])
        a_neg = ph.sb("a_neg", [P, NBLK, STATE])
        d_skip = ph.sb("d_skip", [P, NBLK])
        w_out = ph.sb("w_out", [P, NBLK, D])
        c_bc = ph.sb("c_bc", [P, STATE, SEQ])
        decay = ph.sb("decay", [P, 2, SEQ])
        h = ph.sb("h", [P, SLOTS, SEQ])
        hc = ph.sb("hc", [P, LAG, SEQ])
        u = ph.sb("u", [P, NBLK, SEQ])
        zs = ph.sb("zs", [P, NBLK, SEQ])
        y1 = u
        p_b = ph.ps("p_b", [P, SLOTS, SEQ])
        p_y = ph.ps("p_y", [P, SEQ])

        s_w = ph.sem("weights_loaded")
        s_a = ph.sem("a_ready")
        s_c = [ph.sem(f"c_loaded{i}") for i in range(STATE)]
        s_uz = ph.sem("u_zs_loaded")
        s_b = ph.sem("b_broadcast")
        s_dec = ph.sem("decay_ready")
        s_dbu = ph.sem("dbu_ready")
        s_scan = ph.sem("scan_done")
        s_hc = ph.sem("hc_ready")
        s_acc = ph.sem("hc_summed")
        s_y1 = ph.sem("y_read")
        s_y = ph.sem("y_gated")
        s_o = ph.sem("out_proj_done")
        s_x = ph.sem("residual_added")
        hold = ph.sem("wait_passed")

        with ph.block() as block:

            @block.sync
            def _(sp):
                for dst, src in ((ident, w["ident"]), (sel, w["sel"]), (a_log, w["a_log"]),
                                 (d_skip, w["d_skip"]), (w_out, w["out_proj"])):
                    sp.dma_start(dst[:], src).then_inc(s_w, 16)
                for b in range(BATCH):
                    if b:
                        sp.wait_ge(s_o, b)
                    sp.dma_start(u[:], scratch["u"][b]).then_inc(s_uz, 16)
                    sp.dma_start(zs[:], scratch["zs"][b]).then_inc(s_uz, 16)
                    for s in range(STATE):
                        if b:
                            sp.wait_ge(s_hc, (b - 1) * NIT + STATE + s + 1)
                        sp.dma_start(c_bc[:, s], scratch["c"][b, s:s + 1, :].to_broadcast([P, SEQ])).then_inc(s_c[s], 16)

            def later(b):
                return not isinstance(b, int)

            def accumulate(pe, b, i):
                blk, s = i // STATE, i % STATE
                if s == 0 and (i or later(b)):
                    pe.wait_ge(s_y1, NBLK * b + blk)
                pe.wait_ge(s_hc, b * NIT + i + 1)
                for c in range(CPB):
                    mm = pe.matmul(p_y[:, c * CH:(c + 1) * CH], ident[:], hc[:, i % LAG, c * CH:(c + 1) * CH],
                                   start=(s == 0), stop=(s == STATE - 1))
                mm.then_inc(s_acc, 1)

            @block.tensor
            def _(pe):
                def sequence(b):
                    for i in range(NIT):
                        s = i % STATE
                        if i >= SLOTS:
                            pe.wait_ge(s_scan, b * NIT + i - SLOTS + 1)
                        elif later(b) and i == OUT:
                            pe.wait_ge(s_x, b)
                        elif later(b):
                            pe.wait_ge(s_scan, b * NIT)
                        for c in range(CPB):
                            mm = pe.matmul(p_b[:, i % SLOTS, c * CH:(c + 1) * CH], sel[:, s],
                                           bc_split[:, bass.ds(b * SEQ + c * CH, CH)], start=True, stop=True)
                        mm.then_inc(s_b, 1)
                        if i >= SLOTS:
                            accumulate(pe, b, i - SLOTS)
                    for i in range(NIT - SLOTS, NIT):
                        accumulate(pe, b, i)
                    for k in range(NBLK):
                        pe.wait_ge(s_y, b * NBLK + k + 1)
                        for c in range(CPB):
                            mm = pe.matmul(p_b[:, OUT, c * CH:(c + 1) * CH], w_out[:, k], y1[:, k, c * CH:(c + 1) * CH],
                                           start=(k == 0), stop=(k == NBLK - 1))
                    mm.then_inc(s_o, 1)

                pe.wait_ge(s_w, 16 * 5)
                sequence(0)
                with pe.Fori(1, BATCH) as b:
                    sequence(b)

            @block.scalar
            def _(act):
                def sequence(b):
                    for i in range(NIT):
                        blk, s = i // STATE, i % STATE
                        if i >= 2 or later(b):
                            act.wait_ge(s_scan, b * NIT + max(i - 1, 0))
                        if later(b):
                            waited(act, hold)
                        act.activation(decay[:, i % 2], delta[:, bass.ds(b, 1), blk, :].rearrange("p o t -> p (o t)"), ACT.Exp,
                                       scale=a_neg[:, blk, s:s + 1]).then_inc(s_dec, 1)

                act.wait_ge(s_w, 16 * 5)
                act.activation(a_exp[:], a_log[:], ACT.Exp).then_inc(s_a, 1)
                act.wait_ge(s_a, 1)
                act.mul(a_neg[:], a_exp[:], -1.0).then_inc(s_a, 1)
                act.wait_ge(s_a, 2)
                sequence(0)
                with act.Fori(1, BATCH) as b:
                    sequence(b)

            @block.vector
            def _(dve):
                def gate(b, blk):
                    dve.wait_ge(s_acc, b * NIT + (blk + 1) * STATE)
                    dve.wait_ge(s_uz, (b + 1) * 32)
                    dve.scalar_tensor_tensor(y1[:, blk], u[:, blk], d_skip[:, blk:blk + 1], p_y[:], ALU.mult, ALU.add).then_inc(s_y1, 1)
                    dve.wait_ge(s_y1, b * NBLK + blk + 1)
                    dve.tensor_tensor(y1[:, blk], y1[:, blk], zs[:, blk], ALU.mult).then_inc(s_y, 1)

                def times_b(b, i):
                    dve.wait_ge(s_b, b * NIT + i + 1)
                    dve.tensor_tensor(p_b[:, i % SLOTS], du[:, bass.ds(b, 1), i // STATE, :].rearrange("p o t -> p (o t)"),
                                      p_b[:, i % SLOTS], ALU.mult).then_inc(s_dbu, 1)

                def sequence(b):
                    times_b(b, 0)
                    for i in range(NIT):
                        if i + 1 < NIT:
                            times_b(b, i + 1)
                        dve.wait_ge(s_dec, b * NIT + i + 1)
                        dve.wait_ge(s_dbu, b * NIT + i + 1)
                        if i >= SLOTS or later(b):
                            dve.wait_ge(s_hc, b * NIT + max(i - SLOTS + 1, 0))
                        dve.tensor_tensor_scan(h[:, i % SLOTS], decay[:, i % 2], p_b[:, i % SLOTS], 0.0,
                                               ALU.mult, ALU.add).then_inc(s_scan, 1)
                        if i == STATE + SLOTS - 1:
                            gate(b, 0)
                    gate(b, 1)
                    dve.wait_ge(s_o, b + 1)
                    xt = xT[:, bass.ds(b * SEQ, SEQ)]
                    dve.tensor_tensor(xt, xt, p_b[:, OUT], ALU.add).then_inc(s_x, 1)

                dve.wait_ge(s_w, 16 * 5)
                sequence(0)
                with dve.Fori(1, BATCH) as b:
                    sequence(b)

            @block.gpsimd
            def _(pool):
                def sequence(b):
                    for i in range(NIT):
                        s = i % STATE
                        pool.wait_ge(s_scan, b * NIT + i + 1)
                        pool.wait_ge(s_c[s], b * 16 + 16)
                        if i >= LAG or later(b):
                            pool.wait_ge(s_acc, b * NIT + max(i - LAG + 1, 0))
                        pool.tensor_tensor(hc[:, i % LAG], h[:, i % SLOTS], c_bc[:, s], ALU.mult).then_inc(s_hc, 1)

                sequence(0)
                with pool.Fori(1, BATCH) as b:
                    sequence(b)


EXP0, HID0, SHARED = 16, 256, 2
SLOTS0 = EXP0 + SHARED
TOPK = 2
CAP = -(-TOK * TOPK * 5 // (EXP0 * 4))
NSLOT = EXP0 * CAP
ZROWS = 8
FILL = -3.4028234663852886e38


def layer_norm(nc, xT, lnT, w, name):
    with Phase(nc, name) as ph:
        ones = ph.sb("ones_over_d", [P, P])
        eps = ph.sb("eps", [P, 1])
        sq = ph.sb("sq", [P, 2, CH])
        lnv = ph.sb("lnv", [P, NCH, CH])
        rstd = ph.sb("rstd", [P, NCH, CH])
        p_mean = ph.ps("p_mean", [P, 2, CH])
        p_var = ph.ps("p_var", [P, 2, CH])
        s_w = ph.sem("ones_loaded")
        s_eps = ph.sem("eps_set")
        s_mean = ph.sem("mean_ready")
        s_xc = ph.sem("centred")
        s_sq = ph.sem("squared")
        s_var = ph.sem("var_ready")
        s_lnv = ph.sem("log_var")
        s_rstd = ph.sem("rstd_ready")
        s_xn = ph.sem("normed")

        with ph.block() as block:
            @block.sync
            def _(sp):
                sp.dma_start(ones[:], w["ones_over_d"]).then_inc(s_w, 16)

            @block.tensor
            def _(pe):
                pe.wait_ge(s_w, 16)
                for g in range(NCH + 1):
                    if g < NCH:
                        if g >= 2:
                            pe.wait_ge(s_xc, g - 1)
                        pe.matmul(p_mean[:, g % 2], ones[:], xT[:, g * CH:(g + 1) * CH], start=True, stop=True).then_inc(s_mean, 1)
                    if g:
                        pe.wait_ge(s_sq, g)
                        if g >= 3:
                            pe.wait_ge(s_lnv, g - 2)
                        pe.matmul(p_var[:, (g - 1) % 2], ones[:], sq[:, (g - 1) % 2], start=True, stop=True).then_inc(s_var, 1)

            @block.scalar
            def _(act):
                act.wait_ge(s_eps, 1)
                for g in range(NCH + 1):
                    if g < NCH:
                        act.wait_ge(s_xc, g + 1)
                        if g >= 2:
                            act.wait_ge(s_var, g - 1)
                        act.activation(sq[:, g % 2], lnT[:, g * CH:(g + 1) * CH], ACT.Square).then_inc(s_sq, 1)
                    if g:
                        act.wait_ge(s_var, g)
                        act.activation(lnv[:, g - 1], p_var[:, (g - 1) % 2], ACT.Ln, bias=eps[:]).then_inc(s_lnv, 1)
                for g in range(NCH):
                    act.wait_ge(s_lnv, g + 1)
                    act.activation(rstd[:, g], lnv[:, g], ACT.Exp, scale=-0.5).then_inc(s_rstd, 1)

            @block.vector
            def _(dve):
                dve.memset(eps[:], EPS).then_inc(s_eps, 1)
                for g in range(NCH):
                    tok = slice(g * CH, (g + 1) * CH)
                    dve.wait_ge(s_mean, g + 1)
                    dve.tensor_tensor(lnT[:, tok], xT[:, tok], p_mean[:, g % 2], ALU.subtract).then_inc(s_xc, 1)
                for g in range(NCH):
                    tok = slice(g * CH, (g + 1) * CH)
                    dve.wait_ge(s_rstd, g + 1)
                    dve.wait_ge(s_sq, g + 1)
                    dve.tensor_tensor(lnT[:, tok], lnT[:, tok], rstd[:, g], ALU.mult).then_inc(s_xn, 1)


def router0(nc, lnT, rows, weight, put, get, w, scratch):
    E, T = EXP0, NT
    U32 = mybir.dt.uint32
    with Phase(nc, "router") as ph:
        gate_w = ph.sb("gate_w", [P, E])
        gate_b = ph.sb("gate_b", [P, E])
        prio = ph.sb("prio", [P, E])
        before = ph.sb("before", [P, P], BF16)
        ones = ph.sb("ones", [P, P], BF16)
        again = ph.sb("again", [P, E, T])
        score = ph.sb("score", [P, T, E])
        tmp = ph.sb("tmp", [P, T, E])
        best = ph.sb("best", [P, T])
        norm = ph.sb("norm", [P, T])
        oh = ph.sb("oh", [P, 2, T, E])
        logit = ph.sb("logit", [P, T, E])
        asg = ph.sb("asg", [P, E, T])
        wk = ph.sb("wk", [P, E, T])
        bits = ph.sb("bits", [P, E], U32)
        cand = ph.sb("cand", [P, E], U32)
        flip = ph.sb("flip", [P, E], U32)
        add = ph.sb("add", [P, E], U32)
        cnt = ph.sb("cnt", [P, E])
        need = ph.sb("need", [P, E])
        ge = ph.sb("ge", [P, E, T], BF16)
        gt = ph.sb("gt", [P, E, T], BF16)
        eq = ph.sb("eq", [P, E, T], BF16)
        tot = ph.sb("tot", [P, E, T])
        cum = ph.sb("cum", [P, E, T])
        pre = ph.sb("pre", [P, E, T])
        keep = ph.sb("keep", [P, E, T])
        base = ph.sb("base", [P, E])
        spare = ph.sb("spare", [P, TOPK, T])
        zeros = ph.sb("zeros", [P, ZROWS, D])
        keepb = ph.sb("keepb", [P, E, T], BF16)
        mine = ph.sb("mine", [P, E, T])
        kept = ph.sb("kept", [P, T])
        slot = ph.sb("slot", [P, T])
        off = ph.sb("off", [P, T])
        p_x = ph.ps("p_x", [P, 2, CH // P, D])
        ident = ph.sb("ident", [P, P])
        p_lg = ph.ps("p_lg", [P, T, E])
        p_cnt = ph.ps("p_cnt", [P, E, T])
        p_pre = ph.ps("p_pre", [P, E, T])
        s_w = ph.sem("weights_loaded")
        s_lg = ph.sem("logits_ready")
        s_v = ph.sem("vector_step")
        s_mask = ph.sem("mask_ready")
        s_cnt = ph.sem("count_ready")
        s_exp = ph.sem("exp_done")
        s_zero = ph.sem("zeros_set")
        s_fill = ph.sem("slots_zeroed")
        s_turn = ph.sem("tokens_turned")
        s_row = ph.sem("rows_copied")

        with ph.block() as block:
            @block.sync
            def _(sp):
                for dst, src in ((gate_w, w["gate_w"]), (gate_b, w["gate_b"]), (prio, w["prio"]),
                                 (before, w["before"]), (ones, w["ones_bf16"]), (again, w["again"]),
                                 (base, w["slot_base"]), (spare, w["spare"]), (ident, w["ident"])):
                    sp.dma_start(dst[:], src).then_inc(s_w, 16)
                sp.wait_ge(s_zero, 1)
                for n in range(NSLOT // (P * ZROWS)):
                    sp.dma_start(scratch["slots"][n * P * ZROWS:(n + 1) * P * ZROWS].rearrange("(p r) d -> p r d", r=ZROWS),
                                 zeros[:]).then_inc(s_fill, 16)
                sp.dma_start(scratch["y"][NSLOT:NSLOT + 1], zeros[0:1, 0]).then_inc(s_fill, 16)
                sp.wait_ge(s_fill, 16 * (NSLOT // (P * ZROWS) + 1))

            @block.tensor
            def _(pe):
                pe.wait_ge(s_w, 16 * 9)
                for t in range(T):
                    mm = pe.matmul(p_lg[:, t], lnT[:, t * P:(t + 1) * P], gate_w[:], start=True, stop=True)
                mm.then_inc(s_lg, 1)
                for c in range(NCH):
                    if c >= 2:
                        pe.wait_ge(s_row, c - 1)
                    for t in range(CH // P):
                        mm = pe.transpose(p_x[:, c % 2, t], lnT[:, c * CH + t * P:c * CH + (t + 1) * P], ident[:])
                    mm.then_inc(s_turn, 1)
                with pe.Fori(0, 32) as n:
                    pe.wait_ge(s_mask, n + 1)
                    pe.matmul(p_cnt[:], ones[:], ge[:], start=True, stop=True).then_inc(s_cnt, 1)
                pe.wait_ge(s_mask, 33)
                pe.matmul(p_cnt[:], ones[:], gt[:], start=True, stop=True).then_inc(s_cnt, 1)
                pe.wait_ge(s_mask, 34)
                pe.matmul(p_pre[:], before[:], eq[:], start=True, stop=True)
                pe.matmul(p_cnt[:], ones[:], eq[:], start=True, stop=True).then_inc(s_cnt, 1)
                pe.wait_ge(s_mask, 35)
                pe.matmul(p_pre[:], before[:], keepb[:], start=True, stop=True)
                pe.matmul(p_cnt[:], ones[:], keepb[:], start=True, stop=True).then_inc(s_cnt, 1)

            @block.scalar
            def _(act):
                act.wait_ge(s_v, 3)
                act.activation(tmp[:], score[:], ACT.Exp).then_inc(s_exp, 1)
                for c in range(NCH):
                    act.wait_ge(s_turn, c + 1)
                    act.activation(rows[:, c * (CH // P):(c + 1) * (CH // P)], p_x[:, c % 2], ACT.Copy).then_inc(s_row, 1)

            @block.vector
            def _(dve):
                count = [0]

                def step(ins):
                    count[0] += 1
                    ins.then_inc(s_v, 1)
                    dve.wait_ge(s_v, count[0])

                dve.wait_ge(s_w, 16 * 9)
                dve.memset(zeros[:], 0.0).then_inc(s_zero, 1)
                dve.wait_ge(s_lg, 1)
                step(dve.tensor_copy(logit[:], p_lg[:]))
                step(dve.tensor_reduce(best[:], logit[:], AX.X, ALU.max))
                over = best[:].rearrange("p (t o) -> p t o", o=1).to_broadcast([P, T, E])
                step(dve.tensor_tensor(score[:], logit[:], over, ALU.subtract))
                dve.wait_ge(s_exp, 1)
                step(dve.tensor_reduce(norm[:], tmp[:], AX.X, ALU.add))
                step(dve.reciprocal(norm[:], norm[:]))
                step(dve.tensor_tensor(score[:], tmp[:], norm[:].rearrange("p (t o) -> p t o", o=1).to_broadcast([P, T, E]), ALU.mult))
                bias = gate_b[:].rearrange("p (o e) -> p o e", o=1).to_broadcast([P, T, E])
                order = prio[:].rearrange("p (o e) -> p o e", o=1).to_broadcast([P, T, E])
                step(dve.tensor_tensor(score[:], score[:], bias, ALU.add))
                for k in range(TOPK):
                    step(dve.tensor_reduce(best[:], score[:], AX.X, ALU.max))
                    step(dve.tensor_tensor(tmp[:], score[:], over, ALU.is_ge))
                    step(dve.tensor_tensor(tmp[:], tmp[:], order, ALU.mult))
                    step(dve.tensor_reduce(best[:], tmp[:], AX.X, ALU.max))
                    step(dve.tensor_tensor(oh[:, k], over, order, ALU.is_equal))
                    if k == 0:
                        step(dve.scalar_tensor_tensor(score[:], oh[:, k], FILL, score[:], ALU.mult, ALU.add))
                by_expert = lambda a: a.rearrange("p t e -> p e t")
                step(dve.tensor_tensor(asg[:], by_expert(oh[:, 0]), by_expert(oh[:, 1]), ALU.add))
                step(dve.tensor_scalar(wk[:], asg[:], -1.0, -FILL, ALU.add, ALU.mult))
                step(dve.tensor_tensor(tot[:], asg[:], by_expert(logit[:]), ALU.mult))
                step(dve.tensor_tensor(wk[:], wk[:], tot[:], ALU.add))
                thr = cand[:].bitcast(F32).rearrange("p (e o) -> p e o", o=1).to_broadcast([P, E, T])

                def over_tokens(dst, value):
                    dve.wait_ge(s_cnt, value)
                    step(dve.tensor_reduce(dst, p_cnt[:], AX.X, ALU.add))

                step(dve.memset(cand[:], 0))
                dve.tensor_tensor(ge[:], wk[:], thr, ALU.is_ge).then_inc(s_mask, 1)
                over_tokens(cnt[:], 1)
                step(dve.tensor_scalar(bits[:], cnt[:], CAP - 0.5, float(2 ** 31), ALU.is_ge, ALU.mult))
                step(dve.tensor_scalar(flip[:], bits[:], 31, 31, ALU.logical_shift_right, ALU.logical_shift_left))
                step(dve.tensor_scalar(flip[:].bitcast(mybir.dt.int32), bits[:].bitcast(mybir.dt.int32), 31, None, ALU.arith_shift_right))
                step(dve.tensor_scalar(flip[:], flip[:], 0xFFFFFFFF, 0x80000000, ALU.bitwise_xor, ALU.bitwise_or))
                for n in range(1, 32):
                    bit = 1 << (31 - n)
                    step(dve.scalar_tensor_tensor(cand[:], bits[:], bit, flip[:], ALU.bitwise_or, ALU.bitwise_xor))
                    dve.tensor_tensor(ge[:], wk[:], thr, ALU.is_ge).then_inc(s_mask, 1)
                    over_tokens(cnt[:], n + 1)
                    step(dve.tensor_scalar(add[:], cnt[:], CAP - 0.5, float(bit), ALU.is_ge, ALU.mult))
                    step(dve.tensor_tensor(bits[:], bits[:], add[:], ALU.bitwise_or))
                step(dve.tensor_tensor(cand[:], bits[:], flip[:], ALU.bitwise_xor))
                dve.tensor_tensor(gt[:], wk[:], thr, ALU.is_gt).then_inc(s_mask, 1)
                step(dve.tensor_tensor(pre[:], wk[:], thr, ALU.is_equal))
                over_tokens(cnt[:], 33)
                dve.tensor_tensor(eq[:], pre[:], asg[:], ALU.mult).then_inc(s_mask, 1)
                step(dve.tensor_scalar(need[:], cnt[:], -1.0, float(CAP), ALU.mult, ALU.add))
                def earlier():
                    step(dve.tensor_copy(tot[:], p_cnt[:]))
                    step(dve.tensor_tensor_scan(cum[:].rearrange("p e t -> p (e t)"), again[:].rearrange("p e t -> p (e t)"),
                                                tot[:].rearrange("p e t -> p (e t)"), 0.0, ALU.mult, ALU.add))
                    step(dve.tensor_tensor(cum[:], cum[:], tot[:], ALU.subtract))
                    step(dve.tensor_tensor(pre[:], cum[:], p_pre[:], ALU.add))

                over_e = lambda a: a.rearrange("p (e o) -> p e o", o=1).to_broadcast([P, E, T])
                dve.wait_ge(s_cnt, 34)
                earlier()
                step(dve.tensor_tensor(keep[:], pre[:], over_e(need[:]), ALU.is_lt))
                step(dve.tensor_tensor(keep[:], keep[:], eq[:], ALU.mult))
                step(dve.tensor_tensor(keep[:], keep[:], gt[:], ALU.add))
                dve.tensor_copy(keepb[:], keep[:]).then_inc(s_mask, 1)
                dve.wait_ge(s_cnt, 35)
                earlier()
                step(dve.tensor_tensor(pre[:], pre[:], over_e(base[:]), ALU.add))
                for k in range(TOPK):
                    step(dve.tensor_tensor(mine[:], by_expert(oh[:, k]), keep[:], ALU.mult))
                    step(dve.tensor_reduce(kept[:], by_expert(mine[:]), AX.X, ALU.add))
                    step(dve.tensor_tensor(tot[:], mine[:], pre[:], ALU.mult))
                    step(dve.tensor_reduce(slot[:], by_expert(tot[:]), AX.X, ALU.add))
                    step(dve.tensor_tensor(tot[:], mine[:], by_expert(logit[:]), ALU.mult))
                    step(dve.tensor_reduce(weight[:, k], by_expert(tot[:]), AX.X, ALU.add))
                    step(dve.tensor_scalar(off[:], kept[:], -float(NSLOT), float(NSLOT), ALU.mult, ALU.add))
                    step(dve.tensor_tensor(get[:, k], slot[:], off[:], ALU.add))
                    step(dve.tensor_scalar(kept[:], kept[:], -1.0, 1.0, ALU.mult, ALU.add))
                    step(dve.tensor_tensor(off[:], kept[:], spare[:, k], ALU.mult))
                    step(dve.tensor_tensor(put[:, k], slot[:], off[:], ALU.add))


def experts0(nc, xT, lnT, rows, weight, put, get, w, scratch):
    M = HID0 // P
    SM = SHARED * M
    TILES = (3, 2)
    FIRST = (0, 3)
    U = 2 * EXP0
    EARLY = 6
    with Phase(nc, "experts") as ph:
        ident = ph.sb("ident", [P, P])
        ws = ph.sb("ws", [P, SHARED, 3 * HID0])
        wts = ph.sb("wts", [P, 2, 3 * HID0])
        xr = ph.sb("xr", [P, 2, CAP // P, D])
        xs = ph.sb("xs", [P, 2, CH])
        gated = ph.sb("gated", [P, M, CH])
        g = ph.sb("g", [P, 2, M, CH])
        sg = ph.sb("sg", [P, 2, SM, CH])
        yr = ph.sb("yr", [P, 2, CH // P, D])
        mine = ph.sb("mine", [P, TOPK, NT, D])
        second = ph.sb("second", [P, NT, D])
        p_h = ph.ps("p_h", [P, M, 2, CH])
        p_y = ph.ps("p_y", [P, 2, CH // P, D])
        p_t = ph.ps("p_t", [P, 2, CH // P, D])
        s_id = ph.sem("consts_loaded")
        s_put = ph.sem("rows_scattered")
        s_xr = [ph.sem(f"slots_loaded{i}") for i in range(2)]
        s_w = [ph.sem(f"weights_loaded{i}") for i in range(2)]
        s_wd = [ph.sem(f"down_weights_loaded{i}") for i in range(2)]
        s_t = ph.sem("slots_turned")
        s_xs = ph.sem("turned_copied")
        s_up = ph.sem("up_done")
        s_silu = ph.sem("silu_done")
        s_g = ph.sem("gated_ready")
        s_y = ph.sem("down_done")
        s_yr = ph.sem("rows_copied")
        s_yst = [ph.sem(f"rows_stored{i}") for i in range(2)]
        s_sup = ph.sem("shared_up_done")
        s_ssilu = ph.sem("shared_silu_done")
        s_sg = ph.sem("shared_gated_ready")
        s_sy = ph.sem("shared_down_done")
        s_sx = ph.sem("shared_added")
        s_get = [ph.sem(f"rows_gathered{i}") for i in range(NCH)]
        s_sc = ph.sem("scaled")
        s_acc = ph.sem("weighted_sum")
        s_turn = ph.sem("sums_turned")
        s_x = ph.sem("residual_added")

        last = EXP0 // 2 - 1

        def started(i, units):
            return not isinstance(i, int) or i * 4 >= units

        with ph.block() as block:
            @block.sync
            def _(sp):
                sp.dma_start(ws[:], w["ew"][EXP0:SLOTS0].rearrange("s p n -> p s n")).then_inc(s_id, 16)
                sp.dma_start(ident[:], w["ident"]).then_inc(s_id, 16)

                def load_slots(e, s):
                    slots = scratch["slots"][0:NSLOT].rearrange("(e q p) d -> e p q d", p=P, e=EXP0)
                    sp.dma_start(xr[:, s], slots[bass.ds(e, 1)].rearrange("o p q d -> (o p) q d")).then_inc(s_xr[s], 16)

                def load_up(e, s):
                    sp.dma_start(wts[:, s, 0:2 * HID0], w["ew"][bass.ds(e, 1), :, 0:2 * HID0].rearrange("o p n -> (o p) n")).then_inc(s_w[s], 16)

                def load_down(e, s):
                    sp.dma_start(wts[:, s, 2 * HID0:], w["ew"][bass.ds(e, 1), :, 2 * HID0:].rearrange("o p n -> (o p) n")).then_inc(s_wd[s], 16)

                def store(e, c):
                    sp.wait_ge(s_yr, e * 2 + c + 1)
                    rows_of = scratch["y"][0:NSLOT].rearrange("(e q p) d -> e p q d", p=P, e=EXP0)
                    sp.dma_start(rows_of[bass.ds(e, 1), :, FIRST[c]:FIRST[c] + TILES[c]].rearrange("o p q d -> (o p) q d"),
                                 yr[:, c, 0:TILES[c]]).then_inc(s_yst[c], 16)

                for s in range(2):
                    load_up(s, s)
                    load_down(s, s)
                sp.wait_ge(s_put, 16 * TOPK * NT)
                load_slots(0, 0)
                load_slots(1, 1)
                with sp.Fori(0, EXP0 // 2 - 1) as i:
                    for s in range(2):
                        e = i * 2 + s
                        sp.wait_ge(s_t, e * 2 + 2)
                        load_slots(e + 2, s)
                        store(e, 0)
                        sp.wait_ge(s_up, e * (2 * M) + 2 * M)
                        load_up(e + 2, s)
                        sp.wait_ge(s_y, e * 2 + 2)
                        load_down(e + 2, s)
                        store(e, 1)
                for e in range(EXP0 - 2, EXP0):
                    store(e, 0)
                    store(e, 1)

            @block.tensor
            def _(pe):
                def shared_up(c):
                    for j in range(SM):
                        if c * SM + j >= 2:
                            pe.wait_ge(s_sg, c * SM + j - 1)
                        for n in range(2):
                            mm = pe.matmul(p_h[:, j % 2, n], ws[:, j // M, (n * M + j % M) * P:(n * M + j % M + 1) * P],
                                           lnT[:, c * CH:(c + 1) * CH], start=True, stop=True)
                        mm.then_inc(s_sup, 1)

                def shared_down(c):
                    pe.wait_ge(s_sg, (c + 1) * SM)
                    if c >= 2:
                        pe.wait_ge(s_sx, c - 1)
                    for j in range(SM):
                        mm = pe.matmul(p_y[:, c % 2].rearrange("p t d -> p (t d)"),
                                       ws[:, j // M, (2 * M + j % M) * P:(2 * M + j % M + 1) * P],
                                       sg[:, c % 2, j], start=(j == 0), stop=(j == SM - 1))
                    mm.then_inc(s_sy, 1)

                def turn(i, v):
                    s, c = v // 2, v % 2
                    if c == 0:
                        pe.wait_ge(s_xr[s], i * 16 + 16)
                    if started(i, 2 - v):
                        pe.wait_ge(s_xs, i * 4 + v - 1)
                    for q in range(TILES[c]):
                        mm = pe.transpose(p_t[:, c, q], xr[:, s, FIRST[c] + q], ident[:])
                    mm.then_inc(s_t, 1)

                def up(i, v):
                    s, c = v // 2, v % 2
                    if c == 0:
                        pe.wait_ge(s_w[s], i * 16 + 16)
                    pe.wait_ge(s_xs, i * 4 + v + 1)
                    for m in range(M):
                        if started(i, 1 - v):
                            pe.wait_ge(s_g, (i * 4 + v - 1) * M + m + 1)
                        for n in range(2):
                            mm = pe.matmul(p_h[:, m, n, 0:TILES[c] * P], wts[:, s, (n * M + m) * P:(n * M + m + 1) * P],
                                           xs[:, c, 0:TILES[c] * P], start=True, stop=True)
                        mm.then_inc(s_up, 1)

                def down(i, v):
                    s, c = v // 2, v % 2
                    pe.wait_ge(s_g, (i * 4 + v + 1) * M)
                    if c == 0:
                        pe.wait_ge(s_wd[s], i * 16 + 16)
                    if started(i, 2 - v):
                        pe.wait_ge(s_yr, i * 4 + v - 1)
                    for t in range(TILES[c]):
                        for k in range(M):
                            mm = pe.matmul(p_y[:, c, t], g[:, c, k, t * P:(t + 1) * P],
                                           wts[:, s, (2 * M + k) * P:(2 * M + k + 1) * P], start=(k == 0), stop=(k == M - 1))
                    mm.then_inc(s_y, 1)

                def pair(i, first=False, final=False):
                    for v in range(4):
                        if v < 3:
                            turn(i, v + 1)
                        elif not final:
                            turn(i + 1, 0)
                        up(i, v)
                        if v:
                            down(i, v - 1)
                        elif not first:
                            down(i - 1, 3)

                pe.wait_ge(s_id, 32)
                for c in range(EARLY):
                    shared_up(c)
                    if c:
                        shared_down(c - 1)
                shared_down(EARLY - 1)
                turn(0, 0)
                pe.wait_ge(s_sg, EARLY * SM)
                pe.wait_ge(s_sx, EARLY)
                pair(0, first=True)
                with pe.Fori(1, last) as i:
                    pair(i)
                pair(last, final=True)
                down(last, 3)
                pe.wait_ge(s_yr, U)
                for c in range(EARLY, NCH):
                    shared_up(c)
                for c in range(EARLY, NCH):
                    shared_down(c)
                for c in range(NCH):
                    pe.wait_ge(s_acc, c + 1)
                    if c >= 2:
                        pe.wait_ge(s_x, c - 1)
                    for t in range(CH // P):
                        mm = pe.transpose(p_t[:, c % 2, t], mine[:, 0, c * (CH // P) + t], ident[:])
                    mm.then_inc(s_turn, 1)

            @block.scalar
            def _(act):
                def shared(c):
                    for j in range(SM):
                        act.wait_ge(s_sup, c * SM + j + 1)
                        act.activation(gated[:, j % 2], p_h[:, j % 2, 0], ACT.Silu).then_inc(s_ssilu, 1)

                def silu(i, v):
                    n = TILES[v % 2] * P
                    for m in range(M):
                        act.wait_ge(s_up, (i * 4 + v) * M + m + 1)
                        act.activation(gated[:, m, 0:n], p_h[:, m, 0, 0:n], ACT.Silu).then_inc(s_silu, 1)

                def copy_rows(i, v):
                    s, c = v // 2, v % 2
                    act.wait_ge(s_y, i * 4 + v + 1)
                    if started(i, 2 - v):
                        act.wait_ge(s_yst[c], (i * 2 + s) * 16)
                    act.activation(yr[:, c, 0:TILES[c]], p_y[:, c, 0:TILES[c]], ACT.Copy).then_inc(s_yr, 1)

                def pair(i, first=False):
                    for v in range(4):
                        silu(i, v)
                        if v:
                            copy_rows(i, v - 1)
                        elif not first:
                            copy_rows(i - 1, 3)

                for c in range(EARLY):
                    shared(c)
                pair(0, first=True)
                with act.Fori(1, last + 1) as i:
                    pair(i)
                copy_rows(last, 3)
                for c in range(EARLY, NCH):
                    shared(c)
                for c in range(NCH):
                    act.wait_ge(s_get[c], 16 * TOPK * (CH // P))
                    for t in range(c * (CH // P), (c + 1) * (CH // P)):
                        ins = act.activation(second[:, t], mine[:, 1, t], ACT.Copy, scale=weight[:, 1, t:t + 1])
                    ins.then_inc(s_sc, 1)

            @block.vector
            def _(dve):
                def shared_gate(c):
                    for j in range(SM):
                        dve.wait_ge(s_ssilu, c * SM + j + 1)
                        if c >= 2:
                            dve.wait_ge(s_sy, c - 1)
                        dve.tensor_tensor(sg[:, c % 2, j], gated[:, j % 2], p_h[:, j % 2, 1], ALU.mult).then_inc(s_sg, 1)

                def shared_add(c):
                    dve.wait_ge(s_sy, c + 1)
                    xt = xT[:, c * CH:(c + 1) * CH]
                    dve.scalar_tensor_tensor(xt, p_y[:, c % 2].rearrange("p t d -> p (t d)"), 1.0 / SHARED, xt,
                                             ALU.mult, ALU.add).then_inc(s_sx, 1)

                def copy_slots(i, v):
                    c = v % 2
                    dve.wait_ge(s_t, i * 4 + v + 1)
                    if started(i, 2 - v):
                        dve.wait_ge(s_up, (i * 4 + v - 1) * M)
                    n = TILES[c] * P
                    dve.tensor_copy(xs[:, c, 0:n], p_t[:, c, 0:TILES[c]].rearrange("p t d -> p (t d)")).then_inc(s_xs, 1)

                def gate(i, v):
                    c = v % 2
                    n = TILES[c] * P
                    for m in range(M):
                        dve.wait_ge(s_silu, (i * 4 + v) * M + m + 1)
                        if started(i, 2 - v):
                            dve.wait_ge(s_y, i * 4 + v - 1)
                        dve.tensor_tensor(g[:, c, m, 0:n], gated[:, m, 0:n], p_h[:, m, 1, 0:n], ALU.mult).then_inc(s_g, 1)

                def pair(i, final=False):
                    for v in range(4):
                        if v < 3:
                            copy_slots(i, v + 1)
                        elif not final:
                            copy_slots(i + 1, 0)
                        gate(i, v)

                for c in range(EARLY):
                    shared_gate(c)
                    if c:
                        shared_add(c - 1)
                shared_add(EARLY - 1)
                copy_slots(0, 0)
                pair(0)
                with dve.Fori(1, last) as i:
                    pair(i)
                pair(last, final=True)
                for c in range(EARLY, NCH):
                    shared_gate(c)
                for c in range(EARLY, NCH):
                    shared_add(c)

                def residual(c):
                    dve.wait_ge(s_turn, c + 1)
                    dve.wait_ge(s_sx, NCH)
                    xt = xT[:, c * CH:(c + 1) * CH]
                    dve.tensor_tensor(xt, xt, p_t[:, c % 2].rearrange("p t d -> p (t d)"), ALU.add).then_inc(s_x, 1)

                for c in range(NCH):
                    dve.wait_ge(s_sc, c + 1)
                    for t in range(c * (CH // P), (c + 1) * (CH // P)):
                        ins = dve.scalar_tensor_tensor(mine[:, 0, t], mine[:, 0, t], weight[:, 0, t:t + 1], second[:, t],
                                                       ALU.mult, ALU.add)
                    ins.then_inc(s_acc, 1)
                    if c:
                        residual(c - 1)
                residual(NCH - 1)

            @block.gpsimd
            def _(pool):
                for t in range(NT):
                    for k in range(TOPK):
                        pool.indirect_dma_start(scratch["slots"], bass.IndirectOffsetOnAxis(ap=put[:, k, t:t + 1], axis=0),
                                                rows[:, t], None).then_inc(s_put, 16)
                for c in range(2):
                    pool.wait_ge(s_yst[c], 16 * EXP0)
                for t in range(NT):
                    for k in range(TOPK):
                        pool.indirect_dma_start(mine[:, k, t], None, scratch["y"],
                                                bass.IndirectOffsetOnAxis(ap=get[:, k, t:t + 1], axis=0)).then_inc(s_get[t // (CH // P)], 16)


HEADS, DH = 16, 8
GH = 4
GROUPS = HEADS // GH
UNITS = BATCH * GROUPS
KT = SEQ // P
VW = DH + 1
PARTS = 3
PAIRS = PARTS * PARTS
MROW = 96
SCALE = DH ** -0.5
MASKED = -1e30


def qkv(nc, lnT, w, scratch):
    with Phase(nc, "qkv") as ph:
        wqk = ph.sb("wqk", [P, 2, P])
        wv = ph.sb("wv", [P, P])
        rest = ph.sb("rest", [P, 2, CH])
        parts = ph.sb("parts", [P, 2, 2, PARTS, SEQ], BF16)
        vp = ph.sb("vp", [P, 2, GROUPS, KT, GH, VW])
        p_qk = ph.ps("p_qk", [P, CPB, 2, CH])
        p_v = ph.ps("p_v", [P, CPB, CH // P, P])
        s_w = ph.sem("weights_loaded")
        s_one = ph.sem("ones_set")
        s_qk = ph.sem("projected")
        s_hi = ph.sem("hi_cut")
        s_rest = ph.sem("rest_cut")
        s_mid = ph.sem("mid_cut")
        s_cut = ph.sem("parts_ready")
        s_v = ph.sem("v_projected")
        s_vc = ph.sem("v_copied")
        s_st = [[ph.sem(f"parts_stored{x}{j}") for j in range(2)] for x in range(2)]
        s_vst = [ph.sem(f"v_stored{i}") for i in range(2)]

        with ph.block() as block:
            @block.sync
            def _(sp):
                sp.dma_start(wqk[:], w["wqk"]).then_inc(s_w, 16)
                sp.dma_start(wv[:], w["wv"]).then_inc(s_w, 16)
                for b in range(BATCH):
                    x = b % 2
                    for j in range(2):
                        sp.wait_ge(s_cut, 2 * CPB * b + 2 * (CPB - 1) + j + 1)
                        for a in range(PARTS + 2 * j):
                            sp.dma_start(scratch["parts"][j, b, :, a],
                                         parts[:, x, j, a % PARTS]).then_inc(s_st[x][j], 16)
                    sp.wait_ge(s_vc, CPB * (b + 1))
                    sp.dma_start(scratch["v"][b].rearrange("g p k n -> p g k n"),
                                 vp[:, x].rearrange("p g k h v -> p g k (h v)")).then_inc(s_vst[x], 16)
                for x in range(2):
                    for j in range(2):
                        sp.wait_ge(s_st[x][j], 16 * (PARTS + 2 * j) * BATCH // 2)
                    sp.wait_ge(s_vst[x], 16 * BATCH // 2)

            @block.tensor
            def _(pe):
                pe.wait_ge(s_w, 32)
                for g in range(NCH):
                    c = g % CPB
                    for j in range(2):
                        if g >= CPB:
                            pe.wait_ge(s_rest, 2 * (g - CPB) + j + 1)
                        pe.matmul(p_qk[:, c, j], wqk[:, j], lnT[:, g * CH:(g + 1) * CH], start=True, stop=True).then_inc(s_qk, 1)
                    if g >= CPB:
                        pe.wait_ge(s_vc, g - CPB + 1)
                    for t in range(CH // P):
                        mm = pe.matmul(p_v[:, c, t], lnT[:, g * CH + t * P:g * CH + (t + 1) * P], wv[:], start=True, stop=True)
                    mm.then_inc(s_v, 1)

            @block.scalar
            def _(act):
                act.wait_ge(s_one, 1)
                for g in range(NCH):
                    b, c = g // CPB, g % CPB
                    act.wait_ge(s_v, g + 1)
                    if b >= 2:
                        act.wait_ge(s_vst[b % 2], b // 2 * 16)
                    for t in range(CH // P):
                        ins = act.activation(vp[:, b % 2, :, c * (CH // P) + t, :, 0:DH],
                                             p_v[:, c, t].rearrange("p (g h v) -> p g h v", g=GROUPS, h=GH), ACT.Copy)
                    ins.then_inc(s_vc, 1)

            @block.vector
            def _(dve):
                dve.memset(vp[:], 1.0).then_inc(s_one, 1)
                for g in range(NCH):
                    b, c = g // CPB, g % CPB
                    part = parts[:, b % 2, :, :, c * CH:(c + 1) * CH]
                    for j in range(2):
                        dve.wait_ge(s_qk, g * 2 + j + 1)
                        if b >= 2:
                            dve.wait_ge(s_st[b % 2][j], b // 2 * (16 * (PARTS + 2 * j)))
                        dve.tensor_copy(part[:, j, 0], p_qk[:, c, j]).then_inc(s_hi, 1)
                    for j in range(2):
                        dve.wait_ge(s_hi, g * 2 + j + 1)
                        if g:
                            dve.wait_ge(s_cut, g * 2 + j - 1)
                        dve.tensor_tensor(rest[:, j], p_qk[:, c, j], part[:, j, 0], ALU.subtract).then_inc(s_rest, 1)
                    for j in range(2):
                        dve.wait_ge(s_rest, g * 2 + j + 1)
                        dve.tensor_copy(part[:, j, 1], rest[:, j]).then_inc(s_mid, 1)
                    for j in range(2):
                        dve.wait_ge(s_mid, g * 2 + j + 1)
                        dve.tensor_tensor(part[:, j, 2], rest[:, j], part[:, j, 1], ALU.subtract).then_inc(s_cut, 1)


def attention(nc, att, w, scratch):
    HALF = KT // 2
    NST = KT + HALF
    NEXP = 2 * NST
    LOADS = 16 * (PARTS * (CPB + 1) + 1)
    LAST = UNITS - 1
    SLOTS = 3
    TURNS = (UNITS - 2) // SLOTS
    with Phase(nc, "attn") as ph:
        ident = ph.sb("ident", [P, P])
        identb = ph.sb("identb", [P, P], BF16)
        mask_q = ph.sb("mask_q", [P, P], BF16)
        mask_k = ph.sb("mask_k", [P, P], BF16)
        qs = [ph.sb(f"qs{i}", [P, CPB, GH, CH], BF16) for i in range(SLOTS)]
        ks = [ph.sb(f"ks{i}", [P, GH, SEQ], BF16) for i in range(SLOTS)]
        vs = [ph.sb(f"vs{i}", [P, KT, GH, VW]) for i in range(SLOTS)]
        mx = ph.sb("mx", [P, 2, GH, KT])
        top = ph.sb("top", [P, GH, HALF])
        ntop = ph.sb("ntop", [P, GH, HALF])
        mrest = ph.sb("mrest", [P, GH, HALF])
        mparts = ph.sb("mparts", [P, PARTS, 2, GH, HALF], BF16)
        mt = ph.sb("mt", [PARTS * GH * KT, 2, P], BF16)
        prob = ph.sb("prob", [P, 2, GH, CH])
        ob = ph.sb("ob", [P, 2, CH])
        rden = ph.sb("rden", [P, 2, HALF, GH, 1])
        p_m = ph.ps("p_m", [P, 3, CH])
        p_s = ph.ps("p_s", [P, 2, 2, CH])
        p_o = ph.ps("p_o", [P, CH])

        s_w = ph.sem("masks_loaded")
        s_qset = ph.sem("query_stacks_zeroed")
        s_kset = ph.sem("key_stacks_set")
        s_mx0 = ph.sem("maxima_filled")
        s_po0 = ph.sem("out_bank_zeroed")
        s_load = [ph.sem(f"loaded{i}") for i in range(SLOTS)]
        s_qz = ph.sem("max_rows_zeroed")
        s_job = ph.sem("job_given")
        s_done = ph.sem("job_done")
        s_m = ph.sem("max_step")
        s_mp = ph.sem("max_parts_ready")
        s_kz = ph.sem("key_stacks_zeroed")
        s_mrow = [ph.sem(f"max_rows_loaded{i}") for i in range(2)]
        s_st = ph.sem("scores_ready")
        s_exp = ph.sem("exp_done")
        s_pv = ph.sem("pv_done")
        s_ev = ph.sem("out_copied")
        s_rec = ph.sem("denominators_inverted")
        hold = ph.sem("wait_passed")

        steps = [(half, kt) for half in range(CPB) for kt in range((half + 1) * HALF)]
        half_end = [t for t, (half, kt) in enumerate(steps) if kt == (half + 1) * HALF - 1]

        def width(qt, c):
            return min(CH, (qt + 1) * P - c * CH)

        def first_query(half, kt):
            return max(kt * P - half * CH, 0)

        def maxima(half):
            out = []
            for qt in range(half * HALF, (half + 1) * HALF):
                for c in range(half + 1):
                    n = min(GH, CH // width(qt, c))
                    out += [("max", half, qt, c, range(h, h + n)) for h in range(0, GH, n)]
            return out

        before = maxima(0) + [("rows", 0)] + maxima(1)
        late = maxima(1)
        early = maxima(0)
        beside = early[:3] + [("rows", 1)] + early[3:5] + [("out", 1)] + early[5:] + late[:9] + [("rows", 0)] + late[9:13] + [("out", 0)] + late[13:]
        beside_first = [j for j in beside if j != ("out", 1)]
        beside_last = [("rows", 1), ("out", 1), ("out", 0)]

        def jobs_before(u):
            if isinstance(u, int) and u == 0:
                return len(before)
            return u * len(beside) + len(before) - 1

        def bank(jobs, k):
            return (k - len(jobs)) % 3

        def bank_free(jobs, k, start):
            return start + (k - 2 if k >= 3 else bank(jobs, k) - 2)

        with ph.block() as block:

            @block.sync
            def _(sp):
                for dst, src in ((identb, w["ident_bf16"]), (mask_q, w["mask_q"]), (mask_k, w["mask_k"]), (ident, w["ident"])):
                    sp.dma_start(dst[:], src).then_inc(s_w, 16)

                def load(u, s):
                    part = scratch["parts"].rearrange("j b (g h) a r t -> j (b g) (a r) h t", g=GROUPS)
                    for m in range(PARTS):
                        rows = slice(m * PARTS * DH, (m + 1) * PARTS * DH)
                        src = part[1, bass.ds(u, 1), m * DH:(m + PARTS) * DH]
                        sp.dma_start(ks[s][rows], src.rearrange("o a h t -> (o a) h t")).then_inc(s_load[s], 16)
                        for half in range(CPB):
                            src = part[0, bass.ds(u, 1), 0:PARTS * DH, :, half * CH:(half + 1) * CH]
                            sp.dma_start(qs[s][rows, half], src.rearrange("o a h t -> (o a) h t")).then_inc(s_load[s], 16)
                    v = scratch["v"].rearrange("b g p k n -> (b g) p k n")
                    sp.dma_start(vs[s][:].rearrange("p k h v -> p k (h v)"),
                                 v[bass.ds(u, 1)].rearrange("o p k n -> (o p) k n")).then_inc(s_load[s], 16)

                for s in range(SLOTS):
                    sp.wait_ge(s_qset, s + 1)
                    sp.wait_ge(s_kz, s + 1)
                    load(s, s)
                with sp.Fori(0, TURNS) as i:
                    for s in range(SLOTS):
                        u = i * SLOTS + s + SLOTS
                        sp.wait_ge(s_pv, (u - 2) * NST)
                        load(u, s)
                sp.wait_ge(s_pv, (LAST - 2) * NST)
                load(LAST, LAST % SLOTS)

            @block.tensor
            def _(pe):
                pe.wait_ge(s_w, 64)
                pe.wait_ge(s_po0, 1)

                def give(job, u, s, jobs, k, start, loads):
                    x = bank(jobs, k)
                    if not isinstance(start, int) or bank_free(jobs, k, start) > 0:
                        pe.wait_ge(s_done, bank_free(jobs, k, start))
                    if job[0] == "rows":
                        half = job[1]
                        pe.wait_ge(s_mp, (u + (1 - half)) * 2 + half + 1)
                        pe.transpose(p_m[0:PARTS * GH * KT, x, 0:P // 2].bitcast(BF16),
                                     mparts[:].rearrange("p a c h t -> p (a c h t)"), identb[:]).then_inc(s_job, 1)
                    elif job[0] == "out":
                        half = job[1]
                        pe.wait_ge(s_ev, (u - half) * 2 + half + 1)
                        for t in range(HALF):
                            mm = pe.transpose(p_m[:, x, t * P:(t + 1) * P], ob[:, half, t * P:(t + 1) * P], ident[:])
                        mm.then_inc(s_job, 1)
                    else:
                        _, half, qt, c, heads = job
                        if job == before[0]:
                            pe.wait_ge(s_load[s], loads * LOADS)
                            pe.wait_ge(s_qz, u + 2)
                            if isinstance(u, int) and u + 2 <= SLOTS:
                                pe.wait_ge(s_kset, u + 2)
                        wd = width(qt, c)
                        diagonal = (qt + 1) * P - c * CH <= CH
                        for n, h in enumerate(heads):
                            mm = pe.matmul(p_m[:, x, n * wd:(n + 1) * wd], qs[s][:, half, h, qt % HALF * P:(qt % HALF + 1) * P],
                                           ks[s][:, h, c * CH:c * CH + wd], start=True, stop=not diagonal)
                            if diagonal:
                                mm = pe.matmul(p_m[:, x, (n + 1) * wd - P:(n + 1) * wd], identb[:], mask_q[:], start=False, stop=True)
                        mm.then_inc(s_job, 1)

                def scores(u, s, t, pair):
                    half, kt = steps[t]
                    q0 = first_query(half, kt)
                    k = 2 * t + pair
                    if kt == 0 and pair == 0:
                        pe.wait_ge(s_mrow[half], u * 48 + 48)
                    if not isinstance(u, int) or u * NEXP + k >= 2:
                        pe.wait_ge(s_exp, u * NEXP + k - 1)
                    for j in range(2):
                        h = 2 * pair + j
                        on_diagonal = kt * P >= half * CH
                        mm = pe.matmul(p_s[:, pair, j, 0:CH - q0], ks[s][:, h, kt * P:(kt + 1) * P],
                                       qs[s][:, half, h, q0:CH], start=True, stop=not on_diagonal)
                        if on_diagonal:
                            mm = pe.matmul(p_s[:, pair, j, 0:P], identb[:], mask_k[:], start=False, stop=True)
                    mm.then_inc(s_st, 1)

                def values(u, s, t):
                    half, kt = steps[t]
                    q0 = first_query(half, kt)
                    if kt == 0 and (not isinstance(u, int) or 2 * u + half > 0):
                        pe.wait_ge(s_ev, u * 2 + half)
                    pe.wait_ge(s_exp, u * NEXP + 2 * t + 2)
                    for h in range(GH):
                        mm = pe.matmul(p_o[32 * h:32 * h + VW, q0:CH], vs[s][:, kt, h], prob[:, t % 2, h, 0:CH - q0],
                                       start=(kt == 0), stop=(kt == (half + 1) * HALF - 1))
                    mm.then_inc(s_pv, 1)

                def unit(u, s, jobs, loads):
                    start = jobs_before(u)
                    cols = [CH - first_query(*step) for step in steps]
                    of_maxima = sum(width(j[2], j[3]) * len(j[4]) for j in jobs if j[0] == "max")
                    given, spent = 0, 0

                    def due(t, point):
                        nonlocal given, spent
                        share = (sum(cols[:t]) + cols[t] * point / 3) / sum(cols)
                        while given < len(jobs):
                            job = jobs[given]
                            if job[0] == "max":
                                if spent >= share * of_maxima:
                                    return
                                spent += width(job[2], job[3]) * len(job[4])
                            elif job == ("out", 1) and t < 1 or job == ("out", 0) and t < half_end[0] + 3:
                                return
                            give(job, u, (s + 1) % SLOTS, jobs, given, start, loads)
                            given += 1

                    for t in range(NST):
                        scores(u, s, t, 0)
                        due(t, 1)
                        scores(u, s, t, 1)
                        due(t, 2)
                        if t:
                            values(u, s, t - 1)
                        elif not isinstance(u, int) or u:
                            values(u - 1, (s - 1) % SLOTS, NST - 1)
                        due(t, 3)
                    assert given == len(jobs)

                for k, job in enumerate(before):
                    give(job, -1, 0, before, k, 0, 1)
                unit(0, 0, beside_first, 1)
                with pe.Fori(0, TURNS) as i:
                    for n in range(1, SLOTS + 1):
                        unit(i * SLOTS + n, n % SLOTS, beside, i + (n + 1) // SLOTS + 1)
                for u in range(TURNS * SLOTS + 1, UNITS):
                    unit(u, u % SLOTS, beside if u < LAST else beside_last, (u + 1) // SLOTS + 1)
                values(LAST, LAST % SLOTS, NST - 1)
                give(("out", 1), UNITS, 0, [("out", 1)], 0, jobs_before(LAST) + len(beside_last), 0)

            @block.scalar
            def _(act):
                def copy_out(u, half):
                    act.wait_ge(s_pv, u * NST + half_end[half] + 1)
                    if not isinstance(u, int) or u:
                        act.wait_ge(s_rec, u * 2 + half - 1)
                    act.activation(ob[:, half], p_o[:], ACT.Copy).then_inc(s_ev, 1)

                def unit(u):
                    for t, (half, kt) in enumerate(steps):
                        q0 = first_query(half, kt)
                        for pair in range(2):
                            act.wait_ge(s_st, u * NEXP + 2 * t + pair + 1)
                            if pair == 0 and (not isinstance(u, int) or u * NST + t >= 2):
                                act.wait_ge(s_pv, u * NST + t - 1)
                            act.activation(prob[:, t % 2, 2 * pair:2 * pair + 2, 0:CH - q0], p_s[:, pair, :, 0:CH - q0],
                                           ACT.Exp, scale=SCALE).then_inc(s_exp, 1)
                        if t == half_end[0] + 1:
                            copy_out(u, 0)
                        if t == 0 and (not isinstance(u, int) or u):
                            copy_out(u - 1, 1)

                unit(0)
                with act.Fori(1, UNITS) as u:
                    unit(u)
                copy_out(LAST, 1)

            @block.vector
            def _(dve):
                for s in range(SLOTS):
                    dve.memset(ks[s][:].bitcast(mybir.dt.uint32), 0).then_inc(s_kz, 1)
                    dve.memset(qs[s][:].bitcast(mybir.dt.uint32), 0).then_inc(s_qset, 1)
                dve.memset(p_o[:], 0.0).then_inc(s_po0, 1)
                dve.memset(mx[:], FILL).then_inc(s_mx0, 1)
                dve.memset(mparts[:], 0.0).then_inc(s_mx0, 1)
                dve.wait_ge(s_mx0, 2)

                def cut(q, half, done):
                    dve.wait_ge(s_done, done)
                    tiles = slice(half * HALF, (half + 1) * HALF)
                    dve.tensor_tensor(top[:], mx[:, 0, :, tiles], mx[:, 1, :, tiles], ALU.max).then_inc(s_m, 1)
                    dve.wait_ge(s_m, q * 5 + 1)
                    dve.tensor_scalar(ntop[:], top[:], -1.0, None, ALU.mult).then_inc(s_m, 1)
                    dve.tensor_scalar(mparts[:, 0, half], top[:], -1.0, None, ALU.mult).then_inc(s_m, 1)
                    dve.wait_ge(s_m, q * 5 + 3)
                    dve.tensor_tensor(mrest[:], ntop[:], mparts[:, 0, half], ALU.subtract).then_inc(s_m, 1)
                    dve.wait_ge(s_m, q * 5 + 4)
                    dve.tensor_copy(mparts[:, 1, half], mrest[:]).then_inc(s_m, 1)
                    dve.wait_ge(s_m, q * 5 + 5)
                    dve.tensor_tensor(mparts[:, 2, half], mrest[:], mparts[:, 1, half], ALU.subtract).then_inc(s_mp, 1)

                def do(job, u, jobs, k, start):
                    x = bank(jobs, k)
                    dve.wait_ge(s_job, start + k + 1)
                    if job[0] == "rows":
                        half = job[1]
                        v = u + (1 - half)
                        if not isinstance(v, int) or v:
                            dve.wait_ge(s_mrow[half], v * 48)
                        dve.tensor_copy(mt[:, half], p_m[0:PARTS * GH * KT, x, 0:P // 2].bitcast(BF16)).then_inc(s_done, 1)
                    elif job[0] == "out":
                        half = job[1]
                        v = u - half
                        turned = p_m[:, x].rearrange("p (t h v) -> p t h v", t=HALF, h=GH)
                        if not isinstance(v, int) or v:
                            dve.wait_ge(s_done, start)
                        dve.reciprocal(rden[:, half], turned[:, :, :, DH:VW]).then_inc(s_rec, 1)
                        dve.wait_ge(s_rec, v * 2 + half + 1)
                        dve.tensor_tensor(att[:, bass.ds(v, 1), half * HALF:(half + 1) * HALF].rearrange("p o t (h v) -> p (o t) h v", h=GH),
                                          turned[:, :, :, 0:DH], rden[:, half].to_broadcast([P, HALF, GH, DH]), ALU.mult).then_inc(s_done, 1)
                    else:
                        _, half, qt, c, heads = job
                        wd, n = width(qt, c), len(heads)
                        dve.tensor_reduce(mx[:, c, heads[0]:heads[0] + n, qt:qt + 1],
                                          p_m[:, x, 0:n * wd].rearrange("p (h w) -> p h w", h=n), AX.X, ALU.max).then_inc(s_done, 1)

                def work(u, jobs):
                    start = jobs_before(u)
                    for k, job in enumerate(jobs):
                        do(job, u, jobs, k, start)
                        if job[0] == "max" and job == maxima(job[1])[-1]:
                            cut(u * 2 + 2 + job[1], job[1], start + k + 1)

                for k, job in enumerate(before):
                    do(job, -1, before, k, 0)
                    if job[0] == "max" and job == maxima(job[1])[-1]:
                        cut(job[1], job[1], k + 1)
                work(0, beside_first)
                with dve.Fori(1, LAST) as u:
                    work(u, beside)
                work(LAST, beside_last)
                do(("out", 1), UNITS, [("out", 1)], 0, jobs_before(LAST) + len(beside_last))

            @block.gpsimd
            def _(pool):
                def zero(s):
                    pool.memset(qs[s][MROW:MROW + PARTS].bitcast(mybir.dt.uint32), 0).then_inc(s_qz, 1)

                def max_rows(s, half, done):
                    pool.wait_ge(s_done, done)
                    waited(pool, hold)
                    for a in range(PARTS):
                        n = GH * HALF
                        pool.dma_start(qs[s][MROW + a:MROW + a + 1, half].rearrange("a h (t p) -> a (h t) p", p=P),
                                       mt[(2 * a + half) * n:(2 * a + half + 1) * n, half]).then_inc(s_mrow[half], 16)

                def unit(u, s, jobs):
                    max_rows(s, 1, jobs_before(u) + jobs.index(("rows", 1)) + 1)
                    if jobs == beside and (not isinstance(u, int) or u < LAST - 1):
                        pool.wait_ge(s_pv, u * NST)
                        waited(pool, hold)
                        zero((s + 2) % SLOTS)
                    if jobs != beside_last:
                        max_rows((s + 1) % SLOTS, 0, jobs_before(u) + jobs.index(("rows", 0)) + 1)

                for s in range(SLOTS):
                    pool.wait_ge(s_kz, s + 1)
                    pool.memset(ks[s][MROW:MROW + PARTS], 1.0).then_inc(s_kset, 1)
                    pool.wait_ge(s_qset, s + 1)
                    zero(s)
                max_rows(0, 0, before.index(("rows", 0)) + 1)
                unit(0, 0, beside_first)
                with pool.Fori(0, TURNS) as i:
                    for n in range(1, SLOTS + 1):
                        unit(i * SLOTS + n, n % SLOTS, beside)
                for u in range(TURNS * SLOTS + 1, UNITS):
                    unit(u, u % SLOTS, beside if u < LAST else beside_last)


def attention_out(nc, xT, att, w):
    with Phase(nc, "attn_out") as ph:
        ident = ph.sb("ident", [P, P])
        wo = ph.sb("wo", [P, D])
        heads = ph.sb("heads", [P, 2, CH // P, GROUPS, GH * DH])
        turned = ph.sb("turned", [P, 2, CH])
        p_t = ph.ps("p_t", [P, 2, CH])
        p_o = ph.ps("p_o", [P, 2, CH])
        s_w = ph.sem("weights_loaded")
        s_g = ph.sem("heads_grouped")
        s_t = ph.sem("turned")
        s_c = ph.sem("turned_copied")
        s_o = ph.sem("projected")
        s_x = ph.sem("residual_added")

        with ph.block() as block:
            @block.sync
            def _(sp):
                sp.dma_start(wo[:], w["wo"]).then_inc(s_w, 16)
                sp.dma_start(ident[:], w["ident"]).then_inc(s_w, 16)

            @block.tensor
            def _(pe):
                pe.wait_ge(s_w, 32)
                for c in range(NCH + 1):
                    if c < NCH:
                        pe.wait_ge(s_g, c + 1)
                        if c >= 2:
                            pe.wait_ge(s_c, c - 1)
                        for t in range(CH // P):
                            mm = pe.transpose(p_t[:, c % 2, t * P:(t + 1) * P],
                                              heads[:, c % 2, t].rearrange("p g n -> p (g n)"), ident[:])
                        mm.then_inc(s_t, 1)
                    if c:
                        pe.wait_ge(s_c, c)
                        if c >= 3:
                            pe.wait_ge(s_x, c - 2)
                        pe.matmul(p_o[:, (c - 1) % 2], wo[:], turned[:, (c - 1) % 2], start=True, stop=True).then_inc(s_o, 1)

            @block.scalar
            def _(act):
                for c in range(NCH):
                    act.wait_ge(s_t, c + 1)
                    if c >= 2:
                        act.wait_ge(s_o, c - 1)
                    act.activation(turned[:, c % 2], p_t[:, c % 2], ACT.Copy).then_inc(s_c, 1)

            @block.vector
            def _(dve):
                for c in range(NCH + 1):
                    if c < NCH:
                        b, half = c // CPB, c % CPB
                        tiles = att[:, b * GROUPS:(b + 1) * GROUPS, half * (CH // P):(half + 1) * (CH // P)]
                        if c >= 2:
                            dve.wait_ge(s_t, c - 1)
                        dve.tensor_copy(heads[:, c % 2], tiles.rearrange("p g t n -> p t g n")).then_inc(s_g, 1)
                    if c:
                        dve.wait_ge(s_o, c)
                        xt = xT[:, (c - 1) * CH:c * CH]
                        dve.tensor_tensor(xt, xt, p_o[:, (c - 1) % 2], ALU.add).then_inc(s_x, 1)


EXP1, HID1 = 8, 512
THRESHOLD = 0.125


def router1(nc, xT, lnT, w, scratch):
    E, T = EXP1, NT
    with Phase(nc, "router1") as ph:
        ident = ph.sb("ident", [P, P])
        gate_w = ph.sb("gate_w", [P, E + 1])
        gate_b = ph.sb("gate_b", [P, E + 1])
        b2 = ph.sb("b2", [E, D])
        logit = ph.sb("logit", [P, T, E + 1])
        top = ph.sb("top", [P, T])
        score = ph.sb("score", [P, T, E])
        sig = ph.sb("sig", [P, T])
        total = ph.sb("total", [P, T])
        none = ph.sb("none", [P, T])
        tmp = ph.sb("tmp", [P, T, E])
        wt = ph.sb("wt", [E, TOK])
        p_lg = ph.ps("p_lg", [P, T, E + 1])
        p_t = ph.ps("p_t", [E, 2, CH])
        p_b = ph.ps("p_b", [P, 2, CH])
        s_w = ph.sem("weights_loaded")
        s_lg = ph.sem("logits_ready")
        s_v = ph.sem("vector_step")
        s_e = ph.sem("exp_done")
        s_wt = ph.sem("weights_ready")
        s_t = ph.sem("turned")
        s_tc = ph.sem("turned_copied")
        s_b = ph.sem("bias_product")
        s_x = ph.sem("residual_added")
        s_st = ph.sem("weights_stored")

        with ph.block() as block:
            @block.sync
            def _(sp):
                for dst, src in ((ident, w["ident"]), (gate_w, w["gate1_w"]), (gate_b, w["gate1_b"]), (b2, w["b2"])):
                    sp.dma_start(dst[:], src).then_inc(s_w, 16)
                sp.wait_ge(s_tc, NCH)
                sp.dma_start(scratch["wt"], wt[:]).then_inc(s_st, 16)
                sp.wait_ge(s_st, 16)

            @block.tensor
            def _(pe):
                pe.wait_ge(s_w, 64)
                for t in range(T):
                    mm = pe.matmul(p_lg[:, t], lnT[:, t * P:(t + 1) * P], gate_w[:], start=True, stop=True)
                mm.then_inc(s_lg, 1)
                pe.wait_ge(s_wt, 1)
                for c in range(NCH):
                    if c >= 2:
                        pe.wait_ge(s_tc, c - 1)
                        pe.wait_ge(s_x, c - 1)
                    for t in range(CH // P):
                        mm = pe.transpose(p_t[:, c % 2, t * P:(t + 1) * P], tmp[:, c * (CH // P) + t], ident[:])
                    mm.then_inc(s_t, 1)
                    pe.wait_ge(s_tc, c + 1)
                    pe.matmul(p_b[:, c % 2], b2[:], wt[:, c * CH:(c + 1) * CH], start=True, stop=True).then_inc(s_b, 1)

            @block.scalar
            def _(act):
                act.wait_ge(s_v, 3)
                act.activation(tmp[:], score[:], ACT.Exp).then_inc(s_e, 1)
                act.activation(sig[:], logit[:, :, E], ACT.Exp, scale=-1.0).then_inc(s_e, 1)

            @block.vector
            def _(dve):
                count = [0]

                def step(ins):
                    count[0] += 1
                    ins.then_inc(s_v, 1)
                    dve.wait_ge(s_v, count[0])

                over = lambda a: a.unsqueeze(2).to_broadcast([P, T, E])
                dve.wait_ge(s_w, 64)
                dve.wait_ge(s_lg, 1)
                step(dve.tensor_tensor(logit[:], p_lg[:], gate_b[:].unsqueeze(1).to_broadcast([P, T, E + 1]), ALU.add))
                step(dve.tensor_reduce(top[:], logit[:, :, 0:E], AX.X, ALU.max))
                step(dve.tensor_tensor(score[:], logit[:, :, 0:E], over(top[:]), ALU.subtract))
                dve.wait_ge(s_e, 2)
                step(dve.tensor_reduce(total[:], tmp[:], AX.X, ALU.add))
                step(dve.reciprocal(total[:], total[:]))
                step(dve.tensor_scalar(sig[:], sig[:], 1.0, None, ALU.add))
                step(dve.reciprocal(sig[:], sig[:]))
                step(dve.tensor_scalar(sig[:], sig[:], THRESHOLD, None, ALU.mult))
                step(dve.tensor_tensor(score[:], tmp[:], over(total[:]), ALU.mult))
                step(dve.tensor_tensor(score[:], score[:], over(sig[:]), ALU.subtract))
                step(dve.tensor_scalar(score[:], score[:], 0.0, None, ALU.max))
                step(dve.tensor_reduce(total[:], score[:], AX.X, ALU.add))
                step(dve.tensor_scalar(none[:], total[:], 0.0, None, ALU.is_equal))
                step(dve.tensor_tensor(total[:], total[:], none[:], ALU.add))
                step(dve.reciprocal(total[:], total[:]))
                step(dve.tensor_tensor(tmp[:], score[:], over(total[:]), ALU.mult))
                dve.sem_inc(s_wt, 1)
                for c in range(NCH):
                    dve.wait_ge(s_t, c + 1)
                    dve.tensor_copy(wt[:, c * CH:(c + 1) * CH], p_t[:, c % 2]).then_inc(s_tc, 1)
                    dve.wait_ge(s_b, c + 1)
                    xt = xT[:, c * CH:(c + 1) * CH]
                    dve.tensor_tensor(xt, xt, p_b[:, c % 2], ALU.add).then_inc(s_x, 1)


def experts1(nc, xT, lnT, w, scratch):
    F = HID1 // P
    F32R = mybir.dt.float32r
    ON_POOL = F // 2
    U = CPB * EXP1
    TURNS = NCH // CPB
    with Phase(nc, "experts1") as ph:
        b1 = ph.sb("b1", [P, EXP1, F])
        raw = ph.sb("raw", [P, 2, 2 * HID1])
        wh = ph.sb("wh", [P, EXP1, 2 * HID1], F32R)
        wl = ph.sb("wl", [P, EXP1, 2 * HID1], F32R)
        xh = ph.sb("xh", [P, CPB, CH], F32R)
        xl = ph.sb("xl", [P, CPB, CH], F32R)
        share = ph.sb("share", [P, CPB, EXP1, CH])
        g = ph.sb("g", [P, F, CH])
        gh = ph.sb("gh", [P, 2, F, CH], F32R)
        gl = ph.sb("gl", [P, 2, F, CH], F32R)
        part = ph.sb("part", [P, 2, CH])
        p_h = ph.ps("p_h", [P, F, CH])
        p_y = ph.ps("p_y", [P, 2, CH])
        s_b1 = ph.sem("bias_loaded")
        s_raw = [ph.sem(f"weights_loaded{i}") for i in range(2)]
        s_wh = ph.sem("weights_high")
        s_w = ph.sem("weights_cut")
        s_xh = ph.sem("tokens_high")
        s_xs = ph.sem("tokens_cut")
        s_share = [ph.sem(f"shares_loaded{i}") for i in range(CPB)]
        s_up = ph.sem("up_done")
        s_g = ph.sem("gelu_done")
        s_hi = ph.sem("high_cut")
        s_lp = ph.sem("low_cut_by_pool")
        s_lv = ph.sem("low_cut_by_vector")
        s_y = ph.sem("down_done")
        s_part = ph.sem("weighted")
        s_x = ph.sem("residual_added")

        def products(stationary, moving):
            (ah, al), (bh, bl) = stationary, moving
            return (ah, bh), (al, bh), (ah, bl)

        def later(i, v, units=1):
            return not isinstance(i, int) or i * U + v >= units

        with ph.block() as block:
            @block.sync
            def _(sp):
                sp.dma_start(b1[:], w["b1"]).then_inc(s_b1, 16)

                def weights(e):
                    if e >= 2:
                        sp.wait_ge(s_w, e - 1)
                    sp.dma_start(raw[:, e % 2], w["fw"][e]).then_inc(s_raw[e % 2], 16)

                def shares(c, x):
                    src = scratch["wt"].rearrange("(o e) t -> o e t", o=1)[:, :, bass.ds(c * CH, CH)]
                    sp.dma_start(share[:, x], src.to_broadcast([P, EXP1, CH])).then_inc(s_share[x], 16)

                weights(0)
                weights(1)
                for x in range(CPB):
                    shares(x, x)
                for e in range(2, EXP1):
                    weights(e)
                with sp.Fori(1, TURNS) as i:
                    for x in range(CPB):
                        c = i * CPB + x
                        sp.wait_ge(s_part, (c - 1) * EXP1)
                        shares(c, x)

            @block.tensor
            def _(pe):
                def up(i, v):
                    n, x, e = i * U + v, v // EXP1, v % EXP1
                    if e == 0:
                        pe.wait_ge(s_xs, i * CPB + x + 1)
                    if isinstance(i, int) and x == 0:
                        pe.wait_ge(s_w, e + 1)
                    for m in range(F):
                        if later(i, v):
                            pe.wait_ge(s_g, (n - 1) * F + m + 1)
                        cols = slice(m * P, (m + 1) * P)
                        for k, (a, b) in enumerate(products((wh, wl), (xh, xl))):
                            mm = pe.matmul(p_h[:, m], a[:, e, cols], b[:, x], start=(k == 0), stop=(k == 2))
                        mm.then_inc(s_up, 1)

                def down(i, v):
                    n, e = i * U + v, v % EXP1
                    if later(i, v, 2):
                        pe.wait_ge(s_part, n - 1)
                    for m in range(F):
                        if m < ON_POOL:
                            pe.wait_ge(s_lp, n * ON_POOL + m + 1)
                        else:
                            pe.wait_ge(s_lv, n * (F - ON_POOL) + m - ON_POOL + 1)
                        cols = slice((F + m) * P, (F + m + 1) * P)
                        for k, (a, b) in enumerate(products((wh, wl), (gh, gl))):
                            mm = pe.matmul(p_y[:, v % 2], a[:, e, cols], b[:, v % 2, m],
                                           start=(m == 0 and k == 0), stop=(m == F - 1 and k == 2))
                    mm.then_inc(s_y, 1)

                def turn(i):
                    for v in range(U):
                        up(i, v)
                        if v:
                            down(i, v - 1)
                        elif later(i, v):
                            down(i - 1, U - 1)

                turn(0)
                with pe.Fori(1, TURNS) as i:
                    turn(i)
                down(TURNS - 1, U - 1)

            @block.scalar
            def _(act):
                def turn(i):
                    for v in range(U):
                        n = i * U + v
                        for m in range(F):
                            act.wait_ge(s_up, n * F + m + 1)
                            if later(i, v):
                                if m < ON_POOL:
                                    act.wait_ge(s_lp, (n - 1) * ON_POOL + m + 1)
                                else:
                                    act.wait_ge(s_lv, (n - 1) * (F - ON_POOL) + m - ON_POOL + 1)
                            act.activation(g[:, m], p_h[:, m], ACT.Gelu_apprx_tanh, bias=b1[:, v % EXP1, m:m + 1]).then_inc(s_g, 1)

                act.wait_ge(s_b1, 16)
                turn(0)
                with act.Fori(1, TURNS) as i:
                    turn(i)

            @block.vector
            def _(dve):
                def cut_weights(e):
                    dve.wait_ge(s_raw[e % 2], 16 * (e // 2 + 1))
                    dve.tensor_copy(wh[:, e], raw[:, e % 2]).then_inc(s_wh, 1)
                    dve.wait_ge(s_wh, e + 1)
                    dve.tensor_tensor(wl[:, e], raw[:, e % 2], wh[:, e].bitcast(F32), ALU.subtract).then_inc(s_w, 1)

                def cut_tokens(i, x):
                    c = i * CPB + x
                    tok = bass.ds(c * CH, CH)
                    if later(i, 0) or x >= CPB:
                        dve.wait_ge(s_up, (c - 1) * (EXP1 * F))
                    dve.tensor_copy(xh[:, x], lnT[:, tok]).then_inc(s_xh, 1)
                    dve.wait_ge(s_xh, c + 1)
                    dve.tensor_tensor(xl[:, x], lnT[:, tok], xh[:, x].bitcast(F32), ALU.subtract).then_inc(s_xs, 1)

                def cut(i, v):
                    n = i * U + v
                    if later(i, v, 2):
                        dve.wait_ge(s_y, n - 1)
                    for m in range(F):
                        dve.wait_ge(s_g, n * F + m + 1)
                        dve.tensor_copy(gh[:, v % 2, m], g[:, m]).then_inc(s_hi, 1)
                        if m >= ON_POOL:
                            dve.wait_ge(s_hi, n * F + m + 1)
                            dve.tensor_tensor(gl[:, v % 2, m], g[:, m], gh[:, v % 2, m].bitcast(F32), ALU.subtract).then_inc(s_lv, 1)

                def add(i, v):
                    n, x, e = i * U + v, v // EXP1, v % EXP1
                    dve.wait_ge(s_y, n + 1)
                    if e == 0:
                        dve.wait_ge(s_share[x], i * 16 + 16)
                    if later(i, v, 2):
                        dve.wait_ge(s_x, n - 1)
                    dve.tensor_tensor(part[:, v % 2], p_y[:, v % 2], share[:, x, e], ALU.mult).then_inc(s_part, 1)
                    dve.wait_ge(s_part, n + 1)
                    if later(i, v):
                        dve.wait_ge(s_x, n)
                    tok = bass.ds((i * CPB + x) * CH, CH)
                    dve.tensor_tensor(xT[:, tok], xT[:, tok], part[:, v % 2], ALU.add).then_inc(s_x, 1)

                def turn(i):
                    for v in range(U):
                        if v % EXP1 == 0 and v:
                            cut_tokens(i, v // EXP1)
                        if v == 0 and later(i, v):
                            cut_tokens(i, 0)
                        cut(i, v)
                        if isinstance(i, int) and v + 2 < EXP1:
                            cut_weights(v + 2)
                        if v:
                            add(i, v - 1)
                        elif later(i, v):
                            add(i - 1, U - 1)

                cut_tokens(0, 0)
                cut_weights(0)
                cut_weights(1)
                turn(0)
                with dve.Fori(1, TURNS) as i:
                    turn(i)
                add(TURNS - 1, U - 1)

            @block.gpsimd
            def _(pool):
                def turn(i):
                    for v in range(U):
                        n = i * U + v
                        for m in range(ON_POOL):
                            pool.wait_ge(s_hi, n * F + m + 1)
                            pool.tensor_tensor(gl[:, v % 2, m], g[:, m], gh[:, v % 2, m].bitcast(F32), ALU.subtract).then_inc(s_lp, 1)

                turn(0)
                with pool.Fori(1, TURNS) as i:
                    turn(i)


def shape_constants():
    import numpy as np
    bf16 = mybir.dt.np(BF16)
    sel = np.zeros((P, STATE, P), np.float32)
    for s in range(STATE):
        for part in range(3):
            sel[32 * part + s, s, :] = 1.0
    return {
        "ones_over_d": np.full((P, P), 1.0 / D, np.float32),
        "ident": np.eye(P, dtype=np.float32),
        "sel": sel.astype(bf16),
        "prio": np.tile(EXP0 - np.arange(EXP0, dtype=np.float32), (P, 1)),
        "before": np.triu(np.ones((P, P), np.float32), 1).astype(bf16),
        "ones_bf16": np.ones((P, P), bf16),
        "ident_bf16": np.eye(P).astype(bf16),
        "mask_q": (np.triu(np.ones((P, P), np.float32), 1) * MASKED).astype(bf16),
        "mask_k": (np.tril(np.ones((P, P), np.float32), -1) * MASKED).astype(bf16),
        "slot_base": np.tile(CAP * np.arange(EXP0, dtype=np.float32), (P, 1)),
        "spare": (NSLOT + np.arange(TOPK * TOK, dtype=np.float32)).reshape(TOPK, NT, P).transpose(2, 0, 1).copy(),
        "again": np.tile((np.arange(NT) > 0).astype(np.float32), (P, EXP0, 1)),
    }


def lay_out(inputs):
    import numpy as np
    i = {k: np.asarray(v) for k, v in inputs.items()}
    c = np.ascontiguousarray

    def blocks(a):
        return c(a.reshape((NBLK, P) + a.shape[1:]).swapaxes(0, 1))

    out = {"x": c(i["L0_attn_x"].reshape(TOK, D).T)}
    out["in_proj"] = c(i["L0_attn_in_proj_w"].T)
    out["norm_w"] = c(i["L0_attn_norm_w"].reshape(P, 1))
    out["conv_w"] = blocks(i["L0_attn_conv_w"])
    out["conv_b"] = blocks(i["L0_attn_conv_b"])
    xp = i["L0_attn_x_proj_w"]
    wide = np.zeros((P, INNER), xp.dtype)
    for part in range(3):
        wide[32 * part:32 * part + 32] = xp[RANK:]
    wide[96:96 + RANK] = xp[:RANK]
    out["x_proj"] = blocks(c(wide.T))
    dt = np.zeros((P, INNER), xp.dtype)
    dt[96:96 + RANK] = i["L0_attn_dt_proj_w"].T
    out["dt_proj"] = dt
    out["dt_b"] = blocks(i["L0_attn_dt_proj_b"])
    out["a_log"] = blocks(i["L0_attn_A_log"])
    out["d_skip"] = blocks(i["L0_attn_D"])
    out["out_proj"] = blocks(c(i["L0_attn_out_proj_w"].T))
    out["gate_w"] = c(i["L0_ffn_gate_w"])
    out["gate_b"] = c(np.broadcast_to(i["L0_ffn_gate_b"], (P, EXP0)))

    def expert(w1, w3, w2):
        down = w2.reshape(w2.shape[0], HID0 // P, P, D).swapaxes(1, 2).reshape(w2.shape[0], P, HID0)
        return np.concatenate([w1, w3, down], axis=2)

    out["ew"] = np.concatenate([expert(i["L0_ffn_ew1"], i["L0_ffn_ew3"], i["L0_ffn_ew2"]),
                                expert(i["L0_ffn_sw1"], i["L0_ffn_sw3"], i["L0_ffn_sw2"])], axis=0)
    hk = HEADS * DH
    out["wqk"] = np.stack([i["L1_attn_WQ"].reshape(hk, D).T, i["L1_attn_WK"].reshape(hk, D).T], axis=1)
    out["wv"] = c(i["L1_attn_WV"].reshape(hk, D).T)
    out["wo"] = c(i["L1_attn_WO"].transpose(0, 2, 1).reshape(hk, D))
    out["gate1_w"] = np.concatenate([i["L1_ffn_Wg"], i["L1_ffn_Wt"]], axis=1)
    out["gate1_b"] = c(np.broadcast_to(np.concatenate([i["L1_ffn_bg"], i["L1_ffn_bt"]]), (P, EXP1 + 1)))
    out["b1"] = c(i["L1_ffn_b1"].reshape(EXP1, HID1 // P, P).transpose(2, 0, 1))
    out["b2"] = c(i["L1_ffn_b2"])
    down = i["L1_ffn_W2"].reshape(EXP1, HID1 // P, P, D).swapaxes(1, 2).reshape(EXP1, P, HID1)
    out["fw"] = np.concatenate([i["L1_ffn_W1"], down], axis=2)
    return out


def program(nc, w, scratch, yT, stages=("mamba", "moe0", "attn", "moe1"), x_in=None):
    with Phase(nc, "main") as main:
        xT = main.sb("xT", [P, TOK])
        if x_in is not None:
            with Phase(nc, "load") as ph:
                s_x = ph.sem("x_loaded")
                with ph.block() as block:
                    @block.sync
                    def _(sp):
                        sp.dma_start(xT[:], x_in).then_inc(s_x, 16)
                        sp.wait_ge(s_x, 16)
        if "mamba" in stages:
            with Phase(nc, "mamba") as ph:
                delta = ph.sb("delta", [P, BATCH, NBLK, SEQ])
                du = ph.sb("du", [P, BATCH, NBLK, SEQ])
                bc_split = ph.sb("bc_split", [P, TOK], BF16)
                mamba_prep(nc, xT, delta, du, bc_split, w["x"], w, scratch)
                mamba_scan(nc, xT, delta, du, bc_split, w, scratch)
        if "moe0" in stages:
            with Phase(nc, "moe0") as ph:
                lnT = ph.sb("lnT", [P, TOK])
                rows = ph.sb("rows", [P, NT, D])
                weight = ph.sb("weight", [P, TOPK, NT])
                put = ph.sb("put", [P, TOPK, NT], mybir.dt.uint32)
                get = ph.sb("get", [P, TOPK, NT], mybir.dt.uint32)
                layer_norm(nc, xT, lnT, w, "norm1")
                router0(nc, lnT, rows, weight, put, get, w, scratch)
                experts0(nc, xT, lnT, rows, weight, put, get, w, scratch)
        if "attn" in stages:
            with Phase(nc, "qkv_of") as ph:
                lnT = ph.sb("lnT", [P, TOK])
                layer_norm(nc, xT, lnT, w, "norm2")
                qkv(nc, lnT, w, scratch)
            with Phase(nc, "attn_of") as ph:
                att = ph.sb("att", [P, UNITS, KT, GH * DH])
                attention(nc, att, w, scratch)
                attention_out(nc, xT, att, w)
        if "moe1" in stages:
            with Phase(nc, "moe1") as ph:
                lnT = ph.sb("lnT", [P, TOK])
                layer_norm(nc, xT, lnT, w, "norm3")
                router1(nc, xT, lnT, w, scratch)
                experts1(nc, xT, lnT, w, scratch)
        with Phase(nc, "store") as ph:
            s_y = ph.sem("y_stored")
            with ph.block() as block:
                @block.sync
                def _(sp):
                    sp.dma_start(yT, xT[:]).then_inc(s_y, 16)
                    sp.wait_ge(s_y, 16)


SCRATCH = {
    "u": ((BATCH, P, NBLK, SEQ), F32), "zs": ((BATCH, P, NBLK, SEQ), F32), "c": ((BATCH, STATE, SEQ), F32),
    "parts": ((2, BATCH, HEADS, PARTS + 2, DH, SEQ), BF16), "v": ((BATCH, GROUPS, P, KT, GH * VW), F32),
    "wt": ((EXP1, TOK), F32), "slots": ((NSLOT + TOPK * TOK, D), F32), "y": ((NSLOT + 1, D), F32),
}


def kernel(**inputs):
    import numpy as np
    import concourse.bacc as bacc
    from concourse.bass_utils import run_bass_kernel_spmd

    nc = bacc.Bacc("TRN2", target_bir_lowering=False, num_devices=1)
    arrays = {f"{k}_dram": v for k, v in {**lay_out(inputs), **shape_constants()}.items()}
    w = {k[:-5]: nc.dram_tensor(k, v.shape, mybir.dt.from_np(v.dtype), kind="ExternalInput").ap() for k, v in arrays.items()}
    scratch = {k: nc.dram_tensor(f"{k}_scratch", s, dt, kind="Internal").ap() for k, (s, dt) in SCRATCH.items()}
    yT = nc.dram_tensor("y_dram", (P, TOK), F32, kind="ExternalOutput").ap()
    program(nc, w, scratch, yT)
    got = run_bass_kernel_spmd(nc, [arrays], core_ids=[0]).results[0]["y_dram"]
    return np.ascontiguousarray(got.T).reshape(BATCH, SEQ, D)
```

```python
from contextlib import ExitStack

import concourse.bass as bass
from concourse import mybir

F32 = mybir.dt.float32
BF16 = mybir.dt.bfloat16
ALU = mybir.AluOpType
ACT = mybir.ActivationFunctionType
AX = mybir.AxisListType

P = 128
D = 128
BATCH, SEQ = 4, 1024
TOK = BATCH * SEQ
CH = 512
NCH = TOK // CH
CPB = SEQ // CH
NT = TOK // P
EPS = 1e-5
LN_AND_EXP = "natural_log_exp_and_others"

INNER = 256
NBLK = INNER // P
STATE = 16
RANK = 8
TAPS = 4
HALO = TAPS - 1


FIRST_CONSTANTS = ("ones_over_d", "ident")
SCAN_CONSTANTS = ("sel", "a_log", "d_skip", "out_proj")
LATER_CONSTANTS = ("gate_w", "gate_b", "prio", "before", "ones_bf16", "again", "slot_base", "spare", "same",
                   "first", "ones", "shared", "wqk", "wv", "ident_bf16", "mask_q", "mask_k", "wo",
                   "gate1_w", "gate1_b", "b1", "b2")


class Phase:

    def __init__(self, nc, name):
        self.nc, self.name, self.stack, self.sems = nc, name, ExitStack(), []

    def __enter__(self):
        return self

    def __exit__(self, *what):
        self.stack.close()
        if self.sems:
            self.nc.clear_and_free_semaphores(self.sems)
            self.nc.all_engine_barrier()

    def sb(self, name, shape, dt=F32):
        return self.stack.enter_context(self.nc.sbuf_tensor(f"{self.name}_{name}", shape, dt))

    def ps(self, name, shape, dt=F32):
        return self.stack.enter_context(self.nc.psum_tensor(f"{self.name}_{name}", shape, dt))

    def constants(self, w, names):
        return {n: self.sb(n, list(w[n].shape), w[n].dtype) for n in names}

    def sem(self, name):
        self.sems.append(self.nc.alloc_semaphore(f"{self.name}_{name}"))
        return self.sems[-1]

    def block(self):
        return self.nc.Block()


def waited(eng, passed):
    eng.sem_inc(passed, 1)


def mamba_prep(nc, xT, delta, du, bc_split, const, w, scratch):
    with Phase(nc, "prep") as ph:
        ones = const["ones_over_d"]
        w_in = ph.sb("w_in", [P, 2 * INNER])
        w_x = ph.sb("w_x", [P, NBLK, P])
        w_dt = ph.sb("w_dt", [P, NBLK * P])
        norm_w = ph.sb("norm_w", [P, 1])
        conv_w = ph.sb("conv_w", [P, NBLK, TAPS])
        conv_b = ph.sb("conv_b", [P, NBLK])
        dt_b = ph.sb("dt_b", [P, NBLK])
        eps = ph.sb("eps", [P, 1])
        eps2 = ph.sb("eps2", [P, 1])
        xc = ph.sb("xc", [P, 2, CH])
        sq = ph.sb("sq", [P, CH])
        lnv = ph.sb("lnv", [P, CH])
        rstd = ph.sb("rstd", [P, 2, CH])
        lnv2 = ph.sb("lnv2", [P, CH])
        rms = ph.sb("rms", [P, 2, CH])
        xn = ph.sb("xn", [P, CH])
        hT = ph.sb("hT", [P, CH])
        xi = ph.sb("xi", [P, 2, NBLK, HALO + CH])
        cacc = ph.sb("cacc", [P, NBLK, CH])
        u = ph.sb("u", [P, 2, NBLK, CH])
        zs = ph.sb("zs", [P, 2, NBLK, CH])
        hi = ph.sb("hi", [P, CH], BF16)
        rest = ph.sb("rest", [P, CH])
        mid = ph.sb("mid", [P, CH], BF16)
        crow = ph.sb("crow", [32, 2, CH])
        dtb = ph.sb("dtb", [P, CH])
        absd = ph.sb("absd", [P, NBLK, CH])
        expd = ph.sb("expd", [P, NBLK, CH])
        lnd = ph.sb("lnd", [P, NBLK, CH])
        maxd = ph.sb("maxd", [P, NBLK, CH])

        p_mean = ph.ps("p_mean", [P, CH])
        p_var = ph.ps("p_var", [P, CH])
        p_in = ph.ps("p_in", [P, 2 * NBLK, CH])
        p_x = p_mean
        p_dt = ph.ps("p_dt", [P, NBLK, CH])

        s_w = ph.sem("weights_loaded")
        s_x = [ph.sem(f"x_loaded{i}") for i in range(NCH)]
        s_const = ph.sem("constants_loaded")
        s_zero = ph.sem("zeroed")
        s_mean = ph.sem("mean_ready")
        s_xc = ph.sem("centred")
        s_sq = ph.sem("squared")
        s_var = ph.sem("var_ready")
        s_lnv = ph.sem("log_var")
        s_rstd = ph.sem("rstd_ready")
        s_rms = ph.sem("rms_ready")
        s_xn = ph.sem("normed")
        s_h = ph.sem("h_ready")
        s_in = ph.sem("in_proj_done")
        s_xi = ph.sem("xi_copied")
        s_halo = ph.sem("halo_ready")
        s_cstep = ph.sem("conv_step")
        s_u = ph.sem("u_ready")
        s_zs = ph.sem("z_silu_ready")
        s_xp = ph.sem("x_proj_done")
        s_crow = ph.sem("crow_ready")
        s_split = ph.sem("split_step")
        s_dtb = ph.sem("dt_rows_ready")
        s_dt = ph.sem("dt_proj_done")
        s_abs = ph.sem("abs_done")
        s_exp = ph.sem("exp_done")
        s_ln = ph.sem("log_done")
        s_maxd = ph.sem("max_done")
        s_delta = ph.sem("delta_ready")
        s_du = ph.sem("du_ready")
        s_res = ph.sem("residual_added")
        s_stu = [ph.sem(f"u_stored{i}") for i in range(2)]
        s_stz = [ph.sem(f"z_stored{i}") for i in range(2)]
        s_stc = [ph.sem(f"c_stored{i}") for i in range(2)]

        with ph.block() as block:

            @block.sync
            def _(sp):
                x_dram = w["x"]
                for dst, src in ((ones, w["ones_over_d"]), (w_in, w["in_proj"]), (norm_w, w["norm_w"]),
                                 (w_x, w["x_proj"]), (w_dt, w["dt_proj"]), (conv_w, w["conv_w"]),
                                 (conv_b, w["conv_b"]), (dt_b, w["dt_b"])):
                    sp.dma_start(dst[:], src).then_inc(s_w, 16)
                for g in range(NCH):
                    sp.dma_start(xT[:, g * CH:(g + 1) * CH], x_dram[:, g * CH:(g + 1) * CH]).then_inc(s_x[g], 16)
                for name in ("ident",) + SCAN_CONSTANTS:
                    sp.dma_start(const[name][:], w[name]).then_inc(s_const, 16)
                for g in range(NCH + 3):
                    for sem, chunk, stored, name, src in ((s_zs, g - 1, s_stz, "zs", zs), (s_u, g - 2, s_stu, "u", u)):
                        if 0 <= chunk < NCH:
                            half = chunk % CPB
                            sp.wait_ge(sem, chunk + 1)
                            sp.dma_start(scratch[name][chunk // CPB, :, :, half * CH:(half + 1) * CH],
                                         src[:, chunk % 2]).then_inc(stored[chunk % 2], 16)
                    if g >= 3:
                        chunk, half = g - 3, (g - 3) % CPB
                        sp.wait_ge(s_crow, chunk + 1)
                        sp.dma_start(scratch["c"][chunk // CPB, :, half * CH:(half + 1) * CH],
                                     crow[16:32, chunk % 2]).then_inc(s_stc[chunk % 2], 16)
                sp.wait_ge(s_const, 16 * (1 + len(SCAN_CONSTANTS)))
                for stored in s_stz + s_stu + s_stc:
                    sp.wait_ge(stored, 16 * (NCH // 2))

            @block.tensor
            def _(pe):
                pe.wait_ge(s_w, 16 * 8)
                pe.wait_ge(s_zero, 5)
                for g in range(NCH + 3):
                    a, f, b = g, g - 1, g - 3
                    if a < NCH:
                        pe.wait_ge(s_x[a], 16)
                        if b >= 1:
                            pe.wait_ge(s_split, 6 * b)
                        pe.matmul(p_mean[:], ones[:], xT[:, a * CH:(a + 1) * CH], start=True, stop=True).then_inc(s_mean, 1)
                    if 0 <= f < NCH:
                        pe.wait_ge(s_h, f + 1)
                        if f >= 1:
                            pe.wait_ge(s_xi, f)
                            pe.wait_ge(s_zs, f)
                        for n in range(2 * NBLK):
                            mm = pe.matmul(p_in[:, n], w_in[:, n * P:(n + 1) * P], hT[:], start=True, stop=True)
                        mm.then_inc(s_in, 1)
                    if a < NCH:
                        pe.wait_ge(s_sq, a + 1)
                        if a >= 1:
                            pe.wait_ge(s_lnv, 2 * a)
                        pe.matmul(p_var[:], ones[:], sq[:], start=True, stop=True).then_inc(s_var, 1)
                    if b >= 0:
                        pe.wait_ge(s_u, b + 1)
                        if a < NCH:
                            pe.wait_ge(s_xc, a + 1)
                        elif b >= 1:
                            pe.wait_ge(s_split, 6 * b)
                        for k in range(NBLK):
                            mm = pe.matmul(p_x[:], w_x[:, k], u[:, b % 2, k], start=(k == 0), stop=(k == NBLK - 1))
                        mm.then_inc(s_xp, 1)
                        pe.wait_ge(s_dtb, b + 1)
                        if b >= 1:
                            pe.wait_ge(s_abs, b)
                            pe.wait_ge(s_maxd, b)
                        for k in range(NBLK):
                            mm = pe.matmul(p_dt[:, k], w_dt[:, k * P:(k + 1) * P], dtb[:], start=True, stop=True)
                        mm.then_inc(s_dt, 1)

            @block.scalar
            def _(act):
                act.wait_ge(s_w, 16 * 8)
                act.wait_ge(s_zero, 5)
                for g in range(NCH + 3):
                    a, f, m, b = g, g - 1, g - 2, g - 3
                    act.preload_act_table_set(LN_AND_EXP)
                    if a < NCH:
                        act.wait_ge(s_xc, a + 1)
                        act.activation(sq[:], xc[:, a % 2], ACT.Square).then_inc(s_sq, 1)
                    if 0 <= f < NCH:
                        act.wait_ge(s_in, f + 1)
                        act.wait_ge(s_halo, f + 1)
                        if f >= 2:
                            act.wait_ge(s_cstep, 8 * (f - 1))
                        act.activation(xi[:, f % 2, :, HALO:], p_in[:, 0:NBLK], ACT.Copy).then_inc(s_xi, 1)
                    if a < NCH:
                        act.wait_ge(s_var, a + 1)
                        if a >= 1:
                            act.wait_ge(s_rms, a)
                        act.activation(lnv[:], p_var[:], ACT.Ln, bias=eps[:]).then_inc(s_lnv, 1)
                        act.activation(lnv2[:], p_var[:], ACT.Ln, bias=eps2[:], scale=1.0 + EPS).then_inc(s_lnv, 1)
                        if a >= 2:
                            act.wait_ge(s_h, a - 1)
                            act.wait_ge(s_xn, a - 1)
                        act.wait_ge(s_lnv, 2 * a + 2)
                        act.activation(rms[:, a % 2], lnv2[:], ACT.Exp, scale=-0.5).then_inc(s_rms, 1)
                        act.activation(rstd[:, a % 2], lnv[:], ACT.Exp, scale=-0.5).then_inc(s_rstd, 1)
                    if b >= 0:
                        act.wait_ge(s_xp, b + 1)
                        if b >= 1:
                            act.wait_ge(s_dt, b)
                        act.activation(dtb[96:96 + RANK], p_x[96:96 + RANK], ACT.Copy).then_inc(s_dtb, 1)
                        if b >= 2:
                            act.wait_ge(s_stc[b % 2], 16 * (b // 2))
                        act.activation(crow[:, b % 2], p_x[0:32], ACT.Copy).then_inc(s_crow, 1)
                        act.wait_ge(s_dt, b + 1)
                        if b >= 1:
                            act.wait_ge(s_exp, b)
                        for k in range(NBLK):
                            ins = act.activation(absd[:, k], p_dt[:, k], ACT.Abs, bias=dt_b[:, k:k + 1])
                        ins.then_inc(s_abs, 1)
                        act.wait_ge(s_abs, b + 1)
                        if b >= 1:
                            act.wait_ge(s_ln, b)
                        act.activation(expd[:], absd[:], ACT.Exp, scale=-1.0).then_inc(s_exp, 1)
                        act.wait_ge(s_exp, b + 1)
                        if b >= 1:
                            act.wait_ge(s_delta, b)
                        act.activation(lnd[:], expd[:], ACT.Ln, bias=1.0).then_inc(s_ln, 1)
                    if 0 <= f < NCH:
                        if f >= 2:
                            act.wait_ge(s_stz[f % 2], 16 * (f // 2))
                        act.activation(zs[:, f % 2], p_in[:, NBLK:], ACT.Silu).then_inc(s_zs, 1)
                    if 0 <= m < NCH:
                        act.wait_ge(s_cstep, 8 * m + 8)
                        if m >= 2:
                            act.wait_ge(s_stu[m % 2], 16 * (m // 2))
                            act.wait_ge(s_du, m - 1)
                            act.wait_ge(s_xp, m - 1)
                        act.activation(u[:, m % 2], cacc[:], ACT.Silu).then_inc(s_u, 1)

            @block.vector
            def _(dve):
                dve.memset(dtb[:], 0.0).then_inc(s_zero, 1)
                dve.memset(bc_split[:].bitcast(mybir.dt.uint32), 0).then_inc(s_zero, 1)
                dve.memset(xi[:], 0.0).then_inc(s_zero, 1)
                dve.memset(eps[:], EPS).then_inc(s_zero, 1)
                dve.memset(eps2[:], EPS * EPS).then_inc(s_zero, 1)
                dve.wait_ge(s_w, 16 * 8)
                dve.wait_ge(s_zero, 5)
                for g in range(NCH + 3):
                    a, f, m, b = g, g - 1, g - 2, g - 3
                    if 0 <= f < NCH:
                        dve.wait_ge(s_rms, f + 1)
                        if f >= 1:
                            dve.wait_ge(s_in, f)
                        dve.scalar_tensor_tensor(hT[:], xc[:, f % 2], norm_w[:], rms[:, f % 2], ALU.mult, ALU.mult).then_inc(s_h, 1)
                    if a < NCH:
                        dve.wait_ge(s_mean, a + 1)
                        if a >= 2:
                            dve.wait_ge(s_xn, a - 1)
                        dve.tensor_tensor(xc[:, a % 2], xT[:, a * CH:(a + 1) * CH], p_mean[:], ALU.subtract).then_inc(s_xc, 1)
                    if 0 <= f < NCH:
                        dve.wait_ge(s_rstd, f + 1)
                        if f >= 1:
                            dve.wait_ge(s_res, f)
                        dve.tensor_tensor(xn[:], xc[:, f % 2], rstd[:, f % 2], ALU.mult).then_inc(s_xn, 1)
                        if f >= 2:
                            dve.wait_ge(s_cstep, 8 * (f - 1))
                        if f % CPB == 0:
                            dve.memset(xi[:, f % 2, :, 0:HALO], 0.0).then_inc(s_halo, 1)
                        else:
                            dve.wait_ge(s_xi, f)
                            dve.tensor_copy(xi[:, f % 2, :, 0:HALO], xi[:, (f + 1) % 2, :, CH:CH + HALO]).then_inc(s_halo, 1)
                    if 0 <= m < NCH:
                        dve.wait_ge(s_xi, m + 1)
                        dve.wait_ge(s_halo, m + 1)
                        if m >= 1:
                            dve.wait_ge(s_u, m)
                        for k in range(NBLK):
                            dve.tensor_scalar(cacc[:, k], xi[:, m % 2, k, HALO:], conv_w[:, k, HALO:TAPS],
                                              conv_b[:, k:k + 1], ALU.mult, ALU.add).then_inc(s_cstep, 1)
                        for j in range(HALO):
                            for k in range(NBLK):
                                dve.wait_ge(s_cstep, 8 * m + 2 * j + k + 1)
                                dve.scalar_tensor_tensor(cacc[:, k], xi[:, m % 2, k, j:j + CH], conv_w[:, k, j:j + 1],
                                                         cacc[:, k], ALU.mult, ALU.add).then_inc(s_cstep, 1)
                    if b >= 0:
                        tok = slice(b * CH, (b + 1) * CH)
                        dve.wait_ge(s_crow, b + 1)
                        dve.tensor_copy(hi[0:96], p_x[0:96]).then_inc(s_split, 1)
                        dve.wait_ge(s_split, 6 * b + 1)
                        dve.tensor_tensor(rest[0:96], p_x[0:96], hi[0:96], ALU.subtract).then_inc(s_split, 1)
                        dve.tensor_copy(bc_split[0:32, tok], hi[0:32]).then_inc(s_split, 1)
                        dve.wait_ge(s_split, 6 * b + 2)
                        dve.tensor_copy(mid[0:96], rest[0:96]).then_inc(s_split, 1)
                        dve.wait_ge(s_split, 6 * b + 4)
                        dve.tensor_copy(bc_split[32:64, tok], mid[32:64]).then_inc(s_split, 1)
                        dve.tensor_tensor(bc_split[64:96, tok], rest[64:96], mid[64:96], ALU.subtract).then_inc(s_split, 1)
                        seq, half = b // CPB, b % CPB
                        dve.wait_ge(s_abs, b + 1)
                        if b >= 1:
                            dve.wait_ge(s_delta, b)
                        for k in range(NBLK):
                            ins = dve.tensor_scalar(maxd[:, k], p_dt[:, k], dt_b[:, k:k + 1], 0.0, ALU.add, ALU.max)
                        ins.then_inc(s_maxd, 1)
                        dve.wait_ge(s_ln, b + 1)
                        dve.wait_ge(s_maxd, b + 1)
                        dve.tensor_tensor(delta[:, seq, :, half * CH:(half + 1) * CH], maxd[:], lnd[:], ALU.add).then_inc(s_delta, 1)

            @block.gpsimd
            def _(pool):
                for g in range(1, NCH + 3):
                    if g - 1 < NCH:
                        tok = slice((g - 1) * CH, g * CH)
                        pool.wait_ge(s_xn, g)
                        pool.tensor_tensor(xT[:, tok], xT[:, tok], xn[:], ALU.add).then_inc(s_res, 1)
                    if g >= 3:
                        b = g - 3
                        seq, seg = b // CPB, slice(b % CPB * CH, (b % CPB + 1) * CH)
                        pool.wait_ge(s_delta, b + 1)
                        pool.wait_ge(s_u, b + 1)
                        pool.tensor_tensor(du[:, seq, :, seg], delta[:, seq, :, seg], u[:, b % 2], ALU.mult).then_inc(s_du, 1)


def mamba_scan(nc, xT, delta, du, bc_split, const, scratch):
    NIT = NBLK * STATE
    SLOTS = 3
    OUT = SLOTS - 1
    with Phase(nc, "scan") as ph:
        ident = const["ident"]
        sel = const["sel"]
        a_log = const["a_log"]
        a_exp = ph.sb("a_exp", [P, NBLK, STATE])
        a_neg = ph.sb("a_neg", [P, NBLK, STATE])
        d_skip = const["d_skip"]
        w_out = const["out_proj"]
        c_bc = ph.sb("c_bc", [P, STATE, SEQ])
        decay = ph.sb("decay", [P, 2, SEQ])
        h = ph.sb("h", [P, SLOTS, SEQ])
        hc = ph.sb("hc", [P, SLOTS, SEQ])
        u = ph.sb("u", [P, NBLK, SEQ])
        zs = ph.sb("zs", [P, NBLK, SEQ])
        y1 = u
        p_b = ph.ps("p_b", [P, SLOTS, SEQ])
        p_y = ph.ps("p_y", [P, SEQ])

        s_a = ph.sem("a_ready")
        s_c = [ph.sem(f"c_loaded{i}") for i in range(STATE)]
        s_uz = ph.sem("u_zs_loaded")
        s_b = ph.sem("b_broadcast")
        s_dec = ph.sem("decay_ready")
        s_dbu = ph.sem("dbu_ready")
        s_scan = ph.sem("scan_done")
        s_hc = ph.sem("hc_ready")
        s_acc = ph.sem("hc_summed")
        s_y1 = ph.sem("y_read")
        s_y = ph.sem("y_gated")
        s_o = ph.sem("out_proj_done")
        s_x = ph.sem("residual_added")
        hold = ph.sem("wait_passed")

        with ph.block() as block:

            @block.sync
            def _(sp):
                for b in range(BATCH):
                    for s in range(STATE):
                        if b:
                            sp.wait_ge(s_hc, (b - 1) * NIT + STATE + s + 1)
                        sp.dma_start(c_bc[:, s], scratch["c"][b, s:s + 1, :].to_broadcast([P, SEQ])).then_inc(s_c[s], 16)
                    if b:
                        sp.wait_ge(s_o, b)
                    sp.dma_start(u[:], scratch["u"][b]).then_inc(s_uz, 16)
                    sp.dma_start(zs[:], scratch["zs"][b]).then_inc(s_uz, 16)

            def later(b):
                return not isinstance(b, int)

            def accumulate(pe, b, i):
                blk, s = i // STATE, i % STATE
                if s == 0 and (i or later(b)):
                    pe.wait_ge(s_y1, NBLK * b + blk)
                pe.wait_ge(s_hc, b * NIT + i + 1)
                for c in range(CPB):
                    mm = pe.matmul(p_y[:, c * CH:(c + 1) * CH], ident[:], hc[:, i % SLOTS, c * CH:(c + 1) * CH],
                                   start=(s == 0), stop=(s == STATE - 1))
                mm.then_inc(s_acc, 1)

            def freed(i):
                if i >= SLOTS:
                    return i - SLOTS + 1
                return max(k for k in range(NIT) if k % SLOTS == i) + 1 - NIT

            @block.tensor
            def _(pe):
                def broadcast(b, i):
                    if later(b) and i == OUT:
                        pe.wait_ge(s_x, b)
                    elif later(b) or i >= SLOTS:
                        pe.wait_ge(s_scan, b * NIT + freed(i))
                    for c in range(CPB):
                        mm = pe.matmul(p_b[:, i % SLOTS, c * CH:(c + 1) * CH], sel[:, i % STATE],
                                       bc_split[:, bass.ds(b * SEQ + c * CH, CH)], start=True, stop=True)
                    mm.then_inc(s_b, 1)

                def project(b):
                    for k in range(NBLK):
                        pe.wait_ge(s_y, b * NBLK + k + 1)
                        for c in range(CPB):
                            mm = pe.matmul(p_b[:, OUT, c * CH:(c + 1) * CH], w_out[:, k], y1[:, k, c * CH:(c + 1) * CH],
                                           start=(k == 0), stop=(k == NBLK - 1))
                    mm.then_inc(s_o, 1)

                def sequence(b):
                    broadcast(b, 0)
                    if later(b):
                        accumulate(pe, b - 1, NIT - 2)
                    broadcast(b, 1)
                    if later(b):
                        accumulate(pe, b - 1, NIT - 1)
                        project(b - 1)
                    for i in range(2, NIT):
                        broadcast(b, i)
                        if i >= SLOTS:
                            accumulate(pe, b, i - SLOTS)
                    accumulate(pe, b, NIT - SLOTS)

                sequence(0)
                with pe.Fori(1, BATCH) as b:
                    sequence(b)
                accumulate(pe, BATCH - 1, NIT - 2)
                accumulate(pe, BATCH - 1, NIT - 1)
                project(BATCH - 1)

            @block.scalar
            def _(act):
                def sequence(b):
                    for i in range(NIT):
                        blk, s = i // STATE, i % STATE
                        if i >= 2 or later(b):
                            act.wait_ge(s_scan, b * NIT + i - 1)
                        if later(b):
                            waited(act, hold)
                        act.activation(decay[:, i % 2], delta[:, bass.ds(b, 1), blk, :].rearrange("p o t -> p (o t)"), ACT.Exp,
                                       scale=a_neg[:, blk, s:s + 1]).then_inc(s_dec, 1)

                act.activation(a_exp[:], a_log[:], ACT.Exp).then_inc(s_a, 1)
                act.wait_ge(s_a, 1)
                act.mul(a_neg[:], a_exp[:], -1.0).then_inc(s_a, 1)
                act.wait_ge(s_a, 2)
                sequence(0)
                with act.Fori(1, BATCH) as b:
                    sequence(b)

            @block.vector
            def _(dve):
                def skip(b, blk):
                    dve.wait_ge(s_acc, b * NIT + (blk + 1) * STATE)
                    dve.wait_ge(s_uz, (b + 1) * 32)
                    dve.scalar_tensor_tensor(y1[:, blk], u[:, blk], d_skip[:, blk:blk + 1], p_y[:], ALU.mult, ALU.add).then_inc(s_y1, 1)

                def gate(b, blk):
                    dve.wait_ge(s_y1, b * NBLK + blk + 1)
                    dve.tensor_tensor(y1[:, blk], y1[:, blk], zs[:, blk], ALU.mult).then_inc(s_y, 1)

                def add(b):
                    dve.wait_ge(s_o, b + 1)
                    xt = xT[:, bass.ds(b * SEQ, SEQ)]
                    dve.tensor_tensor(xt, xt, p_b[:, OUT], ALU.add).then_inc(s_x, 1)

                def times_b(b, i):
                    dve.wait_ge(s_b, b * NIT + i + 1)
                    dve.tensor_tensor(p_b[:, i % SLOTS], du[:, bass.ds(b, 1), i // STATE, :].rearrange("p o t -> p (o t)"),
                                      p_b[:, i % SLOTS], ALU.mult).then_inc(s_dbu, 1)

                def scan(b, i):
                    dve.wait_ge(s_dec, b * NIT + i + 1)
                    dve.wait_ge(s_dbu, b * NIT + i + 1)
                    if i >= SLOTS or later(b):
                        dve.wait_ge(s_hc, b * NIT + freed(i))
                    dve.tensor_tensor_scan(h[:, i % SLOTS], decay[:, i % 2], p_b[:, i % SLOTS], 0.0,
                                           ALU.mult, ALU.add).then_inc(s_scan, 1)

                def sequence(b):
                    times_b(b, 0)
                    times_b(b, 1)
                    scan(b, 0)
                    if later(b):
                        skip(b - 1, 1)
                        gate(b - 1, 1)
                    scan(b, 1)
                    if later(b):
                        add(b - 1)
                    times_b(b, 2)
                    for i in range(2, NIT):
                        if i + 1 < NIT:
                            times_b(b, i + 1)
                        scan(b, i)
                        if i == STATE + SLOTS - 2:
                            skip(b, 0)
                        if i == STATE + SLOTS:
                            gate(b, 0)

                sequence(0)
                with dve.Fori(1, BATCH) as b:
                    sequence(b)
                skip(BATCH - 1, 1)
                gate(BATCH - 1, 1)
                add(BATCH - 1)

            @block.gpsimd
            def _(pool):
                def sequence(b):
                    for i in range(NIT):
                        s = i % STATE
                        pool.wait_ge(s_scan, b * NIT + i + 1)
                        pool.wait_ge(s_c[s], b * 16 + 16)
                        if i >= SLOTS or later(b):
                            pool.wait_ge(s_acc, b * NIT + freed(i))
                        pool.tensor_tensor(hc[:, i % SLOTS], h[:, i % SLOTS], c_bc[:, s], ALU.mult).then_inc(s_hc, 1)

                sequence(0)
                with pool.Fori(1, BATCH) as b:
                    sequence(b)


EXP0, HID0, SHARED = 16, 256, 2
SLOTS0 = EXP0 + SHARED
TOPK = 2
CAP = -(-TOK * TOPK * 5 // (EXP0 * 4))
NSLOT = EXP0 * CAP
OCT = 8
ZROWS = 8
FILL = -2.0 ** 127


class Norm:

    def __init__(self, ph, xT, lnT, const, p_mean, p_var):
        self.xT, self.lnT, self.ones = xT, lnT, const["ones_over_d"]
        self.p_mean, self.p_var = p_mean, p_var
        self.eps = ph.sb("eps", [P, 1])
        self.sq = ph.sb("sq", [P, 2, CH])
        self.lnv = ph.sb("lnv", [P, NCH, CH])
        self.rstd = ph.sb("rstd", [P, NCH, CH])
        self.s_eps = ph.sem("eps_set")
        self.s_mean = ph.sem("mean_ready")
        self.s_xc = ph.sem("centred")
        self.s_sq = ph.sem("squared")
        self.s_var = ph.sem("var_ready")
        self.s_lnv = ph.sem("log_var")
        self.s_rstd = ph.sem("rstd_ready")
        self.s_xn = ph.sem("normed")

    def set_eps(self, dve):
        dve.memset(self.eps[:], EPS).then_inc(self.s_eps, 1)

    def mean(self, pe, g):
        if g >= 2:
            pe.wait_ge(self.s_xc, g - 1)
        pe.matmul(self.p_mean[:, g % 2], self.ones[:], self.xT[:, g * CH:(g + 1) * CH], start=True, stop=True).then_inc(self.s_mean, 1)

    def centre(self, dve, g):
        tok = slice(g * CH, (g + 1) * CH)
        dve.wait_ge(self.s_mean, g + 1)
        dve.tensor_tensor(self.lnT[:, tok], self.xT[:, tok], self.p_mean[:, g % 2], ALU.subtract).then_inc(self.s_xc, 1)

    def square(self, act, g):
        act.wait_ge(self.s_xc, g + 1)
        if g >= 2:
            act.wait_ge(self.s_var, g - 1)
        act.activation(self.sq[:, g % 2], self.lnT[:, g * CH:(g + 1) * CH], ACT.Square).then_inc(self.s_sq, 1)

    def variance(self, pe, g):
        pe.wait_ge(self.s_sq, g + 1)
        if g >= 2:
            pe.wait_ge(self.s_lnv, g - 1)
        pe.matmul(self.p_var[:, g % 2], self.ones[:], self.sq[:, g % 2], start=True, stop=True).then_inc(self.s_var, 1)

    def log(self, act, g):
        if g == 0:
            act.wait_ge(self.s_eps, 1)
        act.wait_ge(self.s_var, g + 1)
        act.activation(self.lnv[:, g], self.p_var[:, g % 2], ACT.Ln, bias=self.eps[:]).then_inc(self.s_lnv, 1)

    def exp(self, act, g):
        act.wait_ge(self.s_lnv, g + 1)
        act.activation(self.rstd[:, g], self.lnv[:, g], ACT.Exp, scale=-0.5).then_inc(self.s_rstd, 1)

    def scale(self, dve, g):
        tok = slice(g * CH, (g + 1) * CH)
        dve.wait_ge(self.s_rstd, g + 1)
        dve.wait_ge(self.s_sq, g + 1)
        dve.tensor_tensor(self.lnT[:, tok], self.lnT[:, tok], self.rstd[:, g], ALU.mult).then_inc(self.s_xn, 1)


def layer_norm(nc, xT, lnT, const, w):
    with Phase(nc, "norm") as ph:
        p_mean = ph.ps("p_mean", [P, 2, CH])
        p_var = ph.ps("p_var", [P, 2, CH])
        norm = Norm(ph, xT, lnT, const, p_mean, p_var)
        s_const = ph.sem("constants_loaded")

        with ph.block() as block:
            @block.sync
            def _(sp):
                for n in LATER_CONSTANTS:
                    sp.dma_start(const[n][:], w[n]).then_inc(s_const, 16)
                sp.wait_ge(s_const, 16 * len(LATER_CONSTANTS))

            @block.tensor
            def _(pe):
                for g in range(NCH + 1):
                    if g < NCH:
                        norm.mean(pe, g)
                    if g:
                        norm.variance(pe, g - 1)

            @block.scalar
            def _(act):
                for g in range(NCH + 1):
                    if g < NCH:
                        norm.square(act, g)
                    if g:
                        norm.log(act, g - 1)
                for g in range(NCH):
                    norm.exp(act, g)

            @block.vector
            def _(dve):
                norm.set_eps(dve)
                for g in range(NCH):
                    norm.centre(dve, g)
                for g in range(NCH):
                    norm.scale(dve, g)


def router0(nc, lnT, rows, weight, put, get, const, scratch):
    E, T = EXP0, NT
    U32 = mybir.dt.uint32
    with Phase(nc, "router") as ph:
        gate_w = const["gate_w"]
        gate_b = const["gate_b"]
        prio = const["prio"]
        before = const["before"]
        ones = const["ones_bf16"]
        again = const["again"]
        score = ph.sb("score", [P, T, E])
        tmp = ph.sb("tmp", [P, T, E])
        best = ph.sb("best", [P, T])
        norm = ph.sb("norm", [P, T])
        oh = ph.sb("oh", [P, 2, T, E])
        logit = ph.sb("logit", [P, T, E])
        asg = ph.sb("asg", [P, E, T])
        wk = ph.sb("wk", [P, E, T])
        grouped = ph.sb("grouped", [P, T // OCT, E * OCT])
        wkt = ph.sb("wkt", [P, T // OCT, P])
        same = const["same"]
        first = const["first"]
        onesf = const["ones"]
        bits = ph.sb("bits", [P, 1], U32)
        cand = ph.sb("cand", [P, 1], U32)
        flip = ph.sb("flip", [P, 1], U32)
        found = ph.sb("found", [P, 1], U32)
        add = ph.sb("add", [P, 1], U32)
        reach = ph.sb("reach", [P, T // OCT, P], BF16)
        part = ph.sb("part", [P, 1])
        spread = ph.sb("spread", [P, E])
        limit = ph.sb("limit", [P, E])
        cnt = ph.sb("cnt", [P, E])
        need = ph.sb("need", [P, E])
        gt = ph.sb("gt", [P, E, T], BF16)
        eq = ph.sb("eq", [P, E, T], BF16)
        tot = ph.sb("tot", [P, E, T])
        cum = ph.sb("cum", [P, E, T])
        pre = ph.sb("pre", [P, E, T])
        keep = ph.sb("keep", [P, E, T])
        base = const["slot_base"]
        spare = const["spare"]
        zeros = ph.sb("zeros", [P, ZROWS, D])
        keepb = ph.sb("keepb", [P, E, T], BF16)
        mine = ph.sb("mine", [P, E, T])
        kept = ph.sb("kept", [P, T])
        slot = ph.sb("slot", [P, T])
        off = ph.sb("off", [P, T])
        p_x = ph.ps("p_x", [P, 2, CH // P, D])
        ident = const["ident"]
        p_lg = ph.ps("p_lg", [P, T, E])
        p_cnt = ph.ps("p_cnt", [P, E, T])
        p_pre = ph.ps("p_pre", [P, E, T])
        p_wk = ph.ps("p_wk", [P, T // OCT, P])
        p_n = ph.ps("p_n", [P, E])
        s_lg = ph.sem("logits_ready")
        s_v = ph.sem("vector_step")
        s_mask = ph.sem("mask_ready")
        s_cnt = ph.sem("count_ready")
        s_grp = ph.sem("weights_grouped")
        s_wk = ph.sem("weights_turned")
        s_lim = ph.sem("limit_step")
        s_found = ph.sem("bit_found")
        s_exp = ph.sem("exp_done")
        s_zero = ph.sem("zeros_set")
        s_fill = ph.sem("slots_zeroed")
        s_turn = ph.sem("tokens_turned")
        s_row = ph.sem("rows_copied")

        with ph.block() as block:
            @block.sync
            def _(sp):
                sp.wait_ge(s_zero, 1)
                for n in range(NSLOT // (P * ZROWS)):
                    sp.dma_start(scratch["slots"][n * P * ZROWS:(n + 1) * P * ZROWS].rearrange("(p r) d -> p r d", r=ZROWS),
                                 zeros[:]).then_inc(s_fill, 16)
                sp.dma_start(scratch["y"][NSLOT:NSLOT + 1], zeros[0:1, 0]).then_inc(s_fill, 16)
                sp.wait_ge(s_fill, 16 * (NSLOT // (P * ZROWS) + 1))

            @block.tensor
            def _(pe):
                for t in range(T):
                    mm = pe.matmul(p_lg[:, t], lnT[:, t * P:(t + 1) * P], gate_w[:], start=True, stop=True)
                mm.then_inc(s_lg, 1)
                for c in range(NCH):
                    if c >= 2:
                        pe.wait_ge(s_row, c - 1)
                    for t in range(CH // P):
                        mm = pe.transpose(p_x[:, c % 2, t], lnT[:, c * CH + t * P:c * CH + (t + 1) * P], ident[:])
                    mm.then_inc(s_turn, 1)
                pe.wait_ge(s_grp, 1)
                for n in range(T // OCT):
                    mm = pe.transpose(p_wk[:, n], grouped[:, n], ident[:])
                mm.then_inc(s_wk, 1)
                with pe.Fori(1, 33) as n:
                    pe.wait_ge(s_mask, n)
                    pe.matmul(p_n[:, 0:1], same[:], part[:], start=True, stop=True).then_inc(s_cnt, 1)
                pe.wait_ge(s_lim, 1)
                pe.matmul(p_n[:], onesf[:], spread[:], start=True, stop=True).then_inc(s_lim, 1)
                pe.wait_ge(s_mask, 33)
                pe.matmul(p_cnt[:], ones[:], gt[:], start=True, stop=True).then_inc(s_cnt, 1)
                pe.wait_ge(s_mask, 34)
                pe.matmul(p_pre[:], before[:], eq[:], start=True, stop=True)
                pe.matmul(p_cnt[:], ones[:], eq[:], start=True, stop=True).then_inc(s_cnt, 1)
                pe.wait_ge(s_mask, 35)
                pe.matmul(p_pre[:], before[:], keepb[:], start=True, stop=True)
                pe.matmul(p_cnt[:], ones[:], keepb[:], start=True, stop=True).then_inc(s_cnt, 1)

            @block.scalar
            def _(act):
                act.wait_ge(s_v, 3)
                act.activation(tmp[:], score[:], ACT.Exp).then_inc(s_exp, 1)
                for c in range(NCH):
                    act.wait_ge(s_turn, c + 1)
                    act.activation(rows[:, c * (CH // P):(c + 1) * (CH // P)], p_x[:, c % 2], ACT.Copy).then_inc(s_row, 1)

            @block.vector
            def _(dve):
                count = [0]

                def step(ins):
                    count[0] += 1
                    ins.then_inc(s_v, 1)
                    dve.wait_ge(s_v, count[0])

                dve.memset(zeros[:], 0.0).then_inc(s_zero, 1)
                dve.wait_ge(s_lg, 1)
                step(dve.tensor_copy(logit[:], p_lg[:]))
                step(dve.tensor_reduce(best[:], logit[:], AX.X, ALU.max))
                over = best[:].rearrange("p (t o) -> p t o", o=1).to_broadcast([P, T, E])
                step(dve.tensor_tensor(score[:], logit[:], over, ALU.subtract))
                dve.wait_ge(s_exp, 1)
                step(dve.tensor_reduce(norm[:], tmp[:], AX.X, ALU.add))
                step(dve.reciprocal(norm[:], norm[:]))
                step(dve.tensor_tensor(score[:], tmp[:], norm[:].rearrange("p (t o) -> p t o", o=1).to_broadcast([P, T, E]), ALU.mult))
                bias = gate_b[:].rearrange("p (o e) -> p o e", o=1).to_broadcast([P, T, E])
                order = prio[:].rearrange("p (o e) -> p o e", o=1).to_broadcast([P, T, E])
                step(dve.tensor_tensor(score[:], score[:], bias, ALU.add))
                for k in range(TOPK):
                    step(dve.tensor_reduce(best[:], score[:], AX.X, ALU.max))
                    step(dve.tensor_tensor(tmp[:], score[:], over, ALU.is_ge))
                    step(dve.tensor_tensor(tmp[:], tmp[:], order, ALU.mult))
                    step(dve.tensor_reduce(best[:], tmp[:], AX.X, ALU.max))
                    step(dve.tensor_tensor(oh[:, k], over, order, ALU.is_equal))
                    if k == 0:
                        step(dve.scalar_tensor_tensor(score[:], oh[:, k], FILL, score[:], ALU.mult, ALU.add))
                by_expert = lambda a: a.rearrange("p t e -> p e t")
                step(dve.tensor_tensor(asg[:], by_expert(oh[:, 0]), by_expert(oh[:, 1]), ALU.add))
                step(dve.tensor_scalar(wk[:], asg[:], -1.0, -FILL, ALU.add, ALU.mult))
                step(dve.tensor_tensor(tot[:], asg[:], by_expert(logit[:]), ALU.mult))
                step(dve.tensor_tensor(wk[:], wk[:], tot[:], ALU.add))
                dve.tensor_copy(grouped[:].rearrange("p n (e t) -> p n e t", e=E),
                                wk[:].rearrange("p e (n t) -> p n e t", t=OCT)).then_inc(s_grp, 1)
                dve.wait_ge(s_wk, 1)
                step(dve.tensor_copy(wkt[:], p_wk[:]))

                def count_reaching(n):
                    dve.tensor_scalar(reach[:], wkt[:], cand[:].bitcast(F32), 0.0, ALU.is_ge, ALU.add, accum_out=part[:]).then_inc(s_mask, 1)
                    dve.wait_ge(s_cnt, n + 1)

                step(dve.memset(cand[:], 0))
                count_reaching(0)
                step(dve.tensor_scalar(bits[:], p_n[:, 0:1], CAP - 0.5, float(2 ** 31), ALU.is_ge, ALU.mult))
                step(dve.tensor_scalar(flip[:].bitcast(mybir.dt.int32), bits[:].bitcast(mybir.dt.int32), 31, None, ALU.arith_shift_right))
                step(dve.tensor_scalar(flip[:], flip[:], 0xFFFFFFFF, 0x80000000, ALU.bitwise_xor, ALU.bitwise_or))
                step(dve.tensor_tensor(found[:], bits[:], flip[:], ALU.bitwise_xor))
                step(dve.tensor_scalar(cand[:], found[:], 1 << 30, None, ALU.bitwise_xor))
                for n in range(1, 32):
                    count_reaching(n)
                    step(dve.tensor_scalar(add[:], p_n[:, 0:1], CAP - 0.5, float(1 << (31 - n)), ALU.is_ge, ALU.mult))
                    if n < 31:
                        step(dve.scalar_tensor_tensor(cand[:], add[:], 1 << (30 - n), found[:], ALU.bitwise_or, ALU.bitwise_xor))
                    dve.tensor_tensor(found[:], found[:], add[:], ALU.bitwise_xor).then_inc(s_found, 1)
                dve.wait_ge(s_found, 31)
                dve.tensor_scalar(spread[:], first[:], found[:].bitcast(F32), None, ALU.mult).then_inc(s_lim, 1)
                dve.wait_ge(s_lim, 2)
                step(dve.tensor_copy(limit[:], p_n[:]))
                thr = limit[:].rearrange("p (e o) -> p e o", o=1).to_broadcast([P, E, T])
                dve.tensor_tensor(gt[:], wk[:], thr, ALU.is_gt).then_inc(s_mask, 1)
                step(dve.tensor_tensor(pre[:], wk[:], thr, ALU.is_equal))
                dve.wait_ge(s_cnt, 33)
                step(dve.tensor_reduce(cnt[:], p_cnt[:], AX.X, ALU.add))
                dve.tensor_tensor(eq[:], pre[:], asg[:], ALU.mult).then_inc(s_mask, 1)
                step(dve.tensor_scalar(need[:], cnt[:], -1.0, float(CAP), ALU.mult, ALU.add))

                def earlier():
                    step(dve.tensor_copy(tot[:], p_cnt[:]))
                    step(dve.tensor_tensor_scan(cum[:].rearrange("p e t -> p (e t)"), again[:].rearrange("p e t -> p (e t)"),
                                                tot[:].rearrange("p e t -> p (e t)"), 0.0, ALU.mult, ALU.add))
                    step(dve.tensor_tensor(cum[:], cum[:], tot[:], ALU.subtract))
                    step(dve.tensor_tensor(pre[:], cum[:], p_pre[:], ALU.add))

                over_e = lambda a: a.rearrange("p (e o) -> p e o", o=1).to_broadcast([P, E, T])
                dve.wait_ge(s_cnt, 34)
                earlier()
                step(dve.tensor_tensor(keep[:], pre[:], over_e(need[:]), ALU.is_lt))
                step(dve.tensor_tensor(keep[:], keep[:], eq[:], ALU.mult))
                step(dve.tensor_tensor(keep[:], keep[:], gt[:], ALU.add))
                dve.tensor_copy(keepb[:], keep[:]).then_inc(s_mask, 1)
                dve.wait_ge(s_cnt, 35)
                earlier()
                step(dve.tensor_tensor(pre[:], pre[:], over_e(base[:]), ALU.add))
                for k in range(TOPK):
                    step(dve.tensor_tensor(mine[:], by_expert(oh[:, k]), keep[:], ALU.mult))
                    step(dve.tensor_reduce(kept[:], by_expert(mine[:]), AX.X, ALU.add))
                    step(dve.tensor_tensor(tot[:], mine[:], pre[:], ALU.mult))
                    step(dve.tensor_reduce(slot[:], by_expert(tot[:]), AX.X, ALU.add))
                    step(dve.tensor_tensor(tot[:], mine[:], by_expert(logit[:]), ALU.mult))
                    step(dve.tensor_reduce(weight[:, k], by_expert(tot[:]), AX.X, ALU.add))
                    step(dve.tensor_scalar(off[:], kept[:], -float(NSLOT), float(NSLOT), ALU.mult, ALU.add))
                    step(dve.tensor_tensor(get[:, k], slot[:], off[:], ALU.add))
                    step(dve.tensor_scalar(kept[:], kept[:], -1.0, 1.0, ALU.mult, ALU.add))
                    step(dve.tensor_tensor(off[:], kept[:], spare[:, k], ALU.mult))
                    step(dve.tensor_tensor(put[:, k], slot[:], off[:], ALU.add))


def experts0(nc, xT, lnT, rows, weight, put, get, const, w, scratch):
    M = HID0 // P
    SM = SHARED * M
    TILES = (3, 2)
    FIRST = (0, 3)
    U = 2 * EXP0
    EARLY = 6
    with Phase(nc, "experts") as ph:
        ident = const["ident"]
        ws = const["shared"]
        wts = ph.sb("wts", [P, 2, 3 * HID0])
        xr = ph.sb("xr", [P, 2, CAP // P, D])
        wh = ph.sb("wh", [P, 2, 2 * HID0], mybir.dt.float32r)
        wl = ph.sb("wl", [P, 2, 2 * HID0], mybir.dt.float32r)
        xh = ph.sb("xh", [P, 2, CH], mybir.dt.float32r)
        xl = ph.sb("xl", [P, 2, CH], mybir.dt.float32r)
        gated = ph.sb("gated", [P, M, CH])
        g = ph.sb("g", [P, 2, M, CH])
        sg = ph.sb("sg", [P, 2, SM, CH])
        yr = ph.sb("yr", [P, 2, CH // P, D])
        mine = ph.sb("mine", [P, TOPK, NT, D])
        second = ph.sb("second", [P, NT, D])
        p_h = ph.ps("p_h", [P, M, 2, CH])
        p_y = ph.ps("p_y", [P, 2, CH // P, D])
        p_t = ph.ps("p_t", [P, 2, CH // P, D])
        s_put = ph.sem("rows_scattered")
        s_xr = [ph.sem(f"slots_loaded{i}") for i in range(2)]
        s_w = [ph.sem(f"weights_loaded{i}") for i in range(2)]
        s_wd = [ph.sem(f"down_weights_loaded{i}") for i in range(2)]
        s_t = ph.sem("slots_turned")
        s_xh = ph.sem("slots_high")
        s_xs = ph.sem("slots_cut")
        s_wh = ph.sem("weights_high")
        s_wc = ph.sem("weights_cut")
        s_up = ph.sem("up_done")
        s_silu = ph.sem("silu_done")
        s_g = ph.sem("gated_ready")
        s_y = ph.sem("down_done")
        s_yr = ph.sem("rows_copied")
        s_yst = [ph.sem(f"rows_stored{i}") for i in range(2)]
        s_sup = ph.sem("shared_up_done")
        s_ssilu = ph.sem("shared_silu_done")
        s_sg = ph.sem("shared_gated_ready")
        s_sy = ph.sem("shared_down_done")
        s_sx = ph.sem("shared_added")
        s_get = [ph.sem(f"rows_gathered{i}") for i in range(NCH)]
        s_sc = ph.sem("scaled")
        s_acc = ph.sem("weighted_sum")
        s_turn = ph.sem("sums_turned")
        s_x = ph.sem("residual_added")
        norm = Norm(ph, xT, lnT, const, p_h[:, 0], p_h[:, 1])
        SOON = 6

        last = EXP0 // 2 - 1

        def started(i, units):
            return not isinstance(i, int) or i * 4 >= units

        with ph.block() as block:
            @block.sync
            def _(sp):

                def load_slots(e, s):
                    slots = scratch["slots"][0:NSLOT].rearrange("(e q p) d -> e p q d", p=P, e=EXP0)
                    sp.dma_start(xr[:, s], slots[bass.ds(e, 1)].rearrange("o p q d -> (o p) q d")).then_inc(s_xr[s], 16)

                def load_up(e, s):
                    sp.dma_start(wts[:, s, 0:2 * HID0], w["ew"][bass.ds(e, 1), :, 0:2 * HID0].rearrange("o p n -> (o p) n")).then_inc(s_w[s], 16)

                def load_down(e, s):
                    sp.dma_start(wts[:, s, 2 * HID0:], w["ew"][bass.ds(e, 1), :, 2 * HID0:].rearrange("o p n -> (o p) n")).then_inc(s_wd[s], 16)

                def store(e, c):
                    sp.wait_ge(s_yr, e * 2 + c + 1)
                    rows_of = scratch["y"][0:NSLOT].rearrange("(e q p) d -> e p q d", p=P, e=EXP0)
                    sp.dma_start(rows_of[bass.ds(e, 1), :, FIRST[c]:FIRST[c] + TILES[c]].rearrange("o p q d -> (o p) q d"),
                                 yr[:, c, 0:TILES[c]]).then_inc(s_yst[c], 16)

                for s in range(2):
                    load_up(s, s)
                    load_down(s, s)
                sp.wait_ge(s_put, 16 * TOPK * NT)
                load_slots(0, 0)
                load_slots(1, 1)
                with sp.Fori(0, EXP0 // 2 - 1) as i:
                    for s in range(2):
                        e = i * 2 + s
                        sp.wait_ge(s_t, e * 2 + 2)
                        load_slots(e + 2, s)
                        store(e, 0)
                        sp.wait_ge(s_wc, e + 1)
                        load_up(e + 2, s)
                        sp.wait_ge(s_y, e * 2 + 2)
                        load_down(e + 2, s)
                        store(e, 1)
                for e in range(EXP0 - 2, EXP0):
                    store(e, 0)
                    store(e, 1)

            @block.tensor
            def _(pe):
                def shared_up(c):
                    for j in range(SM):
                        if c * SM + j >= 2:
                            pe.wait_ge(s_sg, c * SM + j - 1)
                        for n in range(2):
                            mm = pe.matmul(p_h[:, j % 2, n], ws[:, j // M, (n * M + j % M) * P:(n * M + j % M + 1) * P],
                                           lnT[:, c * CH:(c + 1) * CH], start=True, stop=True)
                        mm.then_inc(s_sup, 1)

                def shared_down(c):
                    pe.wait_ge(s_sg, (c + 1) * SM)
                    if c >= 2:
                        pe.wait_ge(s_sx, c - 1)
                    for j in range(SM):
                        mm = pe.matmul(p_y[:, c % 2].rearrange("p t d -> p (t d)"),
                                       ws[:, j // M, (2 * M + j % M) * P:(2 * M + j % M + 1) * P],
                                       sg[:, c % 2, j], start=(j == 0), stop=(j == SM - 1))
                    mm.then_inc(s_sy, 1)

                def turn(i, v):
                    s, c = v // 2, v % 2
                    if c == 0:
                        pe.wait_ge(s_xr[s], i * 16 + 16)
                    if started(i, 2 - v):
                        pe.wait_ge(s_xs, i * 4 + v - 1)
                    for q in range(TILES[c]):
                        mm = pe.transpose(p_t[:, c, q], xr[:, s, FIRST[c] + q], ident[:])
                    mm.then_inc(s_t, 1)

                def up(i, v):
                    s, c = v // 2, v % 2
                    if c == 0:
                        pe.wait_ge(s_wc, i * 2 + s + 1)
                    pe.wait_ge(s_xs, i * 4 + v + 1)
                    for m in range(M):
                        if started(i, 1 - v):
                            pe.wait_ge(s_g, (i * 4 + v - 1) * M + m + 1)
                        for n in range(2):
                            cols, slots = slice((n * M + m) * P, (n * M + m + 1) * P), slice(0, TILES[c] * P)
                            for k, (a, b) in enumerate(((wh, xh), (wl, xh), (wh, xl))):
                                mm = pe.matmul(p_h[:, m, n, slots], a[:, s, cols], b[:, c, slots], start=(k == 0), stop=(k == 2))
                        mm.then_inc(s_up, 1)

                def down(i, v):
                    s, c = v // 2, v % 2
                    pe.wait_ge(s_g, (i * 4 + v + 1) * M)
                    if c == 0:
                        pe.wait_ge(s_wd[s], i * 16 + 16)
                    if started(i, 2 - v):
                        pe.wait_ge(s_yr, i * 4 + v - 1)
                    for t in range(TILES[c]):
                        for k in range(M):
                            mm = pe.matmul(p_y[:, c, t], g[:, c, k, t * P:(t + 1) * P],
                                           wts[:, s, (2 * M + k) * P:(2 * M + k + 1) * P], start=(k == 0), stop=(k == M - 1))
                    mm.then_inc(s_y, 1)

                def pair(i, first=False, final=False):
                    for v in range(4):
                        if v < 3:
                            turn(i, v + 1)
                        elif not final:
                            turn(i + 1, 0)
                        up(i, v)
                        if v:
                            down(i, v - 1)
                        elif not first:
                            down(i - 1, 3)

                for c in range(EARLY):
                    shared_up(c)
                    if c:
                        shared_down(c - 1)
                shared_down(EARLY - 1)
                turn(0, 0)
                pe.wait_ge(s_sg, EARLY * SM)
                pe.wait_ge(s_sx, EARLY)
                pair(0, first=True)
                with pe.Fori(1, last) as i:
                    pair(i)
                pair(last, final=True)
                down(last, 3)
                pe.wait_ge(s_yr, U)
                for c in range(EARLY, NCH):
                    shared_up(c)
                for c in range(EARLY, NCH):
                    shared_down(c)
                pe.wait_ge(s_sg, NCH * SM)
                for c in range(NCH + 2):
                    if c < NCH:
                        pe.wait_ge(s_acc, c + 1)
                        if c >= 2:
                            pe.wait_ge(s_x, c - 1)
                        for t in range(CH // P):
                            mm = pe.transpose(p_t[:, c % 2, t], mine[:, 0, c * (CH // P) + t], ident[:])
                        mm.then_inc(s_turn, 1)
                    if 1 <= c <= NCH:
                        pe.wait_ge(s_x, c)
                        norm.mean(pe, c - 1)
                    if c >= 2:
                        norm.variance(pe, c - 2)

            @block.scalar
            def _(act):
                def shared(c):
                    for j in range(SM):
                        act.wait_ge(s_sup, c * SM + j + 1)
                        act.activation(gated[:, j % 2], p_h[:, j % 2, 0], ACT.Silu).then_inc(s_ssilu, 1)

                def silu(i, v):
                    n = TILES[v % 2] * P
                    for m in range(M):
                        act.wait_ge(s_up, (i * 4 + v) * M + m + 1)
                        act.activation(gated[:, m, 0:n], p_h[:, m, 0, 0:n], ACT.Silu).then_inc(s_silu, 1)

                def copy_rows(i, v):
                    s, c = v // 2, v % 2
                    act.wait_ge(s_y, i * 4 + v + 1)
                    if started(i, 2 - v):
                        act.wait_ge(s_yst[c], (i * 2 + s) * 16)
                    act.activation(yr[:, c, 0:TILES[c]], p_y[:, c, 0:TILES[c]], ACT.Copy).then_inc(s_yr, 1)

                def pair(i, first=False):
                    for v in range(4):
                        silu(i, v)
                        if v:
                            copy_rows(i, v - 1)
                        elif not first:
                            copy_rows(i - 1, 3)

                for c in range(EARLY):
                    shared(c)
                pair(0, first=True)
                with act.Fori(1, last + 1) as i:
                    pair(i)
                copy_rows(last, 3)
                for c in range(EARLY, NCH):
                    shared(c)
                for c in range(NCH + 2):
                    if c < NCH:
                        act.wait_ge(s_get[c], 16 * TOPK * (CH // P))
                        for t in range(c * (CH // P), (c + 1) * (CH // P)):
                            ins = act.activation(second[:, t], mine[:, 1, t], ACT.Copy, scale=weight[:, 1, t:t + 1])
                        ins.then_inc(s_sc, 1)
                    if 1 <= c <= NCH:
                        norm.square(act, c - 1)
                    if c >= 2:
                        norm.log(act, c - 2)
                        if c - 2 == SOON - 1:
                            for n in range(SOON):
                                norm.exp(act, n)
                for n in range(SOON, NCH):
                    norm.exp(act, n)

            @block.vector
            def _(dve):
                def shared_gate(c):
                    for j in range(SM):
                        dve.wait_ge(s_ssilu, c * SM + j + 1)
                        if c >= 2:
                            dve.wait_ge(s_sy, c - 1)
                        dve.tensor_tensor(sg[:, c % 2, j], gated[:, j % 2], p_h[:, j % 2, 1], ALU.mult).then_inc(s_sg, 1)

                def shared_add(c):
                    dve.wait_ge(s_sy, c + 1)
                    xt = xT[:, c * CH:(c + 1) * CH]
                    dve.scalar_tensor_tensor(xt, p_y[:, c % 2].rearrange("p t d -> p (t d)"), 1.0 / SHARED, xt,
                                             ALU.mult, ALU.add).then_inc(s_sx, 1)

                def copy_slots(i, v):
                    c = v % 2
                    dve.wait_ge(s_t, i * 4 + v + 1)
                    if started(i, 2 - v):
                        dve.wait_ge(s_up, (i * 4 + v - 1) * M)
                    n = TILES[c] * P
                    turned = p_t[:, c, 0:TILES[c]].rearrange("p t d -> p (t d)")
                    dve.tensor_copy(xh[:, c, 0:n], turned).then_inc(s_xh, 1)
                    dve.wait_ge(s_xh, i * 4 + v + 1)
                    dve.tensor_tensor(xl[:, c, 0:n], turned, xh[:, c, 0:n].bitcast(F32), ALU.subtract).then_inc(s_xs, 1)

                def cut_weights(i, s):
                    dve.wait_ge(s_w[s], i * 16 + 16)
                    if not isinstance(i, int) or i:
                        dve.wait_ge(s_up, (i * 4 + 2 * s - 2) * M)
                    dve.tensor_copy(wh[:, s], wts[:, s, 0:2 * HID0]).then_inc(s_wh, 1)
                    dve.wait_ge(s_wh, i * 2 + s + 1)
                    dve.tensor_tensor(wl[:, s], wts[:, s, 0:2 * HID0], wh[:, s].bitcast(F32), ALU.subtract).then_inc(s_wc, 1)

                def gate(i, v):
                    c = v % 2
                    n = TILES[c] * P
                    for m in range(M):
                        dve.wait_ge(s_silu, (i * 4 + v) * M + m + 1)
                        if started(i, 2 - v):
                            dve.wait_ge(s_y, i * 4 + v - 1)
                        dve.tensor_tensor(g[:, c, m, 0:n], gated[:, m, 0:n], p_h[:, m, 1, 0:n], ALU.mult).then_inc(s_g, 1)

                def pair(i, final=False):
                    for v in range(4):
                        if v < 3:
                            copy_slots(i, v + 1)
                        elif not final:
                            copy_slots(i + 1, 0)
                        gate(i, v)
                        if v == 0:
                            cut_weights(i, 1)
                        elif v == 2 and not final:
                            cut_weights(i + 1, 0)

                for c in range(EARLY):
                    shared_gate(c)
                    if c:
                        shared_add(c - 1)
                shared_add(EARLY - 1)
                cut_weights(0, 0)
                copy_slots(0, 0)
                pair(0)
                with dve.Fori(1, last) as i:
                    pair(i)
                pair(last, final=True)
                for c in range(EARLY, NCH):
                    shared_gate(c)
                for c in range(EARLY, NCH):
                    shared_add(c)

                def residual(c):
                    dve.wait_ge(s_turn, c + 1)
                    dve.wait_ge(s_sx, NCH)
                    xt = xT[:, c * CH:(c + 1) * CH]
                    dve.tensor_tensor(xt, xt, p_t[:, c % 2].rearrange("p t d -> p (t d)"), ALU.add).then_inc(s_x, 1)

                dve.wait_ge(s_sup, NCH * SM)
                norm.set_eps(dve)
                for c in range(NCH + 1):
                    if c < NCH:
                        dve.wait_ge(s_sc, c + 1)
                        for t in range(c * (CH // P), (c + 1) * (CH // P)):
                            ins = dve.scalar_tensor_tensor(mine[:, 0, t], mine[:, 0, t], weight[:, 0, t:t + 1], second[:, t],
                                                           ALU.mult, ALU.add)
                        ins.then_inc(s_acc, 1)
                    if c:
                        residual(c - 1)
                        norm.centre(dve, c - 1)
                for c in range(NCH):
                    norm.scale(dve, c)

            @block.gpsimd
            def _(pool):
                for t in range(NT):
                    for k in range(TOPK):
                        pool.indirect_dma_start(scratch["slots"], bass.IndirectOffsetOnAxis(ap=put[:, k, t:t + 1], axis=0),
                                                rows[:, t], None).then_inc(s_put, 16)
                for c in range(2):
                    pool.wait_ge(s_yst[c], 16 * EXP0)
                for t in range(NT):
                    for k in range(TOPK):
                        pool.indirect_dma_start(mine[:, k, t], None, scratch["y"],
                                                bass.IndirectOffsetOnAxis(ap=get[:, k, t:t + 1], axis=0)).then_inc(s_get[t // (CH // P)], 16)


HEADS, DH = 16, 8
GH = 4
GROUPS = HEADS // GH
UNITS = BATCH * GROUPS
KT = SEQ // P
VW = DH + 1
PARTS = 3
PAIRS = PARTS * PARTS
MROW = 96
SCALE = DH ** -0.5
MASKED = -1e30


def qkv(nc, lnT, const, scratch):
    with Phase(nc, "qkv") as ph:
        wqk = const["wqk"]
        wv = const["wv"]
        rest = ph.sb("rest", [P, 2, CH])
        parts = ph.sb("parts", [P, 2, 2, PARTS, SEQ], BF16)
        vp = ph.sb("vp", [P, 2, GROUPS, KT, GH, VW])
        p_qk = ph.ps("p_qk", [P, CPB, 2, CH])
        p_v = ph.ps("p_v", [P, CPB, CH // P, P])
        s_one = ph.sem("ones_set")
        s_qk = ph.sem("projected")
        s_hi = ph.sem("hi_cut")
        s_rest = ph.sem("rest_cut")
        s_mid = ph.sem("mid_cut")
        s_cut = ph.sem("parts_ready")
        s_v = ph.sem("v_projected")
        s_vc = ph.sem("v_copied")
        s_st = [[ph.sem(f"parts_stored{x}{j}") for j in range(2)] for x in range(2)]
        s_vst = [ph.sem(f"v_stored{i}") for i in range(2)]

        with ph.block() as block:
            @block.sync
            def _(sp):
                for b in range(BATCH):
                    x = b % 2
                    for j in range(2):
                        sp.wait_ge(s_cut, 2 * CPB * b + 2 * (CPB - 1) + j + 1)
                        for a in range(PARTS):
                            sp.dma_start(scratch["parts"][j, b, :, a], parts[:, x, j, a]).then_inc(s_st[x][j], 16)
                    sp.wait_ge(s_vc, CPB * (b + 1))
                    sp.dma_start(scratch["v"][b].rearrange("g p k n -> p g k n"),
                                 vp[:, x].rearrange("p g k h v -> p g k (h v)")).then_inc(s_vst[x], 16)
                for x in range(2):
                    for j in range(2):
                        sp.wait_ge(s_st[x][j], 16 * PARTS * BATCH // 2)
                    sp.wait_ge(s_vst[x], 16 * BATCH // 2)

            @block.tensor
            def _(pe):
                for g in range(NCH):
                    c = g % CPB
                    for j in range(2):
                        if g >= CPB:
                            pe.wait_ge(s_rest, 2 * (g - CPB) + j + 1)
                        pe.matmul(p_qk[:, c, j], wqk[:, j], lnT[:, g * CH:(g + 1) * CH], start=True, stop=True).then_inc(s_qk, 1)
                    if g >= CPB:
                        pe.wait_ge(s_vc, g - CPB + 1)
                    for t in range(CH // P):
                        mm = pe.matmul(p_v[:, c, t], lnT[:, g * CH + t * P:g * CH + (t + 1) * P], wv[:], start=True, stop=True)
                    mm.then_inc(s_v, 1)

            @block.scalar
            def _(act):
                act.wait_ge(s_one, 1)
                for g in range(NCH):
                    b, c = g // CPB, g % CPB
                    part = parts[:, b % 2, :, :, c * CH:(c + 1) * CH]
                    for j in range(2):
                        act.wait_ge(s_qk, g * 2 + j + 1)
                        if b >= 2:
                            act.wait_ge(s_st[b % 2][j], b // 2 * (16 * PARTS))
                        act.activation(part[:, j, 0], p_qk[:, c, j], ACT.Copy).then_inc(s_hi, 1)
                    act.wait_ge(s_v, g + 1)
                    if b >= 2:
                        act.wait_ge(s_vst[b % 2], b // 2 * 16)
                    for t in range(CH // P):
                        ins = act.activation(vp[:, b % 2, :, c * (CH // P) + t, :, 0:DH],
                                             p_v[:, c, t].rearrange("p (g h v) -> p g h v", g=GROUPS, h=GH), ACT.Copy)
                    ins.then_inc(s_vc, 1)
                    for j in range(2):
                        act.wait_ge(s_rest, g * 2 + j + 1)
                        act.activation(part[:, j, 1], rest[:, j], ACT.Copy).then_inc(s_mid, 1)

            @block.vector
            def _(dve):
                dve.memset(vp[:], 1.0).then_inc(s_one, 1)
                for g in range(NCH):
                    b, c = g // CPB, g % CPB
                    part = parts[:, b % 2, :, :, c * CH:(c + 1) * CH]
                    for j in range(2):
                        dve.wait_ge(s_hi, g * 2 + j + 1)
                        if g:
                            dve.wait_ge(s_cut, g * 2 + j - 1)
                        dve.tensor_tensor(rest[:, j], p_qk[:, c, j], part[:, j, 0], ALU.subtract).then_inc(s_rest, 1)
                    for j in range(2):
                        dve.wait_ge(s_mid, g * 2 + j + 1)
                        dve.tensor_tensor(part[:, j, 2], rest[:, j], part[:, j, 1], ALU.subtract).then_inc(s_cut, 1)


def attention(nc, att, const, scratch):
    HALF = KT // 2
    NST = KT + HALF
    NEXP = 2 * NST
    LOADS = 16 * (PARTS * CPB + (2 * PARTS - 1) + 1)
    LAST = UNITS - 1
    SLOTS = 3
    TURNS = (UNITS - 2) // SLOTS
    with Phase(nc, "attn") as ph:
        ident = const["ident"]
        identb = const["ident_bf16"]
        mask_q = const["mask_q"]
        mask_k = const["mask_k"]
        qs = [ph.sb(f"qs{i}", [P, CPB, GH, CH], BF16) for i in range(SLOTS)]
        ks = [ph.sb(f"ks{i}", [P, GH, SEQ], BF16) for i in range(SLOTS)]
        vs = [ph.sb(f"vs{i}", [P, KT, GH, VW]) for i in range(SLOTS)]
        mx = ph.sb("mx", [P, 2, GH, KT])
        top = ph.sb("top", [P, GH, HALF])
        ntop = ph.sb("ntop", [P, GH, HALF])
        mrest = ph.sb("mrest", [P, GH, HALF])
        mparts = ph.sb("mparts", [P, PARTS, 2, GH, HALF], BF16)
        mt = ph.sb("mt", [PARTS * GH * KT, 2, P], BF16)
        prob = ph.sb("prob", [P, 2, GH, CH])
        ob = ph.sb("ob", [P, 2, CH])
        rden = ph.sb("rden", [P, 2, HALF, GH, 1])
        p_m = ph.ps("p_m", [P, 3, CH])
        p_s = ph.ps("p_s", [P, 2, 2, CH])
        p_o = ph.ps("p_o", [P, CH])

        s_qset = ph.sem("query_stacks_zeroed")
        s_kset = ph.sem("key_stacks_set")
        s_mx0 = ph.sem("maxima_filled")
        s_po0 = ph.sem("out_bank_zeroed")
        s_load = [ph.sem(f"loaded{i}") for i in range(SLOTS)]
        s_qz = ph.sem("max_rows_zeroed")
        s_job = ph.sem("job_given")
        s_done = ph.sem("job_done")
        s_m = ph.sem("max_step")
        s_mp = ph.sem("max_parts_ready")
        s_kz = ph.sem("key_stacks_zeroed")
        s_mrow = [ph.sem(f"max_rows_loaded{i}") for i in range(2)]
        s_st = ph.sem("scores_ready")
        s_exp = ph.sem("exp_done")
        s_pv = ph.sem("pv_done")
        s_ev = ph.sem("out_copied")
        s_rec = ph.sem("denominators_inverted")
        hold = ph.sem("wait_passed")

        steps = [(half, kt) for half in range(CPB) for kt in range((half + 1) * HALF)]
        half_end = [t for t, (half, kt) in enumerate(steps) if kt == (half + 1) * HALF - 1]

        def width(qt, c):
            return min(CH, (qt + 1) * P - c * CH)

        def first_query(half, kt):
            return max(kt * P - half * CH, 0)

        def maxima(half):
            out = []
            for qt in range(half * HALF, (half + 1) * HALF):
                for c in range(half + 1):
                    n = min(GH, CH // width(qt, c))
                    out += [("max", half, qt, c, range(h, h + n)) for h in range(0, GH, n)]
            return out

        before = maxima(0) + [("rows", 0)] + maxima(1)
        late = maxima(1)
        early = maxima(0)
        beside = early[:3] + [("rows", 1)] + early[3:5] + [("out", 1)] + early[5:] + late[:9] + [("rows", 0)] + late[9:13] + [("out", 0)] + late[13:]
        beside_first = [j for j in beside if j != ("out", 1)]
        beside_last = [("rows", 1), ("out", 1), ("out", 0)]

        def jobs_before(u):
            if isinstance(u, int) and u == 0:
                return len(before)
            return u * len(beside) + len(before) - 1

        def bank(jobs, k):
            return (k - len(jobs)) % 3

        def bank_free(jobs, k, start):
            return start + (k - 2 if k >= 3 else bank(jobs, k) - 2)

        with ph.block() as block:

            @block.sync
            def _(sp):

                def load(u, s):
                    part = scratch["parts"].rearrange("j b (g h) a r t -> j (b g) (a r) h t", g=GROUPS)
                    for m in range(PARTS):
                        rows = slice(m * PARTS * DH, (m + 1) * PARTS * DH)
                        for first, count, at in ((m, PARTS - m, 0), (0, m, PARTS - m)):
                            if count:
                                src = part[1, bass.ds(u, 1), first * DH:(first + count) * DH]
                                at += m * PARTS
                                sp.dma_start(ks[s][at * DH:(at + count) * DH],
                                             src.rearrange("o a h t -> (o a) h t")).then_inc(s_load[s], 16)
                        for half in range(CPB):
                            src = part[0, bass.ds(u, 1), 0:PARTS * DH, :, half * CH:(half + 1) * CH]
                            sp.dma_start(qs[s][rows, half], src.rearrange("o a h t -> (o a) h t")).then_inc(s_load[s], 16)
                    v = scratch["v"].rearrange("b g p k n -> (b g) p k n")
                    sp.dma_start(vs[s][:].rearrange("p k h v -> p k (h v)"),
                                 v[bass.ds(u, 1)].rearrange("o p k n -> (o p) k n")).then_inc(s_load[s], 16)

                for s in range(SLOTS):
                    sp.wait_ge(s_qset, s + 1)
                    sp.wait_ge(s_kz, s + 1)
                    load(s, s)
                with sp.Fori(0, TURNS) as i:
                    for s in range(SLOTS):
                        u = i * SLOTS + s + SLOTS
                        sp.wait_ge(s_pv, (u - 2) * NST)
                        load(u, s)
                sp.wait_ge(s_pv, (LAST - 2) * NST)
                load(LAST, LAST % SLOTS)

            @block.tensor
            def _(pe):
                pe.wait_ge(s_po0, 1)

                def give(job, u, s, jobs, k, start, loads):
                    x = bank(jobs, k)
                    if not isinstance(start, int) or bank_free(jobs, k, start) > 0:
                        pe.wait_ge(s_done, bank_free(jobs, k, start))
                    if job[0] == "rows":
                        half = job[1]
                        pe.wait_ge(s_mp, (u + (1 - half)) * 2 + half + 1)
                        pe.transpose(p_m[0:PARTS * GH * KT, x, 0:P // 2].bitcast(BF16),
                                     mparts[:].rearrange("p a c h t -> p (a c h t)"), identb[:]).then_inc(s_job, 1)
                    elif job[0] == "out":
                        half = job[1]
                        pe.wait_ge(s_ev, (u - half) * 2 + half + 1)
                        for t in range(HALF):
                            mm = pe.transpose(p_m[:, x, t * P:(t + 1) * P], ob[:, half, t * P:(t + 1) * P], ident[:])
                        mm.then_inc(s_job, 1)
                    else:
                        _, half, qt, c, heads = job
                        if job == before[0]:
                            pe.wait_ge(s_load[s], loads * LOADS)
                            pe.wait_ge(s_qz, u + 2)
                            if isinstance(u, int) and u + 2 <= SLOTS:
                                pe.wait_ge(s_kset, u + 2)
                        wd = width(qt, c)
                        diagonal = (qt + 1) * P - c * CH <= CH
                        for n, h in enumerate(heads):
                            mm = pe.matmul(p_m[:, x, n * wd:(n + 1) * wd], qs[s][:, half, h, qt % HALF * P:(qt % HALF + 1) * P],
                                           ks[s][:, h, c * CH:c * CH + wd], start=True, stop=not diagonal)
                            if diagonal:
                                mm = pe.matmul(p_m[:, x, (n + 1) * wd - P:(n + 1) * wd], identb[:], mask_q[:], start=False, stop=True)
                        mm.then_inc(s_job, 1)

                def scores(u, s, t, pair):
                    half, kt = steps[t]
                    q0 = first_query(half, kt)
                    k = 2 * t + pair
                    if kt == 0 and pair == 0:
                        pe.wait_ge(s_mrow[half], u * 48 + 48)
                    if not isinstance(u, int) or u * NEXP + k >= 2:
                        pe.wait_ge(s_exp, u * NEXP + k - 1)
                    for j in range(2):
                        h = 2 * pair + j
                        on_diagonal = kt * P >= half * CH
                        mm = pe.matmul(p_s[:, pair, j, 0:CH - q0], ks[s][:, h, kt * P:(kt + 1) * P],
                                       qs[s][:, half, h, q0:CH], start=True, stop=not on_diagonal)
                        if on_diagonal:
                            mm = pe.matmul(p_s[:, pair, j, 0:P], identb[:], mask_k[:], start=False, stop=True)
                    mm.then_inc(s_st, 1)

                def values(u, s, t):
                    half, kt = steps[t]
                    q0 = first_query(half, kt)
                    if kt == 0 and (not isinstance(u, int) or 2 * u + half > 0):
                        pe.wait_ge(s_ev, u * 2 + half)
                    pe.wait_ge(s_exp, u * NEXP + 2 * t + 2)
                    for h in range(GH):
                        mm = pe.matmul(p_o[32 * h:32 * h + VW, q0:CH], vs[s][:, kt, h], prob[:, t % 2, h, 0:CH - q0],
                                       start=(kt == 0), stop=(kt == (half + 1) * HALF - 1))
                    mm.then_inc(s_pv, 1)

                def unit(u, s, jobs, loads):
                    start = jobs_before(u)
                    cols = [CH - first_query(*step) for step in steps]
                    of_maxima = sum(width(j[2], j[3]) * len(j[4]) for j in jobs if j[0] == "max")
                    given, spent = 0, 0

                    def due(t, point):
                        nonlocal given, spent
                        share = (sum(cols[:t]) + cols[t] * point / 3) / sum(cols)
                        while given < len(jobs):
                            job = jobs[given]
                            if job[0] == "max":
                                if spent >= share * of_maxima:
                                    return
                                spent += width(job[2], job[3]) * len(job[4])
                            elif job == ("out", 1) and t < 1 or job == ("out", 0) and t < half_end[0] + 3:
                                return
                            give(job, u, (s + 1) % SLOTS, jobs, given, start, loads)
                            given += 1

                    for t in range(NST):
                        scores(u, s, t, 0)
                        due(t, 1)
                        scores(u, s, t, 1)
                        due(t, 2)
                        if t:
                            values(u, s, t - 1)
                        elif not isinstance(u, int) or u:
                            values(u - 1, (s - 1) % SLOTS, NST - 1)
                        due(t, 3)
                    assert given == len(jobs)

                for k, job in enumerate(before):
                    give(job, -1, 0, before, k, 0, 1)
                unit(0, 0, beside_first, 1)
                with pe.Fori(0, TURNS) as i:
                    for n in range(1, SLOTS + 1):
                        unit(i * SLOTS + n, n % SLOTS, beside, i + (n + 1) // SLOTS + 1)
                for u in range(TURNS * SLOTS + 1, UNITS):
                    unit(u, u % SLOTS, beside if u < LAST else beside_last, (u + 1) // SLOTS + 1)
                values(LAST, LAST % SLOTS, NST - 1)
                give(("out", 1), UNITS, 0, [("out", 1)], 0, jobs_before(LAST) + len(beside_last), 0)

            @block.scalar
            def _(act):
                def copy_out(u, half):
                    act.wait_ge(s_pv, u * NST + half_end[half] + 1)
                    if not isinstance(u, int) or u:
                        act.wait_ge(s_rec, u * 2 + half - 1)
                    act.activation(ob[:, half], p_o[:], ACT.Copy).then_inc(s_ev, 1)

                def unit(u):
                    for t, (half, kt) in enumerate(steps):
                        q0 = first_query(half, kt)
                        for pair in range(2):
                            act.wait_ge(s_st, u * NEXP + 2 * t + pair + 1)
                            if pair == 0 and (not isinstance(u, int) or u * NST + t >= 2):
                                act.wait_ge(s_pv, u * NST + t - 1)
                            act.activation(prob[:, t % 2, 2 * pair:2 * pair + 2, 0:CH - q0], p_s[:, pair, :, 0:CH - q0],
                                           ACT.Exp, scale=SCALE).then_inc(s_exp, 1)
                        if t == half_end[0] + 1:
                            copy_out(u, 0)
                        if t == 0 and (not isinstance(u, int) or u):
                            copy_out(u - 1, 1)

                unit(0)
                with act.Fori(1, UNITS) as u:
                    unit(u)
                copy_out(LAST, 1)

            @block.vector
            def _(dve):
                for s in range(SLOTS):
                    dve.memset(ks[s][:].bitcast(mybir.dt.uint32), 0).then_inc(s_kz, 1)
                    dve.memset(qs[s][:].bitcast(mybir.dt.uint32), 0).then_inc(s_qset, 1)
                dve.memset(p_o[:], 0.0).then_inc(s_po0, 1)
                dve.memset(mx[:], FILL).then_inc(s_mx0, 1)
                dve.memset(mparts[:], 0.0).then_inc(s_mx0, 1)
                dve.wait_ge(s_mx0, 2)

                def cut(q, half, done):
                    dve.wait_ge(s_done, done)
                    tiles = slice(half * HALF, (half + 1) * HALF)
                    dve.tensor_tensor(top[:], mx[:, 0, :, tiles], mx[:, 1, :, tiles], ALU.max).then_inc(s_m, 1)
                    dve.wait_ge(s_m, q * 5 + 1)
                    dve.tensor_scalar(ntop[:], top[:], -1.0, None, ALU.mult).then_inc(s_m, 1)
                    dve.tensor_scalar(mparts[:, 0, half], top[:], -1.0, None, ALU.mult).then_inc(s_m, 1)
                    dve.wait_ge(s_m, q * 5 + 3)
                    dve.tensor_tensor(mrest[:], ntop[:], mparts[:, 0, half], ALU.subtract).then_inc(s_m, 1)
                    dve.wait_ge(s_m, q * 5 + 4)
                    dve.tensor_copy(mparts[:, 1, half], mrest[:]).then_inc(s_m, 1)
                    dve.wait_ge(s_m, q * 5 + 5)
                    dve.tensor_tensor(mparts[:, 2, half], mrest[:], mparts[:, 1, half], ALU.subtract).then_inc(s_mp, 1)

                def do(job, u, jobs, k, start):
                    x = bank(jobs, k)
                    dve.wait_ge(s_job, start + k + 1)
                    if job[0] == "rows":
                        half = job[1]
                        v = u + (1 - half)
                        if not isinstance(v, int) or v:
                            dve.wait_ge(s_mrow[half], v * 48)
                        dve.tensor_copy(mt[:, half], p_m[0:PARTS * GH * KT, x, 0:P // 2].bitcast(BF16)).then_inc(s_done, 1)
                    elif job[0] == "out":
                        half = job[1]
                        v = u - half
                        turned = p_m[:, x].rearrange("p (t h v) -> p t h v", t=HALF, h=GH)
                        if not isinstance(v, int) or v:
                            dve.wait_ge(s_done, start)
                        dve.reciprocal(rden[:, half], turned[:, :, :, DH:VW]).then_inc(s_rec, 1)
                        dve.wait_ge(s_rec, v * 2 + half + 1)
                        dve.tensor_tensor(att[:, bass.ds(v, 1), half * HALF:(half + 1) * HALF].rearrange("p o t (h v) -> p (o t) h v", h=GH),
                                          turned[:, :, :, 0:DH], rden[:, half].to_broadcast([P, HALF, GH, DH]), ALU.mult).then_inc(s_done, 1)
                    else:
                        _, half, qt, c, heads = job
                        wd, n = width(qt, c), len(heads)
                        dve.tensor_reduce(mx[:, c, heads[0]:heads[0] + n, qt:qt + 1],
                                          p_m[:, x, 0:n * wd].rearrange("p (h w) -> p h w", h=n), AX.X, ALU.max).then_inc(s_done, 1)

                def work(u, jobs):
                    start = jobs_before(u)
                    for k, job in enumerate(jobs):
                        do(job, u, jobs, k, start)
                        if job[0] == "max" and job == maxima(job[1])[-1]:
                            cut(u * 2 + 2 + job[1], job[1], start + k + 1)

                for k, job in enumerate(before):
                    do(job, -1, before, k, 0)
                    if job[0] == "max" and job == maxima(job[1])[-1]:
                        cut(job[1], job[1], k + 1)
                work(0, beside_first)
                with dve.Fori(1, LAST) as u:
                    work(u, beside)
                work(LAST, beside_last)
                do(("out", 1), UNITS, [("out", 1)], 0, jobs_before(LAST) + len(beside_last))

            @block.gpsimd
            def _(pool):
                def zero(s):
                    pool.memset(qs[s][MROW:MROW + PARTS].bitcast(mybir.dt.uint32), 0).then_inc(s_qz, 1)

                def max_rows(s, half, done):
                    pool.wait_ge(s_done, done)
                    waited(pool, hold)
                    for a in range(PARTS):
                        n = GH * HALF
                        pool.dma_start(qs[s][MROW + a:MROW + a + 1, half].rearrange("a h (t p) -> a (h t) p", p=P),
                                       mt[(2 * a + half) * n:(2 * a + half + 1) * n, half]).then_inc(s_mrow[half], 16)

                def unit(u, s, jobs):
                    max_rows(s, 1, jobs_before(u) + jobs.index(("rows", 1)) + 1)
                    if jobs == beside and (not isinstance(u, int) or u < LAST - 1):
                        pool.wait_ge(s_pv, u * NST)
                        waited(pool, hold)
                        zero((s + 2) % SLOTS)
                    if jobs != beside_last:
                        max_rows((s + 1) % SLOTS, 0, jobs_before(u) + jobs.index(("rows", 0)) + 1)

                for s in range(SLOTS):
                    pool.wait_ge(s_kz, s + 1)
                    pool.memset(ks[s][MROW:MROW + PARTS], 1.0).then_inc(s_kset, 1)
                    pool.wait_ge(s_qset, s + 1)
                    zero(s)
                max_rows(0, 0, before.index(("rows", 0)) + 1)
                unit(0, 0, beside_first)
                with pool.Fori(0, TURNS) as i:
                    for n in range(1, SLOTS + 1):
                        unit(i * SLOTS + n, n % SLOTS, beside)
                for u in range(TURNS * SLOTS + 1, UNITS):
                    unit(u, u % SLOTS, beside if u < LAST else beside_last)


def attention_out(nc, xT, lnT, att, const):
    with Phase(nc, "attn_out") as ph:
        ident = const["ident"]
        wo = const["wo"]
        heads = ph.sb("heads", [P, 2, CH // P, GROUPS, GH * DH])
        turned = ph.sb("turned", [P, 2, CH])
        p_t = ph.ps("p_t", [P, 2, CH])
        p_o = ph.ps("p_o", [P, 2, CH])
        s_g = ph.sem("heads_grouped")
        s_t = ph.sem("turned")
        s_c = ph.sem("turned_copied")
        s_o = ph.sem("projected")
        s_x = ph.sem("residual_added")
        p_mean = ph.ps("p_mean", [P, 2, CH])
        p_var = ph.ps("p_var", [P, 2, CH])
        norm = Norm(ph, xT, lnT, const, p_mean, p_var)

        with ph.block() as block:
            @block.tensor
            def _(pe):
                for c in range(NCH + 3):
                    if c < NCH:
                        pe.wait_ge(s_g, c + 1)
                        if c >= 2:
                            pe.wait_ge(s_c, c - 1)
                        for t in range(CH // P):
                            mm = pe.transpose(p_t[:, c % 2, t * P:(t + 1) * P],
                                              heads[:, c % 2, t].rearrange("p g n -> p (g n)"), ident[:])
                        mm.then_inc(s_t, 1)
                    if 1 <= c <= NCH:
                        pe.wait_ge(s_c, c)
                        if c >= 3:
                            pe.wait_ge(s_x, c - 2)
                        pe.matmul(p_o[:, (c - 1) % 2], wo[:], turned[:, (c - 1) % 2], start=True, stop=True).then_inc(s_o, 1)
                    if 2 <= c <= NCH + 1:
                        pe.wait_ge(s_x, c - 1)
                        norm.mean(pe, c - 2)
                    if c >= 3:
                        norm.variance(pe, c - 3)

            @block.scalar
            def _(act):
                for c in range(NCH + 3):
                    if c < NCH:
                        act.wait_ge(s_t, c + 1)
                        if c >= 2:
                            act.wait_ge(s_o, c - 1)
                        act.activation(turned[:, c % 2], p_t[:, c % 2], ACT.Copy).then_inc(s_c, 1)
                    if 2 <= c <= NCH + 1:
                        norm.square(act, c - 2)
                    if c >= 3:
                        norm.log(act, c - 3)
                for g in range(NCH):
                    norm.exp(act, g)

            @block.vector
            def _(dve):
                norm.set_eps(dve)
                for c in range(NCH + 2):
                    if c < NCH:
                        b, half = c // CPB, c % CPB
                        tiles = att[:, b * GROUPS:(b + 1) * GROUPS, half * (CH // P):(half + 1) * (CH // P)]
                        if c >= 2:
                            dve.wait_ge(s_t, c - 1)
                        dve.tensor_copy(heads[:, c % 2], tiles.rearrange("p g t n -> p t g n")).then_inc(s_g, 1)
                    if 1 <= c <= NCH:
                        dve.wait_ge(s_o, c)
                        xt = xT[:, (c - 1) * CH:c * CH]
                        dve.tensor_tensor(xt, xt, p_o[:, (c - 1) % 2], ALU.add).then_inc(s_x, 1)
                    if c >= 2:
                        norm.centre(dve, c - 2)
                for g in range(NCH):
                    norm.scale(dve, g)


EXP1, HID1 = 8, 512
THRESHOLD = 0.125


def router1(nc, lnT, const, scratch):
    E, T = EXP1, NT
    with Phase(nc, "router1") as ph:
        ident = const["ident"]
        gate_w = const["gate1_w"]
        gate_b = const["gate1_b"]
        logit = ph.sb("logit", [P, T, E + 1])
        top = ph.sb("top", [P, T])
        score = ph.sb("score", [P, T, E])
        sig = ph.sb("sig", [P, T])
        total = ph.sb("total", [P, T])
        none = ph.sb("none", [P, T])
        tmp = ph.sb("tmp", [P, T, E])
        wt = ph.sb("wt", [E, TOK])
        p_lg = ph.ps("p_lg", [P, T, E + 1])
        p_t = ph.ps("p_t", [E, 2, CH])
        s_lg = ph.sem("logits_ready")
        s_v = ph.sem("vector_step")
        s_e = ph.sem("exp_done")
        s_wt = ph.sem("weights_ready")
        s_t = ph.sem("turned")
        s_tc = ph.sem("turned_copied")
        s_st = ph.sem("weights_stored")

        with ph.block() as block:
            @block.sync
            def _(sp):
                sp.wait_ge(s_tc, NCH)
                sp.dma_start(scratch["wt"], wt[:]).then_inc(s_st, 16)
                sp.wait_ge(s_st, 16)

            @block.tensor
            def _(pe):
                for t in range(T):
                    mm = pe.matmul(p_lg[:, t], lnT[:, t * P:(t + 1) * P], gate_w[:], start=True, stop=True)
                mm.then_inc(s_lg, 1)
                pe.wait_ge(s_wt, 1)
                for c in range(NCH):
                    if c >= 2:
                        pe.wait_ge(s_tc, c - 1)
                    for t in range(CH // P):
                        mm = pe.transpose(p_t[:, c % 2, t * P:(t + 1) * P], tmp[:, c * (CH // P) + t], ident[:])
                    mm.then_inc(s_t, 1)

            @block.scalar
            def _(act):
                act.wait_ge(s_v, 3)
                act.activation(tmp[:], score[:], ACT.Exp).then_inc(s_e, 1)
                act.activation(sig[:], logit[:, :, E], ACT.Exp, scale=-1.0).then_inc(s_e, 1)

            @block.vector
            def _(dve):
                count = [0]

                def step(ins):
                    count[0] += 1
                    ins.then_inc(s_v, 1)
                    dve.wait_ge(s_v, count[0])

                over = lambda a: a.unsqueeze(2).to_broadcast([P, T, E])
                dve.wait_ge(s_lg, 1)
                step(dve.tensor_tensor(logit[:], p_lg[:], gate_b[:].unsqueeze(1).to_broadcast([P, T, E + 1]), ALU.add))
                step(dve.tensor_reduce(top[:], logit[:, :, 0:E], AX.X, ALU.max))
                step(dve.tensor_tensor(score[:], logit[:, :, 0:E], over(top[:]), ALU.subtract))
                dve.wait_ge(s_e, 2)
                step(dve.tensor_reduce(total[:], tmp[:], AX.X, ALU.add))
                step(dve.reciprocal(total[:], total[:]))
                step(dve.tensor_scalar(sig[:], sig[:], 1.0, None, ALU.add))
                step(dve.reciprocal(sig[:], sig[:]))
                step(dve.tensor_scalar(sig[:], sig[:], THRESHOLD, None, ALU.mult))
                step(dve.tensor_tensor(score[:], tmp[:], over(total[:]), ALU.mult))
                step(dve.tensor_tensor(score[:], score[:], over(sig[:]), ALU.subtract))
                step(dve.tensor_scalar(score[:], score[:], 0.0, None, ALU.max))
                step(dve.tensor_reduce(total[:], score[:], AX.X, ALU.add))
                step(dve.tensor_scalar(none[:], total[:], 0.0, None, ALU.is_equal))
                step(dve.tensor_tensor(total[:], total[:], none[:], ALU.add))
                step(dve.reciprocal(total[:], total[:]))
                dve.tensor_tensor(tmp[:], score[:], over(total[:]), ALU.mult).then_inc(s_wt, 1)
                for c in range(NCH):
                    dve.wait_ge(s_t, c + 1)
                    dve.tensor_copy(wt[:, c * CH:(c + 1) * CH], p_t[:, c % 2]).then_inc(s_tc, 1)


def experts1(nc, xT, lnT, const, w, scratch):
    F = HID1 // P
    F32R = mybir.dt.float32r
    ON_POOL = F // 2
    U = CPB * EXP1
    TURNS = NCH // CPB
    with Phase(nc, "experts1") as ph:
        b1 = const["b1"]
        b2 = const["b2"]
        raw = ph.sb("raw", [P, 2, 2 * HID1])
        wh = ph.sb("wh", [P, EXP1, 2 * HID1], F32R)
        wl = ph.sb("wl", [P, EXP1, 2 * HID1], F32R)
        xh = ph.sb("xh", [P, CPB, CH], F32R)
        xl = ph.sb("xl", [P, CPB, CH], F32R)
        share = ph.sb("share", [P, CPB, EXP1, CH])
        g = ph.sb("g", [P, F, CH])
        gh = ph.sb("gh", [P, 2, F, CH], F32R)
        gl = ph.sb("gl", [P, 2, F, CH], F32R)
        part = ph.sb("part", [P, 2, CH])
        p_h = ph.ps("p_h", [P, F, CH])
        p_y = ph.ps("p_y", [P, 2, CH])
        s_raw = [ph.sem(f"weights_loaded{i}") for i in range(2)]
        s_wh = ph.sem("weights_high")
        s_w = ph.sem("weights_cut")
        s_xh = ph.sem("tokens_high")
        s_xs = ph.sem("tokens_cut")
        s_share = [ph.sem(f"shares_loaded{i}") for i in range(CPB)]
        s_up = ph.sem("up_done")
        s_g = ph.sem("gelu_done")
        s_hi = ph.sem("high_cut")
        s_lp = ph.sem("low_cut_by_pool")
        s_lv = ph.sem("low_cut_by_vector")
        s_y = ph.sem("down_done")
        s_part = ph.sem("weighted")
        s_x = ph.sem("residual_added")

        def products(stationary, moving):
            (ah, al), (bh, bl) = stationary, moving
            return (ah, bh), (al, bh), (ah, bl)

        def later(i, v, units=1):
            return not isinstance(i, int) or i * U + v >= units

        with ph.block() as block:
            @block.sync
            def _(sp):
                def weights(e):
                    if e >= 2:
                        sp.wait_ge(s_w, e - 1)
                    sp.dma_start(raw[:, e % 2], w["fw"][e]).then_inc(s_raw[e % 2], 16)

                def shares(c, x):
                    src = scratch["wt"].rearrange("(o e) t -> o e t", o=1)[:, :, bass.ds(c * CH, CH)]
                    sp.dma_start(share[:, x], src.to_broadcast([P, EXP1, CH])).then_inc(s_share[x], 16)

                weights(0)
                weights(1)
                for x in range(CPB):
                    shares(x, x)
                for e in range(2, EXP1):
                    weights(e)
                with sp.Fori(1, TURNS) as i:
                    for x in range(CPB):
                        c = i * CPB + x
                        sp.wait_ge(s_part, (c - 1) * EXP1)
                        shares(c, x)

            @block.tensor
            def _(pe):
                def up(i, v):
                    n, x, e = i * U + v, v // EXP1, v % EXP1
                    if e == 0:
                        pe.wait_ge(s_xs, i * CPB + x + 1)
                    if isinstance(i, int) and x == 0:
                        pe.wait_ge(s_w, e + 1)
                    for m in range(F):
                        if later(i, v):
                            pe.wait_ge(s_g, (n - 1) * F + m + 1)
                        cols = slice(m * P, (m + 1) * P)
                        for k, (a, b) in enumerate(products((wh, wl), (xh, xl))):
                            mm = pe.matmul(p_h[:, m], a[:, e, cols], b[:, x], start=(k == 0), stop=(k == 2))
                        mm.then_inc(s_up, 1)

                def down(i, v):
                    n, e = i * U + v, v % EXP1
                    if later(i, v, 2):
                        pe.wait_ge(s_part, n - 1)
                    for m in range(F):
                        if m < ON_POOL:
                            pe.wait_ge(s_lp, n * ON_POOL + m + 1)
                        else:
                            pe.wait_ge(s_lv, n * (F - ON_POOL) + m - ON_POOL + 1)
                        cols = slice((F + m) * P, (F + m + 1) * P)
                        for k, (a, b) in enumerate(products((wh, wl), (gh, gl))):
                            mm = pe.matmul(p_y[:, v % 2], a[:, e, cols], b[:, v % 2, m],
                                           start=(m == 0 and k == 0), stop=(m == F - 1 and k == 2))
                    mm.then_inc(s_y, 1)

                def turn(i):
                    for v in range(U):
                        up(i, v)
                        if v:
                            down(i, v - 1)
                        elif later(i, v):
                            down(i - 1, U - 1)

                turn(0)
                with pe.Fori(1, TURNS) as i:
                    turn(i)
                down(TURNS - 1, U - 1)

            @block.scalar
            def _(act):
                def turn(i):
                    for v in range(U):
                        n = i * U + v
                        for m in range(F):
                            act.wait_ge(s_up, n * F + m + 1)
                            if later(i, v):
                                if m < ON_POOL:
                                    act.wait_ge(s_lp, (n - 1) * ON_POOL + m + 1)
                                else:
                                    act.wait_ge(s_lv, (n - 1) * (F - ON_POOL) + m - ON_POOL + 1)
                            act.activation(g[:, m], p_h[:, m], ACT.Gelu_apprx_tanh, bias=b1[:, v % EXP1, m:m + 1]).then_inc(s_g, 1)

                turn(0)
                with act.Fori(1, TURNS) as i:
                    turn(i)

            @block.vector
            def _(dve):
                def cut_weights(e):
                    dve.wait_ge(s_raw[e % 2], 16 * (e // 2 + 1))
                    dve.tensor_copy(wh[:, e], raw[:, e % 2]).then_inc(s_wh, 1)
                    dve.wait_ge(s_wh, e + 1)
                    dve.tensor_tensor(wl[:, e], raw[:, e % 2], wh[:, e].bitcast(F32), ALU.subtract).then_inc(s_w, 1)

                def cut_tokens(i, x):
                    c = i * CPB + x
                    tok = bass.ds(c * CH, CH)
                    if not isinstance(c, int) or c >= CPB:
                        dve.wait_ge(s_up, (c - 1) * (EXP1 * F))
                    dve.tensor_copy(xh[:, x], lnT[:, tok]).then_inc(s_xh, 1)
                    dve.wait_ge(s_xh, c + 1)
                    dve.tensor_tensor(xl[:, x], lnT[:, tok], xh[:, x].bitcast(F32), ALU.subtract).then_inc(s_xs, 1)

                def cut(i, v):
                    n = i * U + v
                    if later(i, v, 2):
                        dve.wait_ge(s_y, n - 1)
                    for m in range(F):
                        dve.wait_ge(s_g, n * F + m + 1)
                        dve.tensor_copy(gh[:, v % 2, m], g[:, m]).then_inc(s_hi, 1)
                        if m >= ON_POOL:
                            dve.wait_ge(s_hi, n * F + m + 1)
                            dve.tensor_tensor(gl[:, v % 2, m], g[:, m], gh[:, v % 2, m].bitcast(F32), ALU.subtract).then_inc(s_lv, 1)

                def add(i, v):
                    n, x, e = i * U + v, v // EXP1, v % EXP1
                    dve.wait_ge(s_y, n + 1)
                    if e == 0:
                        dve.wait_ge(s_share[x], i * 16 + 16)
                    if later(i, v, 2):
                        dve.wait_ge(s_x, n - 1)
                    dve.scalar_tensor_tensor(part[:, v % 2], p_y[:, v % 2], b2[:, e:e + 1], share[:, x, e], ALU.add, ALU.mult).then_inc(s_part, 1)
                    dve.wait_ge(s_part, n + 1)
                    if later(i, v):
                        dve.wait_ge(s_x, n)
                    tok = bass.ds((i * CPB + x) * CH, CH)
                    dve.tensor_tensor(xT[:, tok], xT[:, tok], part[:, v % 2], ALU.add).then_inc(s_x, 1)

                def turn(i, final=False):
                    for v in range(U):
                        cut(i, v)
                        if v % EXP1 == EXP1 // 2:
                            if v < EXP1:
                                cut_tokens(i, 1)
                            elif not final:
                                cut_tokens(i + 1, 0)
                        if isinstance(i, int) and i == 0 and v + 2 < EXP1:
                            cut_weights(v + 2)
                        if v:
                            add(i, v - 1)
                        elif later(i, v):
                            add(i - 1, U - 1)

                cut_tokens(0, 0)
                cut_weights(0)
                cut_weights(1)
                turn(0)
                with dve.Fori(1, TURNS - 1) as i:
                    turn(i)
                turn(TURNS - 1, final=True)
                add(TURNS - 1, U - 1)

            @block.gpsimd
            def _(pool):
                def turn(i):
                    for v in range(U):
                        n = i * U + v
                        for m in range(ON_POOL):
                            pool.wait_ge(s_hi, n * F + m + 1)
                            pool.tensor_tensor(gl[:, v % 2, m], g[:, m], gh[:, v % 2, m].bitcast(F32), ALU.subtract).then_inc(s_lp, 1)

                turn(0)
                with pool.Fori(1, TURNS) as i:
                    turn(i)


def shape_constants():
    import numpy as np
    bf16 = mybir.dt.np(BF16)
    sel = np.zeros((P, STATE, P), np.float32)
    for s in range(STATE):
        for part in range(3):
            sel[32 * part + s, s, :] = 1.0
    return {
        "ones_over_d": np.full((P, P), 1.0 / D, np.float32),
        "ident": np.eye(P, dtype=np.float32),
        "sel": sel.astype(bf16),
        "prio": np.tile(EXP0 - np.arange(EXP0, dtype=np.float32), (P, 1)),
        "before": np.triu(np.ones((P, P), np.float32), 1).astype(bf16),
        "ones_bf16": np.ones((P, P), bf16),
        "ident_bf16": np.eye(P).astype(bf16),
        "mask_q": (np.triu(np.ones((P, P), np.float32), 1) * MASKED).astype(bf16),
        "mask_k": (np.tril(np.ones((P, P), np.float32), -1) * MASKED).astype(bf16),
        "same": np.kron(np.eye(EXP0), np.ones((OCT, OCT))).astype(np.float32),
        "first": np.kron(np.eye(EXP0), np.eye(OCT)[:, :1]).astype(np.float32),
        "ones": np.ones((P, P), np.float32),
        "slot_base": np.tile(CAP * np.arange(EXP0, dtype=np.float32), (P, 1)),
        "spare": (NSLOT + np.arange(TOPK * TOK, dtype=np.float32)).reshape(TOPK, NT, P).transpose(2, 0, 1).copy(),
        "again": np.tile((np.arange(NT) > 0).astype(np.float32), (P, EXP0, 1)),
    }


def lay_out(inputs):
    import numpy as np
    i = {k: np.asarray(v) for k, v in inputs.items()}
    c = np.ascontiguousarray

    def blocks(a):
        return c(a.reshape((NBLK, P) + a.shape[1:]).swapaxes(0, 1))

    out = {"x": c(i["L0_attn_x"].reshape(TOK, D).T)}
    out["in_proj"] = c(i["L0_attn_in_proj_w"].T)
    out["norm_w"] = c(i["L0_attn_norm_w"].reshape(P, 1))
    out["conv_w"] = blocks(i["L0_attn_conv_w"])
    out["conv_b"] = blocks(i["L0_attn_conv_b"])
    xp = i["L0_attn_x_proj_w"]
    wide = np.zeros((P, INNER), xp.dtype)
    for part in range(3):
        wide[32 * part:32 * part + 32] = xp[RANK:]
    wide[96:96 + RANK] = xp[:RANK]
    out["x_proj"] = blocks(c(wide.T))
    dt = np.zeros((P, INNER), xp.dtype)
    dt[96:96 + RANK] = i["L0_attn_dt_proj_w"].T
    out["dt_proj"] = dt
    out["dt_b"] = blocks(i["L0_attn_dt_proj_b"])
    out["a_log"] = blocks(i["L0_attn_A_log"])
    out["d_skip"] = blocks(i["L0_attn_D"])
    out["out_proj"] = blocks(c(i["L0_attn_out_proj_w"].T))
    out["gate_w"] = c(i["L0_ffn_gate_w"])
    out["gate_b"] = c(np.broadcast_to(i["L0_ffn_gate_b"], (P, EXP0)))

    def expert(w1, w3, w2):
        down = w2.reshape(w2.shape[0], HID0 // P, P, D).swapaxes(1, 2).reshape(w2.shape[0], P, HID0)
        return np.concatenate([w1, w3, down], axis=2)

    out["ew"] = expert(i["L0_ffn_ew1"], i["L0_ffn_ew3"], i["L0_ffn_ew2"])
    out["shared"] = c(expert(i["L0_ffn_sw1"], i["L0_ffn_sw3"], i["L0_ffn_sw2"]).swapaxes(0, 1))
    hk = HEADS * DH
    out["wqk"] = np.stack([i["L1_attn_WQ"].reshape(hk, D).T, i["L1_attn_WK"].reshape(hk, D).T], axis=1)
    out["wv"] = c(i["L1_attn_WV"].reshape(hk, D).T)
    out["wo"] = c(i["L1_attn_WO"].transpose(0, 2, 1).reshape(hk, D))
    out["gate1_w"] = np.concatenate([i["L1_ffn_Wg"], i["L1_ffn_Wt"]], axis=1)
    out["gate1_b"] = c(np.broadcast_to(np.concatenate([i["L1_ffn_bg"], i["L1_ffn_bt"]]), (P, EXP1 + 1)))
    out["b1"] = c(i["L1_ffn_b1"].reshape(EXP1, HID1 // P, P).transpose(2, 0, 1))
    out["b2"] = c(i["L1_ffn_b2"].T)
    down = i["L1_ffn_W2"].reshape(EXP1, HID1 // P, P, D).swapaxes(1, 2).reshape(EXP1, P, HID1)
    out["fw"] = np.concatenate([i["L1_ffn_W1"], down], axis=2)
    return out


def program(nc, w, scratch, yT, stages=("mamba", "moe0", "attn", "moe1"), x_in=None):
    with Phase(nc, "main") as main:
        xT = main.sb("xT", [P, TOK])
        const = main.constants(w, FIRST_CONSTANTS)
        if x_in is not None:
            with Phase(nc, "load") as ph:
                s_x = ph.sem("x_loaded")
                with ph.block() as block:
                    @block.sync
                    def _(sp):
                        sp.dma_start(xT[:], x_in).then_inc(s_x, 16)
                        for n in FIRST_CONSTANTS:
                            sp.dma_start(const[n][:], w[n]).then_inc(s_x, 16)
                        sp.wait_ge(s_x, 48)
        if "mamba" in stages:
            with Phase(nc, "mamba") as ph:
                own = {**const, **ph.constants(w, SCAN_CONSTANTS)}
                delta = ph.sb("delta", [P, BATCH, NBLK, SEQ])
                du = ph.sb("du", [P, BATCH, NBLK, SEQ])
                bc_split = ph.sb("bc_split", [P, TOK], BF16)
                mamba_prep(nc, xT, delta, du, bc_split, own, w, scratch)
                mamba_scan(nc, xT, delta, du, bc_split, own, scratch)
        with Phase(nc, "later") as later:
            const.update(later.constants(w, LATER_CONSTANTS))
            lnT = later.sb("lnT", [P, TOK])
            layer_norm(nc, xT, lnT, const, w)
            if "moe0" in stages:
                with Phase(nc, "moe0") as ph:
                    rows = ph.sb("rows", [P, NT, D])
                    weight = ph.sb("weight", [P, TOPK, NT])
                    put = ph.sb("put", [P, TOPK, NT], mybir.dt.uint32)
                    get = ph.sb("get", [P, TOPK, NT], mybir.dt.uint32)
                    router0(nc, lnT, rows, weight, put, get, const, scratch)
                    experts0(nc, xT, lnT, rows, weight, put, get, const, w, scratch)
            if "attn" in stages:
                qkv(nc, lnT, const, scratch)
                with Phase(nc, "attn_of") as ph:
                    att = ph.sb("att", [P, UNITS, KT, GH * DH])
                    attention(nc, att, const, scratch)
                    attention_out(nc, xT, lnT, att, const)
            if "moe1" in stages:
                router1(nc, lnT, const, scratch)
                experts1(nc, xT, lnT, const, w, scratch)
        with Phase(nc, "store") as ph:
            s_y = ph.sem("y_stored")
            with ph.block() as block:
                @block.sync
                def _(sp):
                    sp.dma_start(yT, xT[:]).then_inc(s_y, 16)
                    sp.wait_ge(s_y, 16)


SCRATCH = {
    "u": ((BATCH, P, NBLK, SEQ), F32), "zs": ((BATCH, P, NBLK, SEQ), F32), "c": ((BATCH, STATE, SEQ), F32),
    "parts": ((2, BATCH, HEADS, PARTS, DH, SEQ), BF16), "v": ((BATCH, GROUPS, P, KT, GH * VW), F32),
    "wt": ((EXP1, TOK), F32), "slots": ((NSLOT + TOPK * TOK, D), F32), "y": ((NSLOT + 1, D), F32),
}


def kernel(**inputs):
    import numpy as np
    import concourse.bacc as bacc
    from concourse.bass_utils import run_bass_kernel_spmd

    nc = bacc.Bacc("TRN2", target_bir_lowering=False, num_devices=1)
    arrays = {f"{k}_dram": v for k, v in {**lay_out(inputs), **shape_constants()}.items()}
    w = {k[:-5]: nc.dram_tensor(k, v.shape, mybir.dt.from_np(v.dtype), kind="ExternalInput").ap() for k, v in arrays.items()}
    scratch = {k: nc.dram_tensor(f"{k}_scratch", s, dt, kind="Internal").ap() for k, (s, dt) in SCRATCH.items()}
    yT = nc.dram_tensor("y_dram", (P, TOK), F32, kind="ExternalOutput").ap()
    program(nc, w, scratch, yT)
    got = run_bass_kernel_spmd(nc, [arrays], core_ids=[0]).results[0]["y_dram"]
    return np.ascontiguousarray(got.T).reshape(BATCH, SEQ, D)
```
